# Optimizing a Trainium2 kernel written in Bass

```python
import numpy as np
import jax
import jax.numpy as jnp

def _softmax(x, axis=-1):
    return jax.nn.softmax(x, axis=axis)

def _gelu(x):
    return jax.nn.gelu(x, approximate=True)

def _silu(x):
    return jax.nn.silu(x)

def _sigmoid(x):
    return jax.nn.sigmoid(x)

def _layernorm(x, axis=-1, eps=1e-05):
    m = jnp.mean(x, axis=axis, keepdims=True)
    v = jnp.var(x, axis=axis, keepdims=True)
    return (x - m) / jnp.sqrt(v + eps)

def _scatter_add(tgt, idx, src, axis=0):
    return tgt.at[idx].add(src)

def _segment_sum(src, seg, n):
    return jax.ops.segment_sum(src, seg, n)
kernel_name = 'mk_vit_tower_cls_d2_tok_img512_r4_780754'

def setup_inputs(seed: int=0):
    np.random.seed(seed)
    _w = jnp.asarray

    def _rec_inputs():
        import jax
        import jax.numpy as jnp
        _rk = jax.random.key(seed)
        x = -0.000392918 + 0.999932 * jax.random.normal(jax.random.fold_in(_rk, 1), (16, 1, 128, 128), jnp.float32)
        cls_tok = 0.02 * jax.random.normal(jax.random.fold_in(_rk, 5), (1, 1, 128), jnp.float32)
        return (x, cls_tok)
    x, cls_tok = _rec_inputs()

    def _L0_tok_setup():
        import math
        import jax, jax.numpy as jnp
        import numpy as np
        PW = PH = 16
        EMB = 128
        HID = 128
        B, H, W = (64, 128, 128)
        L = H // PW * (W // PH)
        SIGMA_ZERO = 0.1

        def _f_noise(x):
            return jnp.sign(x) * jnp.sqrt(jnp.abs(x))

        def _noisy_linear(x, w, b, sw, sb, eps_in, eps_out):
            ei = _f_noise(eps_in)
            eo = _f_noise(eps_out)
            w_n = w + sw * (eo[:, None] * ei[None, :])
            b_n = b + sb * eo
            return x @ w_n.T + b_n

        def _unfold_patches(x):
            b = x.shape[0]
            p = x.reshape(b, H // PW, PW, W // PH, PH)
            p = p.transpose(0, 1, 3, 2, 4)
            return p.reshape(b, L, PW * PH)

        def _pos_encoding(x):
            pos = jnp.arange(L, dtype=jnp.float32)[:, None]
            div = jnp.exp(jnp.arange(0, EMB, 2, dtype=jnp.float32) * (-math.log(10000.0) / EMB))
            ang = pos * div
            pe = jnp.stack([jnp.sin(ang), jnp.cos(ang)], axis=-1).reshape(L, EMB)
            return x + pe[None, :, :]
        key = jax.random.key(seed)
        ks = jax.random.split(key, 12)
        in_f = PW * PH
        sig = SIGMA_ZERO / math.sqrt(in_f)
        bnd1 = 1.0 / math.sqrt(in_f)
        bnd3 = 1.0 / math.sqrt(HID)
        u = lambda k, shape, bnd: jax.random.uniform(k, shape, jnp.float32, -bnd, bnd)
        return {'inputs': jax.random.normal(ks[0], (B, 1, H, W), jnp.float32), 'W1_w': u(ks[1], (HID, in_f), bnd1), 'W1_b': u(ks[2], (HID,), bnd1), 'W1_sw': jnp.full((HID, in_f), sig, jnp.float32), 'W1_sb': jnp.full((HID,), sig, jnp.float32), 'W2_w': u(ks[3], (HID, in_f), bnd1), 'W2_b': u(ks[4], (HID,), bnd1), 'W2_sw': jnp.full((HID, in_f), sig, jnp.float32), 'W2_sb': jnp.full((HID,), sig, jnp.float32), 'W3_w': u(ks[5], (EMB, HID), bnd3), 'W3_b': u(ks[6], (EMB,), bnd3), 'eps_in1': jax.random.normal(ks[7], (in_f,), jnp.float32), 'eps_out1': jax.random.normal(ks[8], (HID,), jnp.float32), 'eps_in2': jax.random.normal(ks[9], (in_f,), jnp.float32), 'eps_out2': jax.random.normal(ks[10], (HID,), jnp.float32)}
    _L0_tok_all = _L0_tok_setup()
    _L0_tok_in = {k: v for k, v in _L0_tok_all.items() if k in ('W1_w', 'W1_b', 'W1_sw', 'W1_sb', 'W2_w', 'W2_b', 'W2_sw', 'W2_sb', 'W3_w', 'W3_b', 'eps_in1', 'eps_out1', 'eps_in2', 'eps_out2')}
    del _L0_tok_all

    def _L0_attn_setup():
        import math
        import jax, jax.numpy as jnp
        import numpy as np
        B, N, D = (32, 256, 128)
        E, S = (256, 128)
        key = jax.random.key(seed)
        ks = jax.random.split(key, 6)
        x = jax.random.normal(ks[0], (B, N, D), dtype=jnp.float32)
        w = jax.random.uniform(ks[1], (2 * N - 1,), dtype=jnp.float32)
        limit = math.sqrt(6.0 / (D + 2 * E + S))
        uv_w = jax.random.uniform(ks[2], (D, 2 * E + S), minval=-limit, maxval=limit, dtype=jnp.float32)
        o_w = jax.random.normal(ks[3], (E, D), dtype=jnp.float32) * 0.02
        gamma = jax.random.uniform(ks[4], (2, S), dtype=jnp.float32)
        beta = jax.random.uniform(ks[5], (2, S), dtype=jnp.float32)
        g = jnp.asarray(math.sqrt(D), dtype=jnp.float32)
        res_scale = jnp.ones((D,), dtype=jnp.float32)
        return {'x': x, 'w': w, 'uv_w': uv_w, 'o_w': o_w, 'gamma': gamma, 'beta': beta, 'g': g, 'res_scale': res_scale}
    _L0_attn_all = _L0_attn_setup()
    _L0_attn_in = {k: v for k, v in _L0_attn_all.items() if k in ('w', 'uv_w', 'o_w', 'gamma', 'beta', 'g', 'res_scale')}
    del _L0_attn_all

    def _L0_ffn_setup():
        import jax, jax.numpy as jnp
        import numpy as np
        B, S, D, O = (1, 512, 128, 128)
        H, QD, K, PK = (8, 64, 16, 64)
        N = PK * PK
        HALF = QD // 2

        def _l2norm(x):
            n = jnp.sqrt(jnp.sum(x * x, axis=-1, keepdims=True))
            return x / jnp.maximum(n, 1e-12)
        key = jax.random.key(seed)
        ks = jax.random.split(key, 9)
        return {'hidden_states': jax.random.normal(ks[0], (B, S, D), jnp.float32), 'Wq': jax.random.normal(ks[1], (H * QD, D), jnp.float32) * 0.02, 'bq': jnp.zeros((H * QD,), jnp.float32), 'ln_g': jnp.ones((QD,), jnp.float32), 'ln_b': jnp.zeros((QD,), jnp.float32), 'keys0': jax.random.normal(ks[2], (PK, HALF), jnp.float32) * 0.02, 'keys1': jax.random.normal(ks[3], (PK, HALF), jnp.float32) * 0.02, 'expert_down': jax.random.normal(ks[4], (N, D), jnp.float32) * 0.02, 'expert_up': jax.random.normal(ks[5], (N, O), jnp.float32) * 0.02}
    _L0_ffn_all = _L0_ffn_setup()
    _L0_ffn_in = {k: v for k, v in _L0_ffn_all.items() if k in ('Wq', 'bq', 'ln_g', 'ln_b', 'keys0', 'keys1', 'expert_down', 'expert_up')}
    del _L0_ffn_all

    def _L1_attn_setup():
        import jax, jax.numpy as jnp
        import numpy as np
        D_MODEL = 128
        NHEAD = 8
        D_FF = 512
        EPS = 1e-05

        def _layernorm(x, gamma, beta):
            mu = jnp.mean(x, axis=-1, keepdims=True)
            var = jnp.mean(jnp.square(x - mu), axis=-1, keepdims=True)
            return (x - mu) * jax.lax.rsqrt(var + EPS) * gamma + beta

        def _rope(x, cos, sin):
            d = x.shape[-1]
            x1, x2 = (x[..., :d // 2], x[..., d // 2:])
            return jnp.concatenate([x1 * cos - x2 * sin, x2 * cos + x1 * sin], axis=-1)
        key = jax.random.key(seed)
        ks = jax.random.split(key, 12)
        B, S = (2, 1024)
        s = 0.02
        inp = {'src': jax.random.normal(ks[0], (B, S, D_MODEL), dtype=jnp.float32), 'Wq': jax.random.normal(ks[1], (D_MODEL, D_MODEL), dtype=jnp.float32) * s, 'Wk': jax.random.normal(ks[2], (D_MODEL, D_MODEL), dtype=jnp.float32) * s, 'Wv': jax.random.normal(ks[3], (D_MODEL, D_MODEL), dtype=jnp.float32) * s, 'Wo': jax.random.normal(ks[4], (D_MODEL, D_MODEL), dtype=jnp.float32) * s, 'W1': jax.random.normal(ks[5], (D_FF, D_MODEL), dtype=jnp.float32) * s, 'b1': jnp.zeros((D_FF,), dtype=jnp.float32), 'W2': jax.random.normal(ks[6], (D_MODEL, D_FF), dtype=jnp.float32) * s, 'b2': jnp.zeros((D_MODEL,), dtype=jnp.float32), 'g1': jnp.ones((D_MODEL,), dtype=jnp.float32), 'be1': jnp.zeros((D_MODEL,), dtype=jnp.float32), 'g2': jnp.ones((D_MODEL,), dtype=jnp.float32), 'be2': jnp.zeros((D_MODEL,), dtype=jnp.float32)}
        return inp
    _L1_attn_all = _L1_attn_setup()
    _L1_attn_in = {k: v for k, v in _L1_attn_all.items() if k in ('Wq', 'Wk', 'Wv', 'Wo', 'W1', 'b1', 'W2', 'b2', 'g1', 'be1', 'g2', 'be2')}
    del _L1_attn_all

    def _L1_ffn_setup():
        import jax, jax.numpy as jnp
        import numpy as np
        B, S, D = (8, 1024, 128)
        H = 512
        O = 128
        E = 8
        TOP_K = 1
        key = jax.random.key(seed)
        ks = jax.random.split(key, 8)
        sc = 0.02
        return {'x': jax.random.normal(ks[0], (B, S, D), dtype=jnp.float32), 'Wr': jax.random.normal(ks[1], (D, E), dtype=jnp.float32) * sc, 'br': jnp.zeros((E,), dtype=jnp.float32), 'W1': jax.random.normal(ks[2], (E, D, H), dtype=jnp.float32) * sc, 'b1': jnp.zeros((E, H), dtype=jnp.float32), 'W2': jax.random.normal(ks[3], (E, H, O), dtype=jnp.float32) * sc, 'b2': jnp.zeros((E, O), dtype=jnp.float32)}
    _L1_ffn_all = _L1_ffn_setup()
    _L1_ffn_in = {k: v for k, v in _L1_ffn_all.items() if k in ('Wr', 'br', 'W1', 'b1', 'W2', 'b2')}
    del _L1_ffn_all
    return {'x': x, 'cls_tok': cls_tok, 'L0_tok_W1_w': _L0_tok_in['W1_w'], 'L0_tok_W1_b': _L0_tok_in['W1_b'], 'L0_tok_W1_sw': _L0_tok_in['W1_sw'], 'L0_tok_W1_sb': _L0_tok_in['W1_sb'], 'L0_tok_W2_w': _L0_tok_in['W2_w'], 'L0_tok_W2_b': _L0_tok_in['W2_b'], 'L0_tok_W2_sw': _L0_tok_in['W2_sw'], 'L0_tok_W2_sb': _L0_tok_in['W2_sb'], 'L0_tok_W3_w': _L0_tok_in['W3_w'], 'L0_tok_W3_b': _L0_tok_in['W3_b'], 'L0_tok_eps_in1': _L0_tok_in['eps_in1'], 'L0_tok_eps_out1': _L0_tok_in['eps_out1'], 'L0_tok_eps_in2': _L0_tok_in['eps_in2'], 'L0_tok_eps_out2': _L0_tok_in['eps_out2'], 'L0_attn_w': _L0_attn_in['w'], 'L0_attn_uv_w': _L0_attn_in['uv_w'], 'L0_attn_o_w': _L0_attn_in['o_w'], 'L0_attn_gamma': _L0_attn_in['gamma'], 'L0_attn_beta': _L0_attn_in['beta'], 'L0_attn_g': _L0_attn_in['g'], 'L0_attn_res_scale': _L0_attn_in['res_scale'], 'L0_ffn_Wq': _L0_ffn_in['Wq'], 'L0_ffn_bq': _L0_ffn_in['bq'], 'L0_ffn_ln_g': _L0_ffn_in['ln_g'], 'L0_ffn_ln_b': _L0_ffn_in['ln_b'], 'L0_ffn_keys0': _L0_ffn_in['keys0'], 'L0_ffn_keys1': _L0_ffn_in['keys1'], 'L0_ffn_expert_down': _L0_ffn_in['expert_down'], 'L0_ffn_expert_up': _L0_ffn_in['expert_up'], 'L1_attn_Wq': _L1_attn_in['Wq'], 'L1_attn_Wk': _L1_attn_in['Wk'], 'L1_attn_Wv': _L1_attn_in['Wv'], 'L1_attn_Wo': _L1_attn_in['Wo'], 'L1_attn_W1': _L1_attn_in['W1'], 'L1_attn_b1': _L1_attn_in['b1'], 'L1_attn_W2': _L1_attn_in['W2'], 'L1_attn_b2': _L1_attn_in['b2'], 'L1_attn_g1': _L1_attn_in['g1'], 'L1_attn_be1': _L1_attn_in['be1'], 'L1_attn_g2': _L1_attn_in['g2'], 'L1_attn_be2': _L1_attn_in['be2'], 'L1_ffn_Wr': _L1_ffn_in['Wr'], 'L1_ffn_br': _L1_ffn_in['br'], 'L1_ffn_W1': _L1_ffn_in['W1'], 'L1_ffn_b1': _L1_ffn_in['b1'], 'L1_ffn_W2': _L1_ffn_in['W2'], 'L1_ffn_b2': _L1_ffn_in['b2']}

def reference(x, cls_tok, L0_tok_W1_w, L0_tok_W1_b, L0_tok_W1_sw, L0_tok_W1_sb, L0_tok_W2_w, L0_tok_W2_b, L0_tok_W2_sw, L0_tok_W2_sb, L0_tok_W3_w, L0_tok_W3_b, L0_tok_eps_in1, L0_tok_eps_out1, L0_tok_eps_in2, L0_tok_eps_out2, L0_attn_w, L0_attn_uv_w, L0_attn_o_w, L0_attn_gamma, L0_attn_beta, L0_attn_g, L0_attn_res_scale, L0_ffn_Wq, L0_ffn_bq, L0_ffn_ln_g, L0_ffn_ln_b, L0_ffn_keys0, L0_ffn_keys1, L0_ffn_expert_down, L0_ffn_expert_up, L1_attn_Wq, L1_attn_Wk, L1_attn_Wv, L1_attn_Wo, L1_attn_W1, L1_attn_b1, L1_attn_W2, L1_attn_b2, L1_attn_g1, L1_attn_be1, L1_attn_g2, L1_attn_be2, L1_ffn_Wr, L1_ffn_br, L1_ffn_W1, L1_ffn_b1, L1_ffn_W2, L1_ffn_b2):
    import jax
    import jax.numpy as jnp

    def _L0_tok_ref(inputs, W1_w, W1_b, W1_sw, W1_sb, W2_w, W2_b, W2_sw, W2_sb, W3_w, W3_b, eps_in1, eps_out1, eps_in2, eps_out2):
        import math
        import jax, jax.numpy as jnp
        import numpy as np
        PW = PH = 16
        EMB = 128
        HID = 128
        B, H, W = (64, 128, 128)
        L = H // PW * (W // PH)
        SIGMA_ZERO = 0.1

        def _f_noise(x):
            return jnp.sign(x) * jnp.sqrt(jnp.abs(x))

        def _noisy_linear(x, w, b, sw, sb, eps_in, eps_out):
            ei = _f_noise(eps_in)
            eo = _f_noise(eps_out)
            w_n = w + sw * (eo[:, None] * ei[None, :])
            b_n = b + sb * eo
            return x @ w_n.T + b_n

        def _unfold_patches(x):
            b = x.shape[0]
            p = x.reshape(b, H // PW, PW, W // PH, PH)
            p = p.transpose(0, 1, 3, 2, 4)
            return p.reshape(b, L, PW * PH)

        def _pos_encoding(x):
            pos = jnp.arange(L, dtype=jnp.float32)[:, None]
            div = jnp.exp(jnp.arange(0, EMB, 2, dtype=jnp.float32) * (-math.log(10000.0) / EMB))
            ang = pos * div
            pe = jnp.stack([jnp.sin(ang), jnp.cos(ang)], axis=-1).reshape(L, EMB)
            return x + pe[None, :, :]
        x = _unfold_patches(inputs)
        g = _noisy_linear(x, W1_w, W1_b, W1_sw, W1_sb, eps_in1, eps_out1)
        x_gate = g * jnp.tanh(jax.nn.softplus(g))
        x_inner = _noisy_linear(x, W2_w, W2_b, W2_sw, W2_sb, eps_in2, eps_out2)
        x = x_gate * x_inner
        x = x @ W3_w.T + W3_b
        return _pos_encoding(x)

    def _L0_attn_ref(x, w, uv_w, o_w, gamma, beta, g, res_scale):
        import math
        import jax, jax.numpy as jnp
        import numpy as np
        B, N, D = (32, 256, 128)
        E, S = (256, 128)
        eps = 1e-05
        sqrt_s = math.sqrt(S)
        n = x.shape[1]
        norm = jnp.maximum(jnp.linalg.norm(x, axis=-1, keepdims=True), eps)
        xn = x / norm * g
        uv = jax.nn.silu(xn @ uv_w)
        u, v, base = (uv[..., :E], uv[..., E:2 * E], uv[..., 2 * E:])
        qk_base = base[:, :, None, :] * gamma + beta
        q, k = (qk_base[:, :, 0, :], qk_base[:, :, 1, :])
        qk = jnp.einsum('bms,bns->bmn', q, k)
        i = jnp.arange(n)
        idx = n - 1 + i[None, :] - i[:, None]
        qk = qk + w[idx][None, :, :]
        kernel = jnp.square(jax.nn.relu(qk / sqrt_s))
        out = u * jnp.einsum('bmn,bne->bme', kernel, v)
        out = out @ o_w
        return x * res_scale + out

    def _L0_ffn_ref(hidden_states, Wq, bq, ln_g, ln_b, keys0, keys1, expert_down, expert_up):
        import jax, jax.numpy as jnp
        import numpy as np
        B, S, D, O = (1, 512, 128, 128)
        H, QD, K, PK = (8, 64, 16, 64)
        N = PK * PK
        HALF = QD // 2

        def _l2norm(x):
            n = jnp.sqrt(jnp.sum(x * x, axis=-1, keepdims=True))
            return x / jnp.maximum(n, 1e-12)
        b, s, d = hidden_states.shape
        q = (hidden_states @ Wq.T + bq).reshape(b, s, H, QD)
        mu = jnp.mean(q, axis=-1, keepdims=True)
        var = jnp.mean((q - mu) ** 2, axis=-1, keepdims=True)
        q = (q - mu) / jnp.sqrt(var + 1e-05) * ln_g + ln_b
        q0, q1 = (q[..., :HALF], q[..., HALF:])
        s0 = jnp.einsum('bshq,eq->bshe', _l2norm(q0), _l2norm(keys0))
        s1 = jnp.einsum('bshq,eq->bshe', _l2norm(q1), _l2norm(keys1))
        sc0, ix0 = jax.lax.top_k(s0, K)
        sc1, ix1 = jax.lax.top_k(s1, K)
        cs = (sc0[..., :, None] + sc1[..., None, :]).reshape(b, s, H, K * K)
        ci = (ix0[..., :, None] + ix1[..., None, :]).reshape(b, s, H, K * K)
        fs, pos = jax.lax.top_k(cs, K)
        fi = jnp.take_along_axis(ci, pos, axis=-1)
        w = jax.nn.softmax(fs, axis=-1)
        down = expert_down[fi]
        up = expert_up[fi]
        inner = jnp.einsum('bsd,bshkd->bshk', hidden_states, down)
        act = jax.nn.gelu(inner, approximate=False)
        out = jnp.einsum('bshk,bshko->bso', act * w, up)
        return out

    def _L1_attn_ref(src, Wq, Wk, Wv, Wo, W1, b1, W2, b2, g1, be1, g2, be2):
        import jax, jax.numpy as jnp
        import numpy as np
        D_MODEL = 128
        NHEAD = 8
        D_FF = 512
        EPS = 1e-05

        def _layernorm(x, gamma, beta):
            mu = jnp.mean(x, axis=-1, keepdims=True)
            var = jnp.mean(jnp.square(x - mu), axis=-1, keepdims=True)
            return (x - mu) * jax.lax.rsqrt(var + EPS) * gamma + beta

        def _rope(x, cos, sin):
            d = x.shape[-1]
            x1, x2 = (x[..., :d // 2], x[..., d // 2:])
            return jnp.concatenate([x1 * cos - x2 * sin, x2 * cos + x1 * sin], axis=-1)
        B, S, D = src.shape
        H = NHEAD
        hd = D // H
        q = (src @ Wq.T).reshape(B, S, H, hd)
        k = (src @ Wk.T).reshape(B, S, H, hd)
        v = (src @ Wv.T).reshape(B, S, H, hd)
        inv_freq = 1.0 / 10000.0 ** (jnp.arange(0, hd, 2, dtype=jnp.float32) / hd)
        t = jnp.arange(S, dtype=jnp.float32)
        freqs = t[:, None] * inv_freq[None, :]
        cos = jnp.cos(freqs)[None, :, None, :]
        sin = jnp.sin(freqs)[None, :, None, :]
        q = _rope(q, cos, sin)
        k = _rope(k, cos, sin)
        scale = 1.0 / jnp.sqrt(jnp.float32(hd))
        scores = jnp.einsum('bqhd,bkhd->bhqk', q, k) * scale
        attn = jax.nn.softmax(scores, axis=-1)
        ctx = jnp.einsum('bhqk,bkhd->bqhd', attn, v).reshape(B, S, D)
        attn_out = ctx @ Wo.T
        x = _layernorm(src + attn_out, g1, be1)
        ffn = jax.nn.relu(x @ W1.T + b1) @ W2.T + b2
        x = _layernorm(x + ffn, g2, be2)
        return x

    def _L1_ffn_ref(x, Wr, br, W1, b1, W2, b2):
        import jax, jax.numpy as jnp
        import numpy as np
        B, S, D = (8, 1024, 128)
        H = 512
        O = 128
        E = 8
        TOP_K = 1
        b, s, d = x.shape
        xf = x.reshape(-1, d)
        router_logits = xf @ Wr + br
        topk_logits, topk_idx = jax.lax.top_k(router_logits, TOP_K)
        topk_gates = jax.nn.softmax(topk_logits, axis=1)
        out = jnp.zeros((xf.shape[0], O), dtype=x.dtype)
        for k in range(TOP_K):
            idx_k = topk_idx[:, k]
            gate_k = topk_gates[:, k:k + 1]
            for e in range(E):
                h = jax.nn.relu(xf @ W1[e] + b1[e])
                oe = h @ W2[e] + b2[e]
                mask = (idx_k == e)[:, None]
                out = out + jnp.where(mask, gate_k * oe, 0.0)
        return out.reshape(b, s, O)
    h = _L0_tok_ref(x, L0_tok_W1_w, L0_tok_W1_b, L0_tok_W1_sw, L0_tok_W1_sb, L0_tok_W2_w, L0_tok_W2_b, L0_tok_W2_sw, L0_tok_W2_sb, L0_tok_W3_w, L0_tok_W3_b, L0_tok_eps_in1, L0_tok_eps_out1, L0_tok_eps_in2, L0_tok_eps_out2)
    h = jnp.concatenate([jnp.broadcast_to(cls_tok, (h.shape[0], 1, h.shape[2])), h], axis=1)
    h = h + _L0_attn_ref(_layernorm(h, axis=-1), L0_attn_w, L0_attn_uv_w, L0_attn_o_w, L0_attn_gamma, L0_attn_beta, L0_attn_g, L0_attn_res_scale)
    h = h + _L0_ffn_ref(_layernorm(h, axis=-1), L0_ffn_Wq, L0_ffn_bq, L0_ffn_ln_g, L0_ffn_ln_b, L0_ffn_keys0, L0_ffn_keys1, L0_ffn_expert_down, L0_ffn_expert_up)
    h = h + _L1_attn_ref(_layernorm(h, axis=-1), L1_attn_Wq, L1_attn_Wk, L1_attn_Wv, L1_attn_Wo, L1_attn_W1, L1_attn_b1, L1_attn_W2, L1_attn_b2, L1_attn_g1, L1_attn_be1, L1_attn_g2, L1_attn_be2)
    h = h + _L1_ffn_ref(_layernorm(h, axis=-1), L1_ffn_Wr, L1_ffn_br, L1_ffn_W1, L1_ffn_b1, L1_ffn_W2, L1_ffn_b2)
    return h

_drawn_inputs = setup_inputs


def setup_inputs(seed=0):
    import zlib

    import numpy as np

    out = dict(_drawn_inputs(seed))
    spreads = {'L0_tok_W1_sw': (0.0062500000931322575, 0.6),
     'L0_tok_W1_sb': (0.0062500000931322575, 0.6),
     'L0_tok_W2_sw': (0.0062500000931322575, 0.6),
     'L0_tok_W2_sb': (0.0062500000931322575, 0.6),
     'L0_attn_res_scale': (1.0, 0.6),
     'L0_ffn_bq': (0.0, 0.8),
     'L0_ffn_ln_g': (1.0, 0.6),
     'L0_ffn_ln_b': (0.0, 0.8),
     'L1_attn_b1': (0.0, 0.8),
     'L1_attn_b2': (0.0, 2.0),
     'L1_attn_g1': (1.0, 0.6),
     'L1_attn_be1': (0.0, 0.8),
     'L1_attn_g2': (1.0, 0.6),
     'L1_attn_be2': (0.0, 0.8),
     'L1_ffn_br': (0.0, 0.8),
     'L1_ffn_b1': (0.0, 0.8),
     'L1_ffn_b2': (0.0, 0.8)}
    factors = {'L0_tok_W1_b': 4.038,
     'L0_tok_W2_b': 3.836,
     'L0_attn_w': 8.0,
     'L0_ffn_Wq': 8.0,
     'L0_ffn_keys0': 8.0,
     'L0_ffn_keys1': 8.0,
     'L0_ffn_expert_down': 8.0,
     'L0_ffn_expert_up': 8.0,
     'L1_attn_Wq': 8.0,
     'L1_attn_Wk': 8.0,
     'L1_attn_Wv': 8.0,
     'L1_attn_Wo': 8.0,
     'L1_attn_W1': 8.0,
     'L1_attn_W2': 8.0,
     'L1_ffn_Wr': 8.0,
     'L1_ffn_W1': 8.0,
     'L1_ffn_W2': 8.0}
    for name, (base, spread) in spreads.items():
        noise = np.random.default_rng([zlib.crc32(name.encode()), seed]).standard_normal(out[name].shape)
        drawn = base * np.exp(spread * noise) if base else spread * noise
        out[name] = jnp.asarray(drawn.astype(out[name].dtype))
    for name, factor in factors.items():
        out[name] = (out[name] * factor).astype(out[name].dtype)
    return out
```

```python
from contextlib import ExitStack

import numpy as np

import concourse.bass as bass
from concourse import mybir

F32 = mybir.dt.float32
BF16 = mybir.dt.bfloat16
U32 = mybir.dt.uint32
ALU = mybir.AluOpType
ACT = mybir.ActivationFunctionType
AX = mybir.AxisListType

P = 128
IMAGES = 16
PATCHES = 64
SEQ = PATCHES + 1
T = IMAGES * SEQ
Q = T // 4
HALF = 2 * Q
TILE = 104
NT = T // TILE
HEADS = 8
KEYS = 64
TOP = 16
LISTS = 2 * HEADS
ROW_LEN = [TOP // (r + 1) for r in range(TOP)]
ROW_AT = [sum(ROW_LEN[:r]) for r in range(TOP)]
CAND = sum(ROW_LEN)
PAIR = 2 * CAND
PAIRS = HEADS // 2
QUAD = 4
GROUPS = TILE // QUAD
PER_BANK = 9
EA, EB = 4, 32
PARTS = 3
HD = 16
EXPERTS = 8
BIG = -1e30
ROUND = 12582912.0

COLS = {}
for _name, _n in (("w1b", 1), ("w1sb", 1), ("w2b", 1), ("w2sb", 1), ("w3b", 1), ("gamma", 2), ("beta", 2),
                  ("res", 1), ("g", 1), ("bq", 4), ("lng", 1), ("lnb", 1), ("b1", 4), ("b2", 1), ("g1", 1),
                  ("be1", 1), ("g2", 1), ("be2", 1), ("mb1", 32), ("mb2", 8), ("cls", 1), ("eps", 1)):
    COLS[_name] = (sum(n for _, n in COLS.values()), _n)
NCOLS = sum(n for _, n in COLS.values())


LOADS = {
    "first": ("eps", "keys", "cols", "tokw", "ident"),
    "tok": ("pat", "centre64", "wq", "w3", "pos"),
    "gau": ("centre", "mean", "ones", "uvw", "relpos", "ow"),
    "keys": ("mean64", "blk32", "down", "identb", "up"),
    "block": ("qkv", "rope", "headmask", "wo", "w1", "w2"),
    "moe": ("wr", "br", "order", "sel8", "mw2"),
    "mw1": ("mw1",),
}
group_of = {name: group for group, names in LOADS.items() for name in names}


def build(nc, I, y):
    with ExitStack() as ctx:
        def sb(name, shape, dt=F32):
            return ctx.enter_context(nc.sbuf_tensor(name, shape, dt))

        def view(arena, at, *shape):
            n = int(np.prod(shape))
            names = " ".join("abcd"[:len(shape)])
            v = arena[:, at:at + n]
            if len(shape) == 1:
                return v
            return v.rearrange(f"p ({names}) -> p {names}", **dict(zip("abcd", shape)))

        sems = {}

        def sem(name):
            if name not in sems:
                sems[name] = ctx.enter_context(nc.semaphore(name))
            return sems[name]

        PS = ctx.enter_context(nc.psum_tensor("PS", [P, 8 * 512], F32))
        B = PS[:, :].rearrange("p (b n) -> p b n", b=8)

        L = {}
        for name, ap in I.items():
            if name not in ("pat", "tokw", "mw1"):
                L[name] = sb("in_" + name, list(ap.shape), ap.dtype)
        cols = L["cols"]

        def col(name, k=0):
            at = COLS[name][0] + k
            return cols[:, at:at + 1]

        arena1 = sb("arena1", [P, 4 * T])
        arena2 = sb("arena2", [P, 4 * T])
        arena3 = sb("arena3", [P, EB * PAIRS * TILE // 2])
        qln = view(arena1, 0, 4, T)
        L["pat"] = view(arena1, 0, 2, IMAGES * PATCHES)
        L["tokw"] = view(arena1, 2 * IMAGES * PATCHES, 2, 2, 2, P)
        L["mw1"] = view(arena3, 0, EXPERTS, 4 * P)
        ct = view(arena1, 0, T)
        x4 = view(arena1, T, T)
        hid = view(arena1, 2 * T, 4, HALF)
        sq2 = view(arena2, 0, 4, T)
        rot = view(arena2, 0, 2, 2, HALF)
        qr = view(arena2, 2 * T, T)
        kr1 = view(arena2, 3 * T, T)
        bt = arena3[0:PAIR, :].bitcast(BF16).rearrange("p (c j b g) -> p c j b g", c=PAIRS, j=QUAD, b=EB)
        ug = view(arena3, 0, 2, 2, Q)
        uo = view(arena3, 4 * Q, 2, 2, Q)
        gres = view(arena3, 8 * Q, 2, Q)
        vtok = view(arena3, 10 * Q, 2, 4, 2 * P)[0:SEQ]
        biased = view(arena3, 10 * Q + 16 * P, 2, 4, SEQ)[0:SEQ]
        relu = view(arena3, 12 * Q + 16 * P, 2, 4, SEQ)[0:SEQ]
        kern = view(arena3, 14 * Q + 16 * P, 2, 4, SEQ)[0:SEQ]

        arena4 = sb("arena4", [P, 4608])
        arena5 = sb("arena5", [P, IMAGES * HEADS * (HD + 1)])
        arena6 = sb("arena6", [P, 6 * Q])
        gate, gcap, gexp, gnum, gden, grec, gact, gmul, prod = (view(arena4, 512 * k, 2, 256) for k in range(9))
        s1 = view(arena4, 0, LISTS, KEYS)[0:TILE]
        s2 = view(arena4, LISTS * KEYS, LISTS, KEYS)[0:TILE]
        aw = arena4[0:PAIR, 2 * LISTS * KEYS:2 * LISTS * KEYS + EA * PARTS * PAIRS * TILE // 2].bitcast(BF16) \
            .rearrange("p (a q c t) -> p a q c t", a=EA, q=PARTS, c=PAIRS)
        z = view(arena5, 0, 2, HALF)
        norm = view(arena5, T, T)
        km = view(arena4, 0, HEADS, SEQ)
        mt = view(arena1, 0, T)[0:EXPERTS]
        mb = view(arena1, 2 * T, 2, Q)
        mtmp = view(arena1, 3 * T, Q)
        macc = view(arena1, 3 * T + Q, Q)
        vaug = view(arena5, 0, IMAGES, HEADS, HD + 1)[0:SEQ]
        mhid = view(arena5, 0, 2, 4, Q)
        qg, kg, base = (view(arena6, 2 * Q * k, 2, Q) for k in range(3))
        sd, pe_, pt = (view(arena6, 2 * Q * k, HEADS, SEQ)[0:SEQ] for k in range(3))

        h = sb("h", [P, T])
        xn = sb("xn", [P, T])
        x2 = sb("x2", [P, T])
        sq = sb("sq", [P, T])
        std = sb("std", [P, T])
        rstd = sb("rstd", [P, T])

        noise = sb("noise", [P, 262])
        nsign = sb("nsign", [P, 262])
        wnt = sb("wnt", [P, 2, 2, P])
        bn = sb("bn", [P, 2])


        ksq = sb("ksq", [KEYS, 2, 32])
        kn = sb("kn", [KEYS, 2])
        knc = sb("knc", [KEYS, 2])
        kr = sb("kr", [KEYS, 2])
        kk = sb("kk", [KEYS, 2, 2, 32])
        kbd = sb("kbd", [P, 4 * KEYS])
        wqc = sb("wqc", [P, 4, P])
        bqc = sb("bqc", [P, 4])
        qn = sb("qn", [TILE, NT * LISTS])
        qnc = sb("qnc", [TILE, NT * LISTS])
        rn = sb("rn", [TILE, NT * LISTS])
        gelu = sb("gelu", [P, EA, T // QUAD])
        qt = sb("qt", [P, PAIRS, TILE])
        vi = sb("vi", [TILE, 2, LISTS, TOP])
        iu = sb("iu", [TILE, LISTS, TOP], U32)
        cc = sb("cc", [TILE, LISTS, CAND])
        c2 = sb("c2", [TILE, HEADS, CAND])
        m8 = sb("m8", [TILE, HEADS, 8])
        m16 = sb("m16", [TILE, HEADS, 8])
        dif = sb("dif", [TILE, HEADS, CAND])
        ex = sb("ex", [TILE, HEADS, CAND])
        wu = sb("wu", [TILE, HEADS, CAND])
        wz = sb("wz", [TILE, HEADS])
        wr = sb("wr", [TILE, HEADS])
        wn = sb("wn", [TILE, HEADS, CAND])
        rem = sb("rem", [TILE, HEADS, CAND])
        eat = sb("eat", [TILE, HEADS, CAND])
        x5 = sb("x5", [TILE, 5, HEADS * CAND], BF16)
        xt = sb("xt", [PAIR, 5 * PAIRS, TILE], BF16)
        ah = sb("ah", [PAIR, EA, PAIRS, TILE], BF16)
        wt = sb("wt", [P, 3 * PER_BANK, EA])
        wg = sb("wg", [P, EA, TILE])

        qb = sb("qb", [P, SEQ])
        mx = sb("mx", [SEQ, HEADS])
        rs = sb("rs", [SEQ, HEADS])
        cn = sb("cn", [SEQ, HEADS, HD])

        lg = sb("lg", [TILE, NT, EXPERTS])
        lm = sb("lm", [TILE, NT])
        leq = sb("leq", [TILE, NT, EXPERTS])
        lord = sb("lord", [TILE, NT, EXPERTS])
        lfirst = sb("lfirst", [TILE, NT])
        lmask = sb("lmask", [TILE, NT, EXPERTS])
        gd = sb("gd", [TILE, NT])
        ge = sb("ge", [TILE, NT])
        gr = sb("gr", [TILE, NT])
        gg = sb("gg", [TILE, NT])
        mgate = sb("mgate", [TILE, NT, EXPERTS])

        block = ctx.enter_context(nc.Block())

        def hold(eng, semaphore, value):
            eng.wait_ge(semaphore, value)
            eng.sem_inc(sem("held"), 1)

        def loaded(eng, name):
            eng.wait_ge(sem("in_" + group_of[name]), 16 * len(LOADS[group_of[name]]))

        def images(ap, n):
            return ap.rearrange("p (i s) -> p i s", i=n)

        def halves(ap, hf):
            return ap[:, hf * HALF:(hf + 1) * HALF].rearrange("p (q n) -> p q n", q=2)

        def banks(first):
            return B[:, first:first + 2, 0:Q]

        def ln_tensor(pe, n, x, ready, count):
            for hf in range(2):
                pe.wait_ge(sem(ready), count(hf))
                for q in range(2):
                    at = (2 * hf + q) * Q
                    last = pe.matmul(B[:, 2 * hf + q, 0:Q], L["centre"][:, :], x[:, at:at + Q], start=True, stop=True)
                last.then_inc(sem("ln_centred"), 1)
            for hf in range(2):
                pe.wait_ge(sem("ln_squared"), 2 * n + hf + 1)
                for q in range(2):
                    at = (2 * hf + q) * Q
                    last = pe.matmul(B[:, 4 + 2 * hf + q, 0:Q], L["mean"][:, :], sq[:, at:at + Q], start=True, stop=True)
                last.then_inc(sem("ln_variance"), 1)

        def ln_scalar(act, n):
            for hf in range(2):
                act.wait_ge(sem("ln_centred"), 2 * n + hf + 1)
                act.activation(halves(sq, hf), banks(2 * hf), ACT.Square).then_inc(sem("ln_squared"), 1)
            for hf in range(2):
                act.wait_ge(sem("ln_variance"), 2 * n + hf + 1)
                act.activation(halves(std, hf), banks(4 + 2 * hf), ACT.Sqrt, bias=col("eps")) \
                   .then_inc(sem("ln_std"), 1)

        def ln_vector(dve, n, out):
            for hf in range(2):
                dve.wait_ge(sem("ln_std"), 2 * n + hf + 1)
                dve.reciprocal(halves(rstd, hf), halves(std, hf)).then_inc(sem("ln_rstd"), 1)
            for hf in range(2):
                dve.wait_ge(sem("ln_rstd"), 2 * n + hf + 1)
                dve.tensor_tensor(halves(out, hf), banks(2 * hf), halves(rstd, hf), ALU.mult) \
                   .then_inc(sem("ln_done"), 1)

        LN_GAU, LN_KEYS, LN_BLOCK, LN_POST1, LN_POST2, LN_MOE = range(6)

        def ln_count(n):
            return lambda hf: 2 * n + hf + 1

        @block.sync
        def _(sp):
            for name in group_of:
                if name == "mw1":
                    sp.wait_ge(sem("pk_scattered"), NT)
                sp.dma_start(L[name][tuple(slice(None) for _ in I[name].shape)], I[name]).then_inc(sem("in_" + group_of[name]), 16)
            sp.wait_ge(sem("out_ready"), 4)
            sp.dma_start(y, h[:, :]).then_inc(sem("out_stored"), 16)
            sp.wait_ge(sem("out_stored"), 16)

        @block.gpsimd
        def _(pool):
            for c in range(4):
                u = c % 2
                pool.wait_ge(sem("tok_num"), c + 1)
                pool.tensor_scalar(gden[:, u, :], gnum[:, u, :], 2.0, None, ALU.add).then_inc(sem("tok_den"), 1)
                pool.wait_ge(sem("tok_rec"), c + 1)
                pool.tensor_tensor(gact[:, u, :], gnum[:, u, :], grec[:, u, :], ALU.mult).then_inc(sem("tok_tanh"), 1)
                pool.wait_ge(sem("tok_tanh"), c + 1)
                pool.tensor_tensor(gmul[:, u, :], gact[:, u, :], gate[:, u, :], ALU.mult).then_inc(sem("tok_mish"), 1)
            for c in range(4):
                pool.wait_ge(sem("gau_relu"), c + 1)
                pool.tensor_tensor(kern[:, c % 2], relu[:, c % 2], relu[:, c % 2], ALU.mult) \
                    .then_inc(sem("gau_kernel"), 1)

            def onehot_weights():
                for a in range(EA):
                    last = pool.tensor_tensor(
                        aw[:, a].rearrange("p q c t -> p q (c t)"),
                        ah[:, a].rearrange("p c t -> p (c t)").unsqueeze(1).to_broadcast([PAIR, PARTS, PAIRS * TILE]),
                        xt[:, 0:PARTS * PAIRS, :].rearrange("p (q c) t -> p q (c t)", q=PARTS), ALU.mult)
                last.then_inc(sem("pk_aw"), 1)

            def weight_parts(i):
                parts = x5[:, :, :].rearrange("p k (h c) -> p k h c", h=HEADS)
                hold(pool, sem("pk_weights"), i + 1)
                pool.tensor_copy(parts[:, 0], wn[:, :, :]).then_inc(sem("pk_split"), 1)
                hold(pool, sem("pk_split"), i * 4 + 1)
                pool.tensor_tensor(rem[:, :, :], wn[:, :, :], parts[:, 0], ALU.subtract).then_inc(sem("pk_split"), 1)
                hold(pool, sem("pk_split"), i * 4 + 2)
                pool.tensor_copy(parts[:, 1], rem[:, :, :]).then_inc(sem("pk_split"), 1)
                hold(pool, sem("pk_split"), i * 4 + 3)
                pool.tensor_tensor(parts[:, 2], rem[:, :, :], parts[:, 1], ALU.subtract).then_inc(sem("pk_split"), 1)

            def pool_tile(i, prev):
                if prev:
                    pool.wait_ge(sem("pk_ah"), i)
                    onehot_weights()
                weight_parts(i)

            pool_tile(0, False)
            with pool.Fori(1, NT) as i:
                pool_tile(i, True)
            pool.wait_ge(sem("pk_ah"), NT)
            onehot_weights()

            for hf in range(2):
                for k, out in ((0, qr), (1, kr1)):
                    pool.wait_ge(sem("rot_parts"), 4 * hf + 2 * k + 2)
                    pool.tensor_tensor(out[:, hf * HALF:(hf + 1) * HALF], rot[:, k, 0], rot[:, k, 1], ALU.add) \
                        .then_inc(sem("rot_done"), 1)

            def head_keys(i):
                pool.tensor_copy(qb[:, :], qr[:, bass.ds(i * SEQ, SEQ)]).then_inc(sem("at_operands"), 1)
                pool.tensor_tensor(
                    km[:, :, :], kr1[:, bass.ds(i * SEQ, SEQ)].unsqueeze(1).to_broadcast([P, HEADS, SEQ]),
                    L["headmask"][:, :].unsqueeze(2).to_broadcast([P, HEADS, SEQ]), ALU.mult) \
                    .then_inc(sem("at_operands"), 1)

            pool.wait_ge(sem("rot_done"), 4)
            loaded(pool, "headmask")
            head_keys(0)
            with pool.Fori(1, IMAGES) as i:
                hold(pool, sem("at_scores"), i)
                head_keys(i)

        @block.scalar
        def _(act):
            loaded(act, "eps")
            act.activation(noise[:, :], L["eps"][:, :], ACT.Abs).then_inc(sem("noise_abs"), 1)
            act.activation(nsign[:, :], L["eps"][:, :], ACT.Sign).then_inc(sem("noise_sign"), 1)
            act.wait_ge(sem("noise_abs"), 1)
            act.activation(noise[:, :], noise[:, :], ACT.Sqrt).then_inc(sem("noise_sqrt"), 1)
            act.wait_ge(sem("key_sum"), 1)
            act.activation(kn[:, :], kn[:, :], ACT.Sqrt).then_inc(sem("key_norm"), 1)
            for c in range(4):
                act.wait_ge(sem("tok_gate"), 2 * c + 2)
                act.activation(gexp[:, c % 2, :], gcap[:, c % 2, :], ACT.Exp).then_inc(sem("tok_exp"), 1)

            ln_scalar(act, LN_GAU)
            for hf in range(2):
                act.wait_ge(sem("ln_done"), 2 * LN_GAU + hf + 1)
                act.activation(halves(sq, hf), halves(xn, hf), ACT.Square).then_inc(sem("l2_squared"), 1)
            for hf in range(2):
                act.wait_ge(sem("l2_sum"), hf + 1)
                act.activation(halves(norm, hf), banks(4 + 2 * hf), ACT.Sqrt).then_inc(sem("l2_norm"), 1)
            def gau_silu(c):
                u = c % 2
                k = 4 * u
                for blk in range(2):
                    act.wait_ge(sem("gau_uv"), 3 * c + blk + 1)
                    act.activation(ug[:, u, blk, :], B[:, k + blk, 0:Q], ACT.Silu).then_inc(sem("gau_u"), 1)
                act.wait_ge(sem("gau_uv"), 3 * c + 3)
                act.activation(base[:, u, :], B[:, k + 2, 0:Q], ACT.Silu).then_inc(sem("gau_base"), 1)
                for pr in range(2):
                    act.wait_ge(sem("gau_v"), 2 * c + pr + 1)
                    act.activation(vtok[:, u, 2 * pr:2 * pr + 2, :],
                                   B[0:SEQ, k + (3 if pr == 0 else 0), :].rearrange("p (i n) -> p i n", i=2),
                                   ACT.Silu).then_inc(sem("gau_vtok"), 1)

            def gau_relu(c):
                act.wait_ge(sem("gau_biased"), c + 1)
                act.activation(relu[:, c % 2], biased[:, c % 2], ACT.Relu, scale=float(1.0 / np.sqrt(np.float32(P)))) \
                   .then_inc(sem("gau_relu"), 1)

            for c in range(0, 4, 2):
                gau_silu(c)
                gau_silu(c + 1)
                gau_relu(c)
                gau_relu(c + 1)

            ln_scalar(act, LN_KEYS)
            for m in range(8):
                def squares(m):
                    act.wait_ge(sem("q_centred"), m + 1)
                    act.activation(halves(sq, m % 2), banks(2 * (m % 2)), ACT.Square, bias=bqc[:, m // 2:m // 2 + 1]) \
                       .then_inc(sem("q_squared"), 1)

                def affine(m):
                    hf = m % 2
                    act.wait_ge(sem("q_z"), m + 1)
                    zz = z[:, hf, :]
                    act.activation(qln[:, m // 2, hf * HALF:(hf + 1) * HALF], zz, ACT.Identity,
                                   bias=col("lnb"), scale=col("lng")).then_inc(sem("q_ln"), 1)
                    act.activation(sq2[:, m // 2, hf * HALF:(hf + 1) * HALF], zz, ACT.Square,
                                   bias=col("lnb"), scale=col("lng")).then_inc(sem("q_ln"), 1)
                if m == 0:
                    squares(0)
                if m + 1 < 8:
                    squares(m + 1)
                act.wait_ge(sem("q_variance"), m + 1)
                act.activation(halves(std, m % 2), banks(4 + 2 * (m % 2)), ACT.Sqrt, bias=col("eps")) \
                   .then_inc(sem("q_std"), 1)
                if m:
                    affine(m - 1)
            affine(7)
            act.wait_ge(sem("q_norm2"), 1)
            act.activation(qn[:, :], B[0:TILE, 0, 0:NT * LISTS], ACT.Sqrt).then_inc(sem("q_norm"), 1)
            for c in range(NT // 2):
                act.wait_ge(sem("pk_inner"), c + 1)
                for j in range(QUAD):
                    r = slice(EB * j, EB * (j + 1))
                    src = B[r, 4:8, 0:2 * TILE].rearrange("p a (i j g) -> p a i j g", i=2, j=QUAD)[:, :, :, j, :]
                    last = act.activation(gelu[r, :, 2 * c * GROUPS:2 * (c + 1) * GROUPS]
                                          .rearrange("p a (i g) -> p a i g", i=2), src, ACT.Gelu)
                last.then_inc(sem("pk_gelu"), 1)

            def queries(i):
                act.activation(qt[:, :, :], qln[:, :, bass.ds(i * TILE, TILE)], ACT.Copy).then_inc(sem("pk_qt"), 1)

            def scores_out(i):
                act.wait_ge(sem("pk_scores"), i + 1)
                act.activation(s1[:, :, :].rearrange("p l e -> p (l e)"), PS[0:TILE, 0:LISTS * KEYS], ACT.Copy) \
                   .then_inc(sem("pk_s1"), 1)

            def transposed_out(i):
                for k in range(3):
                    n = min(8, 20 - 8 * k)
                    act.wait_ge(sem("pk_turned"), i * 3 + k + 1)
                    act.activation(xt[:, 8 * k:8 * k + n, :].rearrange("p k t -> p (k t)"),
                                   PS[0:PAIR, (2 + k) * 512:(3 + k) * 512].bitcast(BF16)[:, 0:n * TILE], ACT.Copy) \
                       .then_inc(sem("pk_xt"), 1)

            def act_tile(i, prev, more):
                if more:
                    act.wait_ge(sem("pk_scores"), i + 1)
                    queries(i + 1)
                if prev:
                    transposed_out(i - 1)
                if more:
                    act.wait_ge(sem("pk_lists"), i + 1)
                    scores_out(i + 1)
                act.wait_ge(sem("pk_dif"), i + 1)
                act.activation(ex[:, :, :], dif[:, :, :], ACT.Exp).then_inc(sem("pk_exp"), 1)

            act.wait_ge(sem("q_ln"), 16)
            queries(0)
            scores_out(0)
            act_tile(0, False, True)
            with act.Fori(1, NT - 1) as i:
                act_tile(i, True, True)
            act_tile(NT - 1, True, False)
            transposed_out(NT - 1)

            ln_scalar(act, LN_BLOCK)
            for g in range(4):
                act.wait_ge(sem("at_v"), g + 1)
                act.activation(vaug[:, 4 * g:4 * g + 4, :, 0:HD],
                               B[0:SEQ, g, :].rearrange("p (i h d) -> p i h d", i=4, h=HEADS),
                               ACT.Copy).then_inc(sem("at_vaug"), 1)

            def exps(i):
                act.wait_ge(sem("at_dif"), i + 1)
                act.activation(pe_[:, :, :], sd[:, :, :], ACT.Exp, scale=float(HD) ** -0.5).then_inc(sem("at_exp"), 1)

            def probs_out(i):
                act.wait_ge(sem("at_turned"), i + 1)
                act.activation(pt[:, :, :].rearrange("p (b h) n -> p b (h n)", b=2),
                               B[0:SEQ, 2:4, 0:4 * SEQ], ACT.Copy).then_inc(sem("at_pt"), 1)

            def context_out(i):
                act.wait_ge(sem("at_cturned"), i + 1)
                act.activation(ct[:, bass.ds(i * SEQ, SEQ)], B[:, 5, 0:SEQ], ACT.Copy).then_inc(sem("at_ct"), 1)

            exps(0)
            with act.Fori(1, IMAGES) as i:
                probs_out(i - 1)
                exps(i)
                context_out(i - 1)
            probs_out(IMAGES - 1)
            context_out(IMAGES - 1)

            ln_scalar(act, LN_POST1)
            for hf in range(2):
                act.wait_ge(sem("ln_done"), 2 * LN_POST1 + hf + 1)
                act.activation(halves(x4, hf), halves(x2, hf), ACT.Identity, bias=col("be1"), scale=col("g1")) \
                   .then_inc(sem("post1"), 1)
            for hf in range(2):
                for k in range(4):
                    act.wait_ge(sem("ff_up"), 4 * hf + k + 1)
                    act.activation(hid[:, k, :].rearrange("p (q n) -> p q n", q=2), banks(2 * (k % 2)), ACT.Relu,
                                   bias=col("b1", k)).then_inc(sem("ff_hid"), 1)
            ln_scalar(act, LN_POST2)
            for hf in range(2):
                act.wait_ge(sem("ln_done"), 2 * LN_POST2 + hf + 1)
                act.activation(halves(x4, hf), halves(x2, hf), ACT.Identity, bias=col("be2"), scale=col("g2")) \
                   .then_inc(sem("post2"), 1)

            ln_scalar(act, LN_MOE)
            act.wait_ge(sem("moe_gdif"), 1)
            act.activation(ge[:, :], gd[:, :], ACT.Exp).then_inc(sem("moe_gexp"), 1)
            for k in range(3):
                n = min(4, NT - 4 * k)
                act.wait_ge(sem("moe_turned"), k + 1)
                act.activation(mt[:, 4 * k * TILE:(4 * k + n) * TILE], B[0:EXPERTS, k, 0:n * TILE], ACT.Copy) \
                   .then_inc(sem("moe_mt"), 1)
            act.sem_inc(sem("moe_hid"), 4)
            act.sem_inc(sem("moe_mb"), 2)
            with act.Fori(0, 4) as c:
                for e in range(EXPERTS):
                    act.wait_ge(sem("moe_down"), c * 8 + e + 1)
                    for k in range(4):
                        act.wait_ge(sem("moe_up"), c * 32 + 4 * e + k + 1)
                        act.activation(mhid[:, e % 2, k, :], B[:, k, 0:Q], ACT.Relu, bias=col("mb1", 4 * e + k)) \
                           .then_inc(sem("moe_hid"), 1)
                    act.wait_ge(sem("moe_tmp"), c * 8 + e + 1)
                    act.wait_ge(sem("moe_mask"), c * 8 + e + 1)
                    act.activation(mb[:, e % 2, :], B[:, 6 + e % 2, 0:Q], ACT.Copy).then_inc(sem("moe_mb"), 1)

        @block.tensor
        def _(pe):
            def tok_out(pe, c):
                if c == 0:
                    loaded(pe, "w3")
                pe.wait_ge(sem("tok_prod"), c + 1)
                if c >= 2:
                    pe.wait_ge(sem("tok_h"), c)
                pe.matmul(B[:, 4 + c % 2, 0:256], L["w3"][:, :], prod[:, c % 2, :], start=True, stop=True) \
                  .then_inc(sem("tok_third"), 1)

            loaded(pe, "ident")
            pe.wait_ge(sem("key_unit"), 2)
            pe.transpose(B[:, 7, 0:KEYS], kk[:, :, :, :].rearrange("p a b c -> p (a b c)"), L["ident"][0:KEYS, 0:KEYS]) \
              .then_inc(sem("key_turned"), 1)
            loaded(pe, "wq")
            loaded(pe, "centre64")
            loaded(pe, "cols")
            for k in range(4):
                pe.matmul(B[:, 6, k * P:(k + 1) * P], L["wq"][:, k, :], L["centre64"][:, :], start=True, stop=True)
            last = pe.matmul(B[:, 5, 0:4], L["centre64"][:, :], cols[:, COLS["bq"][0]:COLS["bq"][0] + 4],
                             start=True, stop=True)
            last.then_inc(sem("wq_centred"), 1)

            pe.wait_ge(sem("tok_weights"), 4)
            loaded(pe, "pat")
            for c in range(4):
                if c >= 2:
                    pe.wait_ge(sem("tok_gate"), 2 * (c - 2) + 2)
                    pe.wait_ge(sem("tok_prod"), c - 1)
                for br in range(2):
                    for k in range(2):
                        last = pe.matmul(B[:, 2 * (c % 2) + br, 0:256], wnt[:, br, k, :],
                                         L["pat"][:, k, c * 256:(c + 1) * 256], start=(k == 0), stop=(k == 1))
                    last.then_inc(sem("tok_linear"), 1)
                if c >= 1:
                    tok_out(pe, c - 1)
            tok_out(pe, 3)

            loaded(pe, "centre")
            ln_tensor(pe, LN_GAU, h, "tok_h", lambda hf: 2 * hf + 3)
            for hf in range(2):
                pe.wait_ge(sem("l2_squared"), hf + 1)
                pe.wait_ge(sem("ln_std"), 2 * LN_GAU + hf + 1)
                for q in range(2):
                    at = (2 * hf + q) * Q
                    last = pe.matmul(B[:, 4 + 2 * hf + q, 0:Q], L["ones"][:, :], sq[:, at:at + Q], start=True, stop=True)
                last.then_inc(sem("l2_sum"), 1)

            def gau_in(c):
                k = 4 * (c % 2)
                pe.wait_ge(sem("l2_done"), c // 2 + 1)
                if c >= 2:
                    pe.wait_ge(sem("gau_h"), c - 1)
                x = x2[:, c * Q:(c + 1) * Q]
                for n, at in ((0, 0), (1, P), (2, 4 * P)):
                    pe.matmul(B[:, k + n, 0:Q], L["uvw"][:, at:at + P], x, start=True, stop=True) \
                      .then_inc(sem("gau_uv"), 1)
                for pr in range(2):
                    if pr:
                        pe.wait_ge(sem("gau_u"), 2 * c + 1)
                    for m in range(2):
                        at = c * Q + (2 * pr + m) * SEQ
                        last = pe.matmul(B[0:SEQ, k + (3 if pr == 0 else 0), m * 256:(m + 1) * 256],
                                         x2[:, at:at + SEQ], L["uvw"][:, 2 * P:4 * P], start=True, stop=True)
                    last.then_inc(sem("gau_v"), 1)

            def gau_scores(c):
                k = 4 * (c % 2)
                pe.wait_ge(sem("gau_qk"), 2 * c + 2)
                for m in range(4):
                    last = pe.matmul(B[0:SEQ, k + 2, m * SEQ:(m + 1) * SEQ], kg[:, c % 2, m * SEQ:(m + 1) * SEQ],
                                     qg[:, c % 2, m * SEQ:(m + 1) * SEQ], start=True, stop=True)
                last.then_inc(sem("gau_scores"), 1)

            def gau_mix(c):
                u, k = c % 2, 4 * (c % 2)
                pe.wait_ge(sem("gau_kernel"), c + 1)
                pe.wait_ge(sem("gau_vtok"), 2 * c + 2)
                for blk in range(2):
                    for m in range(4):
                        last = pe.matmul(B[:, k + (1, 3)[blk], m * SEQ:(m + 1) * SEQ],
                                         vtok[:, u, m, blk * P:(blk + 1) * P], kern[:, u, m, :], start=True, stop=True)
                    last.then_inc(sem("gau_mixed"), 1)
                pe.wait_ge(sem("gau_uo"), 2 * c + 2)
                for blk in range(2):
                    last = pe.matmul(B[:, k + 2, 0:Q], L["ow"][:, blk, :], uo[:, u, blk, :],
                                     start=(blk == 0), stop=(blk == 1))
                last.then_inc(sem("gau_out"), 1)

            loaded(pe, "uvw")
            loaded(pe, "ow")
            for c in range(0, 4, 2):
                gau_in(c)
                gau_in(c + 1)
                gau_scores(c)
                gau_scores(c + 1)
                gau_mix(c)
                gau_mix(c + 1)

            ln_tensor(pe, LN_KEYS, h, "gau_h", lambda hf: 2 * hf + 2)
            pe.wait_ge(sem("wqc_ready"), 2)
            loaded(pe, "mean64")

            def q_centre(m):
                if m >= 2:
                    pe.wait_ge(sem("q_z"), m - 1)
                for q in range(2):
                    at = (2 * (m % 2) + q) * Q
                    last = pe.matmul(B[:, 2 * (m % 2) + q, 0:Q], wqc[:, m // 2, :], x2[:, at:at + Q],
                                     start=True, stop=True)
                last.then_inc(sem("q_centred"), 1)

            pe.wait_ge(sem("ln_done"), 2 * LN_KEYS + 2)
            q_centre(0)
            q_centre(1)
            for m in range(8):
                pe.wait_ge(sem("q_squared"), m + 1)
                if m >= 2:
                    pe.wait_ge(sem("q_std"), m - 1)
                for q in range(2):
                    at = (2 * (m % 2) + q) * Q
                    last = pe.matmul(B[:, 4 + 2 * (m % 2) + q, 0:Q], L["mean64"][:, :], sq[:, at:at + Q],
                                     start=True, stop=True)
                last.then_inc(sem("q_variance"), 1)
                if m + 2 < 8:
                    q_centre(m + 2)
            pe.wait_ge(sem("q_ln"), 16)
            loaded(pe, "blk32")
            for t in range(NT):
                for k in range(4):
                    at = t * LISTS + 4 * k
                    last = pe.matmul(B[0:TILE, 0, at:at + 4], sq2[:, k, t * TILE:(t + 1) * TILE], L["blk32"][:, :],
                                     start=True, stop=True)
            last.then_inc(sem("q_norm2"), 1)
            loaded(pe, "down")
            for c in range(NT // 2):
                if c:
                    pe.wait_ge(sem("pk_gelu"), c)
                for a in range(EA):
                    last = pe.matmul(B[:, 4 + a, 0:2 * TILE], L["down"][:, a, :],
                                     x2[:, 2 * c * TILE:2 * (c + 1) * TILE],
                                     start=True, stop=True)
                last.then_inc(sem("pk_inner"), 1)

            def pk_scores(i):
                pe.wait_ge(sem("pk_qt"), i + 1)
                for k in range(PAIRS):
                    last = pe.matmul(PS[0:TILE, k * 256:(k + 1) * 256], qt[:, k, :], kbd[:, :], start=True, stop=True)
                last.then_inc(sem("pk_scores"), 1)

            def pk_turn(i):
                pe.wait_ge(sem("pk_split"), i * 4 + 4)
                pe.wait_ge(sem("pk_ab"), i * 2 + 2)
                for k in range(5 * PAIRS):
                    if k == 16:
                        pe.wait_ge(sem("pk_h"), i + 1)
                    bank = PS[0:PAIR, (2 + k // 8) * 512:(3 + k // 8) * 512].bitcast(BF16)
                    arr, pr = k // PAIRS, k % PAIRS
                    last = pe.transpose(bank[:, (k % 8) * TILE:(k % 8 + 1) * TILE],
                                        x5[:, arr, pr * PAIR:(pr + 1) * PAIR], L["identb"][0:TILE, 0:TILE])
                    if k % 8 == 7 or k == 5 * PAIRS - 1:
                        last.then_inc(sem("pk_turned"), 1)

            def pk_scatter(i):
                pe.wait_ge(sem("pk_bt"), i + 1)
                pe.wait_ge(sem("pk_aw"), i + 1)
                for g in range(GROUPS):
                    for k in range(PAIRS):
                        last = pe.matmul(
                            B[:, 5 + g // PER_BANK, (g % PER_BANK) * 48:(g % PER_BANK + 1) * 48],
                            bt[:, k, :, :, g].rearrange("p j b -> p (j b)"),
                            aw[:, :, :, k, :].rearrange("p a q (j g) -> p j a q g", j=QUAD)[:, :, :, :, g],
                            start=(k == 0), stop=(k == PAIRS - 1))
                last.then_inc(sem("pk_scattered"), 1)

            def pk_up(i):
                pe.wait_ge(sem("pk_wg"), i * 4 + 4)
                for a in range(EA):
                    last = pe.matmul(B[:, 4, 0:TILE], L["up"][:, a, :], wg[:, a, :], start=(a == 0), stop=(a == EA - 1))
                last.then_inc(sem("pk_out"), 1)

            def pe_tile(i, prev, more):
                if prev:
                    pk_turn(i - 1)
                if more:
                    pe.wait_ge(sem("pk_s1"), i + 1)
                    pk_scores(i + 1)
                if prev:
                    pk_scatter(i - 1)
                    pk_up(i - 1)

            pe.wait_ge(sem("kbd_ready"), 5)
            pe.wait_ge(sem("q_norm"), 1)
            loaded(pe, "identb")
            loaded(pe, "up")
            pk_scores(0)
            pe_tile(0, False, True)
            with pe.Fori(1, NT - 1) as i:
                pe_tile(i, True, True)
            pe_tile(NT - 1, True, False)
            pk_turn(NT - 1)
            pk_scatter(NT - 1)
            pk_up(NT - 1)

            ln_tensor(pe, LN_BLOCK, h, "pk_h", lambda hf: NT + 1)
            loaded(pe, "qkv")
            pe.wait_ge(sem("ln_done"), 2 * LN_BLOCK + 2)
            for hf in range(2):
                for k in range(4):
                    if hf:
                        pe.wait_ge(sem("rot_parts"), k + 1)
                    for q in range(2):
                        at = (2 * hf + q) * Q
                        last = pe.matmul(B[:, 2 * k + q, 0:Q], L["qkv"][:, k, :], x2[:, at:at + Q],
                                         start=True, stop=True)
                    last.then_inc(sem("rot_linear"), 1)
            for g in range(4):
                pe.wait_ge(sem("rot_parts"), 4 + g // 2 + 1)
                for m in range(4):
                    at = (4 * g + m) * SEQ
                    last = pe.matmul(B[0:SEQ, g, m * P:(m + 1) * P], x2[:, at:at + SEQ], L["qkv"][:, 4, :],
                                     start=True, stop=True)
                last.then_inc(sem("at_v"), 1)

            def at_scores(i):
                pe.wait_ge(sem("at_operands"), i * 2 + 2)
                for b in range(2):
                    last = pe.matmul(B[0:SEQ, b, 0:4 * SEQ], qb[:, :],
                                     km[:, 4 * b:4 * b + 4, :].rearrange("p h n -> p (h n)"), start=True, stop=True)
                last.then_inc(sem("at_scores"), 1)

            def at_context(i):
                pe.wait_ge(sem("at_exp"), i + 1)
                for hh in range(HEADS):
                    last = pe.transpose(B[0:SEQ, 2 + hh // 4, (hh % 4) * SEQ:(hh % 4 + 1) * SEQ], pe_[:, hh, :],
                                        L["ident"][0:SEQ, 0:SEQ])
                last.then_inc(sem("at_turned"), 1)

            def at_context2(i):
                pe.wait_ge(sem("at_pt"), i + 1)
                for hh in range(HEADS):
                    last = pe.matmul(B[0:SEQ, 4, hh * (HD + 1):(hh + 1) * (HD + 1)], pt[:, hh, :],
                                     vaug[:, bass.ds(i, 1), hh, :].rearrange("p i d -> p (i d)"),
                                     start=True, stop=True)
                last.then_inc(sem("at_context"), 1)
                pe.wait_ge(sem("at_cn"), i + 1)
                pe.transpose(B[:, 5, 0:SEQ], cn[:, :, :].rearrange("p h d -> p (h d)"), L["ident"][0:SEQ, 0:SEQ]) \
                  .then_inc(sem("at_cturned"), 1)

            pe.wait_ge(sem("at_vaug"), 4)
            pe.wait_ge(sem("vaug_ones"), 1)
            at_scores(0)
            with pe.Fori(1, IMAGES) as i:
                at_context(i - 1)
                pe.wait_ge(sem("at_dif"), i)
                at_scores(i)
                at_context2(i - 1)
            at_context(IMAGES - 1)
            at_context2(IMAGES - 1)

            loaded(pe, "wo")
            pe.wait_ge(sem("at_ct"), IMAGES)
            for hf in range(2):
                for q in range(2):
                    at = (2 * hf + q) * Q
                    last = pe.matmul(B[:, 2 * hf + q, 0:Q], L["wo"][:, :], ct[:, at:at + Q], start=True, stop=True)
                last.then_inc(sem("wo_out"), 1)
            ln_tensor(pe, LN_POST1, xn, "wo_res", lambda hf: hf + 1)
            loaded(pe, "w1")
            loaded(pe, "w2")
            for hf in range(2):
                pe.wait_ge(sem("post1"), 2)
                for k in range(4):
                    if 4 * hf + k >= 2:
                        pe.wait_ge(sem("ff_hid"), 4 * hf + k - 1)
                    for q in range(2):
                        at = (2 * hf + q) * Q
                        last = pe.matmul(B[:, 2 * (k % 2) + q, 0:Q], L["w1"][:, k, :], x4[:, at:at + Q],
                                         start=True, stop=True)
                    last.then_inc(sem("ff_up"), 1)
                pe.wait_ge(sem("ff_hid"), 4 * hf + 4)
                for q in range(2):
                    for k in range(4):
                        last = pe.matmul(B[:, 4 + 2 * hf + q, 0:Q], L["w2"][:, k, :], hid[:, k, q * Q:(q + 1) * Q],
                                         start=(k == 0), stop=(k == 3))
                last.then_inc(sem("ff_down"), 1)
            ln_tensor(pe, LN_POST2, xn, "ff_res", lambda hf: hf + 1)

            ln_tensor(pe, LN_MOE, h, "post_h", lambda hf: hf + 1)
            loaded(pe, "wr")
            pe.wait_ge(sem("ln_done"), 2 * LN_MOE + 2)
            for t in range(NT):
                last = pe.matmul(B[0:TILE, 4, t * EXPERTS:(t + 1) * EXPERTS], x2[:, t * TILE:(t + 1) * TILE],
                                 L["wr"][:, :], start=True, stop=True)
            last.then_inc(sem("moe_logits"), 1)
            pe.wait_ge(sem("moe_gate"), 1)
            for t in range(NT):
                last = pe.transpose(B[0:EXPERTS, t // 4, (t % 4) * TILE:(t % 4 + 1) * TILE], mgate[:, t, :],
                                    L["ident"][0:TILE, 0:TILE])
                if t % 4 == 3 or t == NT - 1:
                    last.then_inc(sem("moe_turned"), 1)
            pe.wait_ge(sem("moe_mt"), 3)
            for name in ("sel8", "mw1", "mw2"):
                loaded(pe, name)
            pe.sem_inc(sem("moe_down"), 2)

            def moe_down(c, e):
                pe.wait_ge(sem("moe_hid"), c * 32 + 4 * e + 8)
                pe.wait_ge(sem("moe_tmp"), c * 8 + e + 1)
                for k in range(4):
                    last = pe.matmul(B[:, 4 + e % 2, 0:Q], L["mw2"][:, e, k, :], mhid[:, e % 2, k, :],
                                     start=(k == 0), stop=(k == 3))
                last.then_inc(sem("moe_down"), 1)

            with pe.Fori(0, 4) as c:
                for e in range(EXPERTS):
                    hold(pe, sem("moe_mb"), c * 8 + e + 1)
                    pe.matmul(B[:, 6 + e % 2, 0:Q], L["sel8"][:, e, :], mt[:, bass.ds(c * Q, Q)],
                              start=True, stop=True).then_inc(sem("moe_mask"), 1)
                    for k in range(4):
                        pe.wait_ge(sem("moe_hid"), c * 32 + 4 * e + k + 1)
                        pe.matmul(B[:, k, 0:Q], L["mw1"][:, e, k * P:(k + 1) * P], x2[:, bass.ds(c * Q, Q)],
                                  start=True, stop=True).then_inc(sem("moe_up"), 1)
                    if e:
                        moe_down(c, e - 1)
                moe_down(c, EXPERTS - 1)

        @block.vector
        def _(dve):
            loaded(dve, "keys")
            dve.tensor_tensor(ksq[:, :, :], L["keys"][:, :, :], L["keys"][:, :, :], ALU.mult).then_inc(sem("key_sq"), 1)
            dve.wait_ge(sem("key_sq"), 1)
            dve.tensor_reduce(kn[:, :], ksq[:, :, :], AX.X, ALU.add).then_inc(sem("key_sum"), 1)
            dve.wait_ge(sem("noise_sqrt"), 1)
            dve.wait_ge(sem("noise_sign"), 1)
            dve.tensor_tensor(noise[:, :], noise[:, :], nsign[:, :], ALU.mult).then_inc(sem("noise_done"), 1)
            dve.wait_ge(sem("noise_done"), 1)
            loaded(dve, "tokw")
            loaded(dve, "cols")
            for br in range(2):
                for k in range(2):
                    dve.scalar_tensor_tensor(wnt[:, br, k, :], noise[:, 6 + br * P:6 + (br + 1) * P],
                                             noise[:, 2 * br + k:2 * br + k + 1], L["tokw"][:, br, 1, k, :],
                                             ALU.mult, ALU.mult).then_inc(sem("tok_sw"), 1)
                dve.scalar_tensor_tensor(bn[:, br:br + 1], col(("w1sb", "w2sb")[br]), noise[:, 4 + br:5 + br],
                                         col(("w1b", "w2b")[br]), ALU.mult, ALU.add).then_inc(sem("tok_bias"), 1)
            for br in range(2):
                for k in range(2):
                    dve.wait_ge(sem("tok_sw"), 2 * br + k + 1)
                    dve.tensor_tensor(wnt[:, br, k, :], wnt[:, br, k, :], L["tokw"][:, br, 0, k, :], ALU.add) \
                       .then_inc(sem("tok_weights"), 1)
            dve.wait_ge(sem("key_norm"), 1)
            dve.tensor_scalar(knc[:, :], kn[:, :], 1e-12, None, ALU.max).then_inc(sem("key_floor"), 1)
            dve.wait_ge(sem("key_floor"), 1)
            dve.reciprocal(kr[:, :], knc[:, :]).then_inc(sem("key_rec"), 1)
            dve.wait_ge(sem("key_rec"), 1)
            for d in range(2):
                dve.tensor_tensor(kk[:, d], L["keys"][:, :, :], kr[:, :].unsqueeze(2).to_broadcast([KEYS, 2, 32]),
                                  ALU.mult).then_inc(sem("key_unit"), 1)
            dve.memset(kbd[:, :], 0.0).then_inc(sem("kbd_ready"), 1)
            dve.memset(wg[:, :, :], 0.0).then_inc(sem("wg_zero"), 1)
            dve.wait_ge(sem("kbd_ready"), 1)
            dve.wait_ge(sem("key_turned"), 1)
            for j in range(4):
                dve.tensor_copy(kbd[32 * j:32 * j + 32, j * KEYS:(j + 1) * KEYS], B[32 * j:32 * j + 32, 7, 0:KEYS]) \
                   .then_inc(sem("kbd_ready"), 1)
            dve.wait_ge(sem("wq_centred"), 1)
            dve.tensor_copy(wqc[:, :, :].rearrange("p k n -> p (k n)"), B[:, 6, :]).then_inc(sem("wqc_ready"), 1)
            dve.tensor_copy(bqc[:, :], B[:, 5, 0:4]).then_inc(sem("wqc_ready"), 1)

            hv = h[:, :].rearrange("p (i s) -> p i s", i=IMAGES)
            dve.tensor_copy(hv[:, :, 0:1], col("cls").unsqueeze(1).to_broadcast([P, IMAGES, 1])) \
               .then_inc(sem("tok_h"), 1)
            dve.wait_ge(sem("tok_bias"), 2)
            loaded(dve, "pos")

            def tok_gate(c):
                u = c % 2
                dve.wait_ge(sem("tok_linear"), 2 * c + 2)
                if c >= 2:
                    dve.wait_ge(sem("tok_mish"), c - 1)
                dve.tensor_scalar(gate[:, u, :], B[:, 2 * u, 0:256], bn[:, 0:1], None, ALU.add) \
                   .then_inc(sem("tok_gate"), 1)
                dve.tensor_scalar(gcap[:, u, :], B[:, 2 * u, 0:256], bn[:, 0:1], 20.0, ALU.add, ALU.min) \
                   .then_inc(sem("tok_gate"), 1)

            def tok_mid(c):
                u = c % 2
                dve.wait_ge(sem("tok_exp"), c + 1)
                dve.scalar_tensor_tensor(gnum[:, u, :], gexp[:, u, :], 2.0, gexp[:, u, :], ALU.add, ALU.mult) \
                   .then_inc(sem("tok_num"), 1)
                dve.wait_ge(sem("tok_den"), c + 1)
                dve.reciprocal(grec[:, u, :], gden[:, u, :]).then_inc(sem("tok_rec"), 1)

            def tok_end(c):
                u = c % 2
                dve.wait_ge(sem("tok_mish"), c + 1)
                dve.scalar_tensor_tensor(prod[:, u, :], B[:, 2 * u + 1, 0:256], bn[:, 1:2], gmul[:, u, :],
                                         ALU.add, ALU.mult).then_inc(sem("tok_prod"), 1)
                dve.wait_ge(sem("tok_third"), c + 1)
                dve.scalar_tensor_tensor(
                    hv[:, 4 * c:4 * c + 4, 1:SEQ], B[:, 4 + u, 0:256].rearrange("p (i s) -> p i s", i=4), col("w3b"),
                    L["pos"][:, :].unsqueeze(1).to_broadcast([P, 4, PATCHES]), ALU.add, ALU.add) \
                    .then_inc(sem("tok_h"), 1)

            tok_gate(0)
            for c in range(4):
                if c + 1 < 4:
                    tok_gate(c + 1)
                tok_mid(c)
                tok_end(c)

            ln_vector(dve, LN_GAU, xn)
            for hf in range(2):
                dve.wait_ge(sem("l2_norm"), hf + 1)
                dve.tensor_scalar(halves(std, hf), halves(norm, hf), 1e-5, None, ALU.max).then_inc(sem("l2_floor"), 1)
                dve.wait_ge(sem("l2_floor"), hf + 1)
                dve.reciprocal(halves(rstd, hf), halves(std, hf)).then_inc(sem("l2_rec"), 1)
                dve.wait_ge(sem("l2_rec"), hf + 1)
                dve.scalar_tensor_tensor(x2[:, hf * HALF:(hf + 1) * HALF], xn[:, hf * HALF:(hf + 1) * HALF], col("g"),
                                         rstd[:, hf * HALF:(hf + 1) * HALF], ALU.mult, ALU.mult) \
                   .then_inc(sem("l2_done"), 1)
            loaded(dve, "relpos")

            def gau_qk(c):
                u = c % 2
                dve.wait_ge(sem("gau_base"), c + 1)
                for k, out in enumerate((qg, kg)):
                    dve.tensor_scalar(out[:, u, :], base[:, u, :], col("gamma", k), col("beta", k), ALU.mult, ALU.add) \
                       .then_inc(sem("gau_qk"), 1)

            def gau_bias(c):
                dve.wait_ge(sem("gau_scores"), c + 1)
                dve.tensor_tensor(biased[:, c % 2], B[0:SEQ, 4 * (c % 2) + 2, 0:Q].rearrange("p (i s) -> p i s", i=4),
                                  L["relpos"][:, :].unsqueeze(1).to_broadcast([SEQ, 4, SEQ]), ALU.add) \
                   .then_inc(sem("gau_biased"), 1)

            def gau_gate(c):
                u, k = c % 2, 4 * (c % 2)
                for blk in range(2):
                    dve.wait_ge(sem("gau_mixed"), 2 * c + blk + 1)
                    dve.tensor_tensor(uo[:, u, blk, :], B[:, k + (1, 3)[blk], 0:Q], ug[:, u, blk, :], ALU.mult) \
                       .then_inc(sem("gau_uo"), 1)

            def gau_add(c):
                u, at = c % 2, c * Q
                dve.wait_ge(sem("gau_out"), c + 1)
                dve.scalar_tensor_tensor(gres[:, u, :], xn[:, at:at + Q], col("res"), B[:, 4 * u + 2, 0:Q],
                                         ALU.mult, ALU.add).then_inc(sem("gau_res"), 1)
                dve.wait_ge(sem("gau_res"), c + 1)
                dve.tensor_tensor(h[:, at:at + Q], h[:, at:at + Q], gres[:, u, :], ALU.add).then_inc(sem("gau_h"), 1)

            for c in range(0, 4, 2):
                gau_qk(c)
                gau_qk(c + 1)
                gau_bias(c)
                gau_bias(c + 1)
                gau_gate(c)
                gau_add(c)
                gau_gate(c + 1)
                gau_add(c + 1)

            ln_vector(dve, LN_KEYS, x2)
            for m in range(8):
                hf = m % 2
                dve.wait_ge(sem("q_std"), m + 1)
                dve.reciprocal(halves(rstd, hf), halves(std, hf)).then_inc(sem("q_rstd"), 1)
                dve.wait_ge(sem("q_rstd"), m + 1)
                if m >= 2:
                    dve.wait_ge(sem("q_ln"), 2 * (m - 2) + 2)
                dve.scalar_tensor_tensor(z[:, hf, :].rearrange("p (q n) -> p q n", q=2), banks(2 * hf),
                                         bqc[:, m // 2:m // 2 + 1], halves(rstd, hf), ALU.add, ALU.mult) \
                   .then_inc(sem("q_z"), 1)
            dve.wait_ge(sem("q_norm"), 1)
            dve.tensor_scalar(qnc[:, :], qn[:, :], 1e-12, None, ALU.max).then_inc(sem("q_floor"), 1)
            dve.wait_ge(sem("q_floor"), 1)
            dve.reciprocal(rn[:, :], qnc[:, :]).then_inc(sem("q_rn"), 1)
            dve.wait_ge(sem("pk_gelu"), NT // 2)
            dve.wait_ge(sem("wg_zero"), 1)
            dve.memset(B[:, 7, (GROUPS - 2 * PER_BANK) * 48:PER_BANK * 48], 0.0).then_inc(sem("pad_zero"), 1)
            dve.wait_ge(sem("q_rn"), 1)
            dve.wait_ge(sem("pad_zero"), 1)

            vals, idxs = vi[:, 0], vi[:, 1]

            def top_lists(i):
                hold(dve, sem("pk_s1"), i + 1)
                for l in range(LISTS):
                    last = dve.max(vals[:, l, 0:8], s1[:, l, :])
                last.then_inc(sem("pk_top8"), 1)
                hold(dve, sem("pk_top8"), i * 2 + 1)
                for l in range(LISTS):
                    dve.max_index(iu[:, l, 0:8], vals[:, l, 0:8], s1[:, l, :])
                    last = dve.match_replace(s2[:, l, :], vals[:, l, 0:8], s1[:, l, :], BIG)
                last.then_inc(sem("pk_lists"), 1)
                hold(dve, sem("pk_lists"), i + 1)
                for l in range(LISTS):
                    last = dve.max(vals[:, l, 8:16], s2[:, l, :])
                last.then_inc(sem("pk_top8"), 1)
                hold(dve, sem("pk_top8"), i * 2 + 2)
                for l in range(LISTS):
                    last = dve.max_index(iu[:, l, 8:16], vals[:, l, 8:16], s2[:, l, :])
                last.then_inc(sem("pk_index"), 1)
                dve.wait_ge(sem("pk_index"), i + 1)
                dve.tensor_tensor(vals, vals, rn[:, bass.ds(i * LISTS, LISTS)].unsqueeze(2)
                                  .to_broadcast([TILE, LISTS, TOP]), ALU.mult).then_inc(sem("pk_vi"), 1)
                dve.tensor_copy(idxs, iu[:, :, :]).then_inc(sem("pk_vi"), 1)

            def onehots(i):
                dve.wait_ge(sem("pk_xt"), i * 3 + 3)
                for a in range(EA):
                    last = dve.tensor_scalar(ah[:, a].rearrange("p c t -> p (c t)"),
                                             xt[:, 3 * PAIRS:4 * PAIRS, :].rearrange("p c t -> p (c t)"),
                                             float(a), None, ALU.is_equal)
                last.then_inc(sem("pk_ah"), 1)
                for b in range(EB):
                    last = dve.tensor_scalar(bt[:, :, :, b, :],
                                             xt[:, 4 * PAIRS:5 * PAIRS, :].rearrange("p c (j g) -> p c j g", j=QUAD),
                                             float(b), None, ALU.is_equal)
                last.then_inc(sem("pk_bt"), 1)

            def candidates(i):
                v = vi[:, :, :, :].rearrange("p k (h l) r -> p (k h) l r", l=2)
                first, second = v[:, :, 0, :], v[:, :, 1, :]
                dve.wait_ge(sem("pk_vi"), i * 2 + 2)
                for r in range(5):
                    n = ROW_LEN[r]
                    dve.tensor_tensor(cc[:, :, ROW_AT[r]:ROW_AT[r] + n],
                                      first[:, :, r:r + 1].to_broadcast([TILE, LISTS, n]), second[:, :, 0:n],
                                      ALU.add).then_inc(sem("pk_cand"), 1)
                dve.tensor_tensor(cc[:, :, ROW_AT[5]:ROW_AT[8]].rearrange("p k (r c) -> p k r c", c=2),
                                  first[:, :, 5:8].unsqueeze(3).to_broadcast([TILE, LISTS, 3, 2]),
                                  second[:, :, 0:2].unsqueeze(2).to_broadcast([TILE, LISTS, 3, 2]),
                                  ALU.add).then_inc(sem("pk_cand"), 1)
                dve.tensor_tensor(cc[:, :, ROW_AT[8]:CAND], first[:, :, 8:16],
                                  second[:, :, 0:1].to_broadcast([TILE, LISTS, 8]), ALU.add) \
                   .then_inc(sem("pk_cand"), 1)
                hold(dve, sem("pk_cand"), i * 7 + 7)
                for k in range(HEADS):
                    last = dve.max(m8[:, k, :], cc[:, k, :])
                last.then_inc(sem("pk_m"), 1)
                hold(dve, sem("pk_m"), i * 3 + 1)
                dve.tensor_tensor(dif[:, :, :], cc[:, 0:HEADS, :], m8[:, :, 0:1].to_broadcast([TILE, HEADS, CAND]),
                                  ALU.subtract).then_inc(sem("pk_dif"), 1)
                for k in range(HEADS):
                    last = dve.match_replace(c2[:, k, :], m8[:, k, :], cc[:, k, :], BIG)
                last.then_inc(sem("pk_m"), 1)
                hold(dve, sem("pk_m"), i * 3 + 2)
                for k in range(HEADS):
                    last = dve.max(m16[:, k, :], c2[:, k, :])
                last.then_inc(sem("pk_m"), 1)
                hold(dve, sem("pk_m"), i * 3 + 3)
                for k in range(HEADS):
                    last = dve.match_replace(c2[:, k, :], m16[:, k, :], c2[:, k, :], BIG)
                last.then_inc(sem("pk_taken"), 1)
                x5v = x5[:, :, :].rearrange("p k (h c) -> p k h c", h=HEADS)
                dve.tensor_scalar(eat[:, :, :], cc[:, HEADS:, :], -15.5, 1.0 / EB, ALU.add, ALU.mult) \
                   .then_inc(sem("pk_eat"), 1)
                dve.wait_ge(sem("pk_eat"), i + 1)
                dve.tensor_scalar(x5v[:, 3], eat[:, :, :], ROUND, ROUND, ALU.add, ALU.subtract) \
                   .then_inc(sem("pk_ab"), 1)
                dve.wait_ge(sem("pk_ab"), i * 2 + 1)
                dve.scalar_tensor_tensor(x5v[:, 4], x5v[:, 3], -float(EB), cc[:, HEADS:, :], ALU.mult, ALU.add) \
                   .then_inc(sem("pk_ab"), 1)

            def weights(i):
                dve.wait_ge(sem("pk_exp"), i + 1)
                dve.wait_ge(sem("pk_taken"), i + 1)
                dve.scalar_tensor_tensor(wu[:, :, :], c2[:, :, :], 0.1 * BIG, ex[:, :, :], ALU.is_lt, ALU.mult) \
                   .then_inc(sem("pk_wu"), 1)
                dve.wait_ge(sem("pk_wu"), i + 1)
                dve.tensor_reduce(wz[:, :], wu[:, :, :], AX.X, ALU.add).then_inc(sem("pk_wz"), 1)
                dve.wait_ge(sem("pk_wz"), i + 1)
                dve.reciprocal(wr[:, :], wz[:, :]).then_inc(sem("pk_wr"), 1)
                dve.wait_ge(sem("pk_wr"), i + 1)
                dve.tensor_tensor(wn[:, :, :], wu[:, :, :], wr[:, :].unsqueeze(2).to_broadcast([TILE, HEADS, CAND]),
                                  ALU.mult).then_inc(sem("pk_weights"), 1)

            def gather_weights(i):
                dve.wait_ge(sem("pk_scattered"), i + 1)
                for j in range(QUAD):
                    r = slice(EB * j, EB * (j + 1))
                    src = B[r, 5:8, 0:PER_BANK * 48].rearrange("p k (g t a q) -> p k g t a q", g=PER_BANK, t=QUAD, q=PARTS)
                    dve.tensor_reduce(wt[r, :, :].rearrange("p (k g) a -> p k g a", k=3), src[:, :, :, j], AX.X,
                                      ALU.add).then_inc(sem("pk_wt"), 1)
                for j in range(QUAD):
                    r = slice(EB * j, EB * (j + 1))
                    dve.wait_ge(sem("pk_wt"), i * 4 + j + 1)
                    dve.tensor_tensor(wg[r, :, j * GROUPS:(j + 1) * GROUPS],
                                      wt[r, 0:GROUPS, :].rearrange("p g a -> p a g"),
                                      gelu[r, :, bass.ds(i * GROUPS, GROUPS)], ALU.mult).then_inc(sem("pk_wg"), 1)

            def add_experts(i):
                dve.wait_ge(sem("pk_out"), i + 1)
                at = bass.ds(i * TILE, TILE)
                dve.tensor_tensor(h[:, at], h[:, at], B[:, 4, 0:TILE], ALU.add).then_inc(sem("pk_h"), 1)

            def dve_tile(i, prev):
                top_lists(i)
                if prev:
                    onehots(i - 1)
                candidates(i)
                if prev:
                    gather_weights(i - 1)
                weights(i)
                if prev:
                    add_experts(i - 1)

            dve.sem_inc(sem("pk_h"), 1)
            dve_tile(0, False)
            with dve.Fori(1, NT) as i:
                dve_tile(i, True)
            onehots(NT - 1)
            gather_weights(NT - 1)
            add_experts(NT - 1)

            dve.memset(vaug[:, :, :, HD:HD + 1], 1.0).then_inc(sem("vaug_ones"), 1)
            ln_vector(dve, LN_BLOCK, x2)
            loaded(dve, "rope")
            for hf in range(2):
                for k in range(4):
                    dve.wait_ge(sem("rot_linear"), 4 * hf + k + 1)
                    if hf and k % 2 == 0:
                        dve.wait_ge(sem("rot_done"), k // 2 + 1)
                    dve.tensor_tensor(rot[:, k // 2, k % 2, :].rearrange("p (q i s) -> p q i s", q=2, i=4),
                                      B[:, 2 * k:2 * k + 2, 0:Q].rearrange("p q (i s) -> p q i s", i=4),
                                      L["rope"][:, k % 2, :].unsqueeze(1).unsqueeze(1).to_broadcast([P, 2, 4, SEQ]),
                                      ALU.mult).then_inc(sem("rot_parts"), 1)

            def at_shift(i):
                dve.wait_ge(sem("at_scores"), i + 1)
                sc = B[0:SEQ, 0:2, 0:4 * SEQ].rearrange("p b (h n) -> p b h n", h=4)
                dve.tensor_reduce(mx[:, :].rearrange("p (b h) -> p b h", b=2), sc, AX.X, ALU.max) \
                   .then_inc(sem("at_max"), 1)
                dve.wait_ge(sem("at_max"), i + 1)
                dve.tensor_tensor(sd[:, :, :].rearrange("p (b h) n -> p b h n", b=2), sc,
                                  mx[:, :].rearrange("p (b h) -> p b h", b=2).unsqueeze(3)
                                  .to_broadcast([SEQ, 2, 4, SEQ]), ALU.subtract).then_inc(sem("at_dif"), 1)

            def at_normalise(i):
                cx = B[0:SEQ, 4, 0:HEADS * (HD + 1)].rearrange("p (h d) -> p h d", h=HEADS)
                dve.wait_ge(sem("at_context"), i + 1)
                dve.reciprocal(rs[:, :], cx[:, :, HD]).then_inc(sem("at_rs"), 1)
                dve.wait_ge(sem("at_rs"), i + 1)
                dve.tensor_tensor(cn[:, :, :], cx[:, :, 0:HD], rs[:, :].unsqueeze(2).to_broadcast([SEQ, HEADS, HD]),
                                  ALU.mult).then_inc(sem("at_cn"), 1)

            at_shift(0)
            with dve.Fori(1, IMAGES) as i:
                dve.wait_ge(sem("at_exp"), i)
                at_shift(i)
                at_normalise(i - 1)
            at_normalise(IMAGES - 1)

            for hf in range(2):
                dve.wait_ge(sem("wo_out"), hf + 1)
                dve.tensor_tensor(halves(xn, hf), banks(2 * hf), halves(x2, hf), ALU.add).then_inc(sem("wo_res"), 1)
            ln_vector(dve, LN_POST1, x2)
            for hf in range(2):
                dve.wait_ge(sem("ff_down"), hf + 1)
                dve.scalar_tensor_tensor(halves(xn, hf), banks(4 + 2 * hf), col("b2"), halves(x4, hf),
                                         ALU.add, ALU.add).then_inc(sem("ff_res"), 1)
            ln_vector(dve, LN_POST2, x2)
            for hf in range(2):
                dve.wait_ge(sem("post2"), hf + 1)
                dve.tensor_tensor(halves(h, hf), halves(h, hf), halves(x4, hf), ALU.add).then_inc(sem("post_h"), 1)

            ln_vector(dve, LN_MOE, x2)
            loaded(dve, "br")
            loaded(dve, "order")
            dve.wait_ge(sem("moe_logits"), 1)
            wide = [TILE, NT, EXPERTS]
            dve.tensor_tensor(lg[:, :, :], B[0:TILE, 4, 0:NT * EXPERTS].rearrange("p (t e) -> p t e", t=NT),
                              L["br"][:, :].unsqueeze(1).to_broadcast(wide), ALU.add).then_inc(sem("moe_route"), 1)
            dve.wait_ge(sem("moe_route"), 1)
            dve.tensor_reduce(lm[:, :], lg[:, :, :], AX.X, ALU.max).then_inc(sem("moe_route"), 1)
            dve.wait_ge(sem("moe_route"), 2)
            dve.tensor_tensor(gd[:, :], lm[:, :], lm[:, :], ALU.subtract).then_inc(sem("moe_gdif"), 1)
            dve.tensor_tensor(leq[:, :, :], lg[:, :, :], lm[:, :].unsqueeze(2).to_broadcast(wide), ALU.is_equal) \
               .then_inc(sem("moe_route"), 1)
            dve.wait_ge(sem("moe_route"), 3)
            dve.tensor_tensor(lord[:, :, :], leq[:, :, :], L["order"][:, :].unsqueeze(1).to_broadcast(wide),
                              ALU.mult).then_inc(sem("moe_route"), 1)
            dve.wait_ge(sem("moe_route"), 4)
            dve.tensor_reduce(lfirst[:, :], lord[:, :, :], AX.X, ALU.max).then_inc(sem("moe_route"), 1)
            dve.wait_ge(sem("moe_route"), 5)
            dve.tensor_tensor(lmask[:, :, :], L["order"][:, :].unsqueeze(1).to_broadcast(wide),
                              lfirst[:, :].unsqueeze(2).to_broadcast(wide), ALU.is_equal).then_inc(sem("moe_route"), 1)
            dve.wait_ge(sem("moe_gexp"), 1)
            dve.reciprocal(gr[:, :], ge[:, :]).then_inc(sem("moe_route"), 1)
            dve.wait_ge(sem("moe_route"), 7)
            dve.tensor_tensor(gg[:, :], ge[:, :], gr[:, :], ALU.mult).then_inc(sem("moe_route"), 1)
            dve.wait_ge(sem("moe_route"), 8)
            dve.tensor_tensor(mgate[:, :, :], lmask[:, :, :], gg[:, :].unsqueeze(2).to_broadcast(wide), ALU.mult) \
               .then_inc(sem("moe_gate"), 1)

            dve.sem_inc(sem("moe_tmp"), 2)
            with dve.Fori(0, 4) as c:
                for e in range(EXPERTS):
                    dve.wait_ge(sem("moe_down"), c * 8 + e + 3)
                    dve.wait_ge(sem("moe_mb"), c * 8 + e + 3)
                    if e:
                        dve.wait_ge(sem("moe_acc"), c * 8 + e)
                    dve.scalar_tensor_tensor((mtmp if e else macc)[:, :], B[:, 4 + e % 2, 0:Q], col("mb2", e),
                                             mb[:, e % 2, :], ALU.add, ALU.mult).then_inc(sem("moe_tmp"), 1)
                    if e:
                        dve.wait_ge(sem("moe_tmp"), c * 8 + e + 3)
                        dve.tensor_tensor(macc[:, :], macc[:, :], mtmp[:, :], ALU.add).then_inc(sem("moe_acc"), 1)
                    else:
                        dve.wait_ge(sem("moe_tmp"), c * 8 + 3)
                        dve.sem_inc(sem("moe_acc"), 1)
                dve.wait_ge(sem("moe_acc"), c * 8 + 8)
                at = bass.ds(c * Q, Q)
                dve.tensor_tensor(h[:, at], h[:, at], macc[:, :], ALU.add).then_inc(sem("out_ready"), 1)
                dve.wait_ge(sem("out_ready"), c + 1)


def layouts(x, cls_tok, **w):
    f = np.float32
    a = {k: np.asarray(v) for k, v in w.items()}
    x = np.asarray(x)
    out = {}
    out["eps"] = np.concatenate(
        [a["L0_tok_eps_in1"].reshape(2, P).T, a["L0_tok_eps_in2"].reshape(2, P).T,
         a["L0_tok_eps_out1"][:, None], a["L0_tok_eps_out2"][:, None],
         np.broadcast_to(a["L0_tok_eps_out1"], (P, P)), np.broadcast_to(a["L0_tok_eps_out2"], (P, P))], axis=1)
    out["keys"] = np.stack([a["L0_ffn_keys0"], a["L0_ffn_keys1"]], axis=1)
    cols = {
        "w1b": a["L0_tok_W1_b"], "w1sb": a["L0_tok_W1_sb"], "w2b": a["L0_tok_W2_b"], "w2sb": a["L0_tok_W2_sb"],
        "w3b": a["L0_tok_W3_b"], "gamma": a["L0_attn_gamma"].T, "beta": a["L0_attn_beta"].T,
        "res": a["L0_attn_res_scale"], "g": np.broadcast_to(a["L0_attn_g"].reshape(1), (P,)),
        "bq": a["L0_ffn_bq"].reshape(4, P).T,
        "lng": np.concatenate([a["L0_ffn_ln_g"]] * 2), "lnb": np.concatenate([a["L0_ffn_ln_b"]] * 2),
        "b1": a["L1_attn_b1"].reshape(4, P).T, "b2": a["L1_attn_b2"], "g1": a["L1_attn_g1"], "be1": a["L1_attn_be1"],
        "g2": a["L1_attn_g2"], "be2": a["L1_attn_be2"], "mb1": a["L1_ffn_b1"].reshape(32, P).T,
        "mb2": a["L1_ffn_b2"].T, "cls": np.asarray(cls_tok).reshape(P), "eps": np.full((P,), 1e-5, f),
    }
    out["cols"] = np.concatenate([cols[k].reshape(P, n) for k, (_, n) in COLS.items()], axis=1)
    out["tokw"] = np.stack([np.stack([a[f"L0_tok_W{br}_{k}"].T.reshape(2, P, P).transpose(1, 0, 2)
                                      for k in ("w", "sw")], axis=1) for br in (1, 2)], axis=1)
    out["pat"] = x.reshape(IMAGES, 8, 16, 8, 16).transpose(2, 4, 0, 1, 3).reshape(2, P, IMAGES * PATCHES) \
        .transpose(1, 0, 2)
    out["ident"] = np.eye(P, dtype=f)
    head = np.arange(P) // 64
    out["centre64"] = (np.eye(P) - (head[:, None] == head) / 64).astype(f)
    out["wq"] = a["L0_ffn_Wq"].reshape(4, P, P).transpose(1, 0, 2)
    out["w3"] = a["L0_tok_W3_w"].T
    div = np.exp(np.arange(0, P, 2, dtype=f) * f(-np.log(10000.0) / P)).astype(f)
    ang = (np.arange(PATCHES, dtype=f)[:, None] * div).astype(f)
    out["pos"] = np.stack([np.sin(ang), np.cos(ang)], axis=-1).reshape(PATCHES, P).T.astype(f)
    out["centre"] = (np.eye(P) - 1.0 / P).astype(f)
    out["mean"] = np.full((P, P), 1.0 / P, f)
    out["ones"] = np.ones((P, P), f)
    out["uvw"] = a["L0_attn_uv_w"]
    out["relpos"] = a["L0_attn_w"][SEQ - 1 + np.arange(SEQ)[:, None] - np.arange(SEQ)[None, :]]
    out["ow"] = a["L0_attn_o_w"].reshape(2, P, P).transpose(1, 0, 2)
    out["mean64"] = ((head[:, None] == head) / 64).astype(f)
    out["blk32"] = (np.arange(P)[:, None] // 32 == np.arange(4)).astype(f)
    out["down"] = np.tile(a["L0_ffn_expert_down"][:P].T.reshape(P, EA, 1, EB), (1, 1, QUAD, 1)).reshape(P, EA, P)
    out["identb"] = np.eye(P, dtype=mybir.dt.np(BF16))
    out["up"] = np.tile(a["L0_ffn_expert_up"][:P].reshape(EA, EB, P).transpose(1, 0, 2), (QUAD, 1, 1))
    swap = np.arange(P) ^ 8
    wq, wk = a["L1_attn_Wq"], a["L1_attn_Wk"]
    out["qkv"] = np.stack([wq.T, wq[swap].T, wk.T, wk[swap].T, a["L1_attn_Wv"].T], axis=1)
    inv = (1.0 / (f(10000.0) ** (np.arange(0, HD, 2, dtype=f) / f(HD)))).astype(f)
    fr = (np.arange(SEQ, dtype=f)[:, None] * inv).astype(f)
    d = np.arange(P) % HD
    out["rope"] = np.stack([np.cos(fr)[:, d % 8].T, np.where(d < 8, -1.0, 1.0)[:, None] * np.sin(fr)[:, d % 8].T],
                           axis=1).astype(f)
    out["headmask"] = (np.arange(P)[:, None] // HD == np.arange(HEADS)).astype(f)
    out["wo"] = a["L1_attn_Wo"].T
    out["w1"] = a["L1_attn_W1"].T.reshape(P, 4, P)
    out["w2"] = a["L1_attn_W2"].T.reshape(4, P, P).transpose(1, 0, 2)
    out["wr"] = a["L1_ffn_Wr"]
    out["br"] = np.broadcast_to(a["L1_ffn_br"], (TILE, EXPERTS))
    out["order"] = np.broadcast_to(np.arange(EXPERTS, 0, -1).astype(f), (TILE, EXPERTS))
    out["sel8"] = np.broadcast_to(np.eye(EXPERTS, dtype=f)[:, :, None], (EXPERTS, EXPERTS, P))
    out["mw2"] = a["L1_ffn_W2"].reshape(EXPERTS, 4, P, P).transpose(2, 0, 1, 3)
    out["mw1"] = a["L1_ffn_W1"].transpose(1, 0, 2)
    return out


def kernel(**inputs):
    import concourse.bacc as _bacc
    from concourse.bass_utils import run_bass_kernel_spmd as _run

    nc = _bacc.Bacc("TRN2", target_bir_lowering=False, num_devices=1)
    arrays, aps = {}, {}
    for name, v in layouts(**inputs).items():
        v = np.ascontiguousarray(v)
        arrays["in_" + name + "_dram"] = v
        aps[name] = nc.dram_tensor("in_" + name + "_dram", v.shape, mybir.dt.from_np(v.dtype), kind="ExternalInput").ap()
    y = nc.dram_tensor("out_dram", (P, T), F32, kind="ExternalOutput").ap()
    build(nc, aps, y)
    r = _run(nc, [arrays], core_ids=[0])
    return np.ascontiguousarray(r.results[0]["out_dram"].T.reshape(IMAGES, SEQ, P))
```

```python
from contextlib import ExitStack

import numpy as np

import concourse.bass as bass
from concourse import mybir

F32 = mybir.dt.float32
BF16 = mybir.dt.bfloat16
U32 = mybir.dt.uint32
ALU = mybir.AluOpType
ACT = mybir.ActivationFunctionType
AX = mybir.AxisListType

P = 128
IMAGES = 16
PATCHES = 64
SEQ = PATCHES + 1
T = IMAGES * SEQ
Q = T // 4
HALF = 2 * Q
EIGHTH = Q // 2
TILE = 104
NT = T // TILE
HEADS = 8
KEYS = 64
TOP = 16
LISTS = 2 * HEADS
DVE_A = 2
DVE_B = 28
ROW_LEN = [TOP // (r + 1) for r in range(TOP)]
ROW_AT = [sum(ROW_LEN[:r]) for r in range(TOP)]
CAND = sum(ROW_LEN)
PAIR = 2 * CAND
PAIRS = HEADS // 2
QUAD = 4
GROUPS = TILE // QUAD
PER_BANK = 9
EA, EB = 4, 32
PARTS = 3
HD = 16
EXPERTS = 8
BIG = -1e30
ROUND = 12582912.0

COLS = {}
for _name, _n in (("w1b", 1), ("w1sb", 1), ("w2b", 1), ("w2sb", 1), ("w3b", 1), ("gamma", 2), ("beta", 2),
                  ("res", 1), ("g", 1), ("bq", 4), ("lng", 1), ("lnb", 1), ("b1", 4), ("b2", 1), ("g1", 1),
                  ("be1", 1), ("g2", 1), ("be2", 1), ("mb1", 32), ("mb2", 8), ("cls", 1), ("eps", 1)):
    COLS[_name] = (sum(n for _, n in COLS.values()), _n)
NCOLS = sum(n for _, n in COLS.values())


LOADS = {
    "first": ("eps", "keys", "cols", "tokw", "ident"),
    "tok": ("pat", "centre64", "wq", "w3", "pos"),
    "gau": ("centre", "mean", "ones", "back", "uvw", "relpos", "ow"),
    "keys": ("mean64", "blk32", "down", "identb", "up"),
    "block": ("qkv", "rope", "headmask", "wo", "w1", "w2"),
    "moe": ("wr", "br", "order", "sel8", "mw2"),
    "mw1": ("mw1",),
}
group_of = {name: group for group, names in LOADS.items() for name in names}


def build(nc, I, y):
    with ExitStack() as ctx:
        def sb(name, shape, dt=F32):
            return ctx.enter_context(nc.sbuf_tensor(name, shape, dt))

        def view(arena, at, *shape):
            n = int(np.prod(shape))
            names = " ".join("abcd"[:len(shape)])
            v = arena[:, at:at + n]
            if len(shape) == 1:
                return v
            return v.rearrange(f"p ({names}) -> p {names}", **dict(zip("abcd", shape)))

        sems = {}

        def sem(name):
            if name not in sems:
                sems[name] = ctx.enter_context(nc.semaphore(name))
            return sems[name]

        PS = ctx.enter_context(nc.psum_tensor("PS", [P, 8 * 512], F32))
        B = PS[:, :].rearrange("p (b n) -> p b n", b=8)

        L = {}
        for name, ap in I.items():
            if name not in ("pat", "tokw", "mw1"):
                L[name] = sb("in_" + name, list(ap.shape), ap.dtype)
        cols = L["cols"]

        def col(name, k=0):
            at = COLS[name][0] + k
            return cols[:, at:at + 1]

        arena1 = sb("arena1", [P, 4 * T])
        arena2 = sb("arena2", [P, 4 * T])
        arena3 = sb("arena3", [P, EB * PAIRS * TILE // 2])
        qln = view(arena1, 0, 4, T)
        L["pat"] = view(arena1, 0, 2, IMAGES * PATCHES)
        L["tokw"] = view(arena1, 2 * IMAGES * PATCHES, 2, 2, 2, P)
        L["mw1"] = view(arena3, 0, EXPERTS, 4 * P)
        ct = view(arena1, 0, T)
        x4 = view(arena1, T, T)
        hid = view(arena1, 2 * T, 4, HALF)
        sq2 = view(arena2, 0, 4, T)
        rot = view(arena2, 0, 2, 2, HALF)
        qr = view(arena2, 2 * T, T)
        kr1 = view(arena2, 3 * T, T)
        bt = arena3[0:PAIR, :].bitcast(BF16).rearrange("p (c j b g) -> p c j b g", c=PAIRS, j=QUAD, b=EB)
        ug = view(arena3, 0, 2, 2, Q)
        uo = view(arena3, 4 * Q, 2, 2, Q)
        gres = view(arena3, 8 * Q, 2, Q)
        vtok = view(arena3, 10 * Q, 2, 4, 2 * P)[0:SEQ]
        biased = view(arena3, 10 * Q + 16 * P, 2, 4, SEQ)[0:SEQ]
        relu = view(arena3, 12 * Q + 16 * P, 2, 4, SEQ)[0:SEQ]
        sd, pt = (view(arena3, EXPERTS * 4 * P + 2 * HEADS * SEQ * k, 2, HEADS, SEQ)[0:SEQ] for k in range(2))
        kern = view(arena3, 14 * Q + 16 * P, 2, 4, SEQ)[0:SEQ]

        arena4 = sb("arena4", [P, 4608])
        arena5 = sb("arena5", [P, IMAGES * HEADS * (HD + 1)])
        arena6 = sb("arena6", [P, 6 * Q])
        gate, gcap, gexp, gnum, gden, grec, gact, gmul, prod = (view(arena4, 512 * k, 2, 256) for k in range(9))
        s1 = view(arena4, 0, LISTS, KEYS)[0:TILE]
        s2 = view(arena4, LISTS * KEYS, LISTS, KEYS)[0:TILE]
        aw = arena4[0:PAIR, 2 * LISTS * KEYS:2 * LISTS * KEYS + EA * PARTS * PAIRS * TILE // 2].bitcast(BF16) \
            .rearrange("p (a q c t) -> p a q c t", a=EA, q=PARTS, c=PAIRS)
        z = view(arena5, 0, 2, HALF)
        km = view(arena4, 0, 2, HEADS, SEQ)
        mt = view(arena1, 0, T)[0:EXPERTS]
        mb = view(arena1, 2 * T, 2, Q)
        mtmp = view(arena1, 3 * T, Q)
        macc = view(arena1, 3 * T + Q, Q)
        vaug = view(arena5, 0, IMAGES, HEADS, HD + 1)[0:SEQ]
        mhid = view(arena5, 0, 2, 4, Q)
        qg, kg, base = (view(arena6, 2 * Q * k, 2, Q) for k in range(3))
        pe_ = view(arena6, 0, 2, HEADS, SEQ)[0:SEQ]

        h = sb("h", [P, T])
        xn = sb("xn", [P, T])
        x2 = sb("x2", [P, T])
        sq = sb("sq", [P, T])
        dev = sb("dev", [P, 2, EIGHTH])
        inv = sb("inv", [P, 2, EIGHTH])

        noise = sb("noise", [P, 262])
        nsign = sb("nsign", [P, 262])
        wnt = sb("wnt", [P, 2, 2, P])
        bn = sb("bn", [P, 2])


        ksq = sb("ksq", [KEYS, 2, 32])
        kn = sb("kn", [KEYS, 2])
        knc = sb("knc", [KEYS, 2])
        kr = sb("kr", [KEYS, 2])
        kk = sb("kk", [KEYS, 2, 2, 32])
        kbd = sb("kbd", [P, 4 * KEYS])
        wqc = sb("wqc", [P, 4, P])
        bqc = sb("bqc", [P, 4])
        qn = sb("qn", [TILE, NT * LISTS])
        qnc = sb("qnc", [TILE, NT * LISTS])
        rn = sb("rn", [TILE, NT * LISTS])
        gelu = sb("gelu", [P, EA, T // QUAD])
        qt = sb("qt", [P, PAIRS, TILE])
        vi = sb("vi", [TILE, 2, LISTS, TOP])
        iu = sb("iu", [TILE, LISTS, TOP], U32)
        cc = sb("cc", [TILE, LISTS, CAND])
        c2 = sb("c2", [TILE, HEADS, CAND])
        m8 = sb("m8", [TILE, HEADS, 8])
        m16 = sb("m16", [TILE, HEADS, 8])
        mneg = sb("mneg", [TILE, HEADS])
        ex = sb("ex", [TILE, HEADS, CAND])
        wu = sb("wu", [TILE, HEADS, CAND])
        wz = sb("wz", [TILE, HEADS])
        wr = sb("wr", [TILE, HEADS])
        wn = sb("wn", [TILE, HEADS, CAND])
        rem = sb("rem", [TILE, HEADS, CAND])
        x4b = sb("x4b", [TILE, PARTS + 1, HEADS * CAND], BF16)
        xt = sb("xt", [PAIR, (PARTS + 1) * PAIRS, TILE], BF16)
        ebf = sb("ebf", [PAIR, PAIRS * TILE], BF16)
        ea = sb("ea", [PAIR, PAIRS * TILE], BF16)
        eb = sb("eb", [PAIR, PAIRS * TILE], BF16)
        ah = sb("ah", [PAIR, EA, PAIRS, TILE], BF16)
        wt = sb("wt", [P, 3 * PER_BANK, EA])
        wg = sb("wg", [P, EA, TILE])

        qb = sb("qb", [P, 2, SEQ])
        mx = sb("mx", [SEQ, 2, HEADS])
        rs = sb("rs", [SEQ, 2, HEADS])
        cn = sb("cn", [SEQ, 2, HEADS, HD])

        lg = sb("lg", [TILE, NT, EXPERTS])
        lm = sb("lm", [TILE, NT])
        leq = sb("leq", [TILE, NT, EXPERTS])
        lord = sb("lord", [TILE, NT, EXPERTS])
        lfirst = sb("lfirst", [TILE, NT])
        lmask = sb("lmask", [TILE, NT, EXPERTS])
        gd = sb("gd", [TILE, NT])
        ge = sb("ge", [TILE, NT])
        gr = sb("gr", [TILE, NT])
        gg = sb("gg", [TILE, NT])
        mgate = sb("mgate", [TILE, NT, EXPERTS])

        block = ctx.enter_context(nc.Block())

        def hold(eng, semaphore, value):
            eng.wait_ge(semaphore, value)
            eng.sem_inc(sem("held"), 1)

        def loaded(eng, name):
            eng.wait_ge(sem("in_" + group_of[name]), 16 * len(LOADS[group_of[name]]))

        def images(ap, n):
            return ap.rearrange("p (i s) -> p i s", i=n)

        def halves(ap, hf):
            return ap[:, hf * HALF:(hf + 1) * HALF].rearrange("p (q n) -> p q n", q=2)

        def banks(first):
            return B[:, first:first + 2, 0:Q]

        def spread(pe, stat, x, hf, bank):
            for q in range(4):
                at = hf * HALF + q * EIGHTH
                last = pe.matmul(B[32 * q:32 * q + 32, bank, 0:EIGHTH], L[stat][:, :], x[:, at:at + EIGHTH],
                                 start=True, stop=True)
            return last

        def gathered(pe, x, bank):
            for q in range(4):
                at = (q % 2) * EIGHTH
                last = pe.matmul(B[:, bank + q // 2, at:at + EIGHTH], L["back"][:, q, :], x, start=True, stop=True)
            return last

        def ln_tensor(pe, n, x, ready, count):
            for hf in range(2):
                pe.wait_ge(sem(ready), count(hf))
                for q in range(2):
                    at = (2 * hf + q) * Q
                    last = pe.matmul(B[:, 2 * hf + q, 0:Q], L["centre"][:, :], x[:, at:at + Q], start=True, stop=True)
                last.then_inc(sem("ln_centred"), 1)
            for hf in range(2):
                pe.wait_ge(sem("ln_squared"), 2 * n + hf + 1)
                spread(pe, "mean", sq, hf, 4 + 2 * hf).then_inc(sem("ln_variance"), 1)
            for hf in range(2):
                pe.wait_ge(sem("ln_inverse"), 2 * n + hf + 1)
                gathered(pe, inv[:, hf, :], 4 + 2 * hf).then_inc(sem("ln_rstd"), 1)

        def ln_scalar(act, n):
            for hf in range(2):
                act.wait_ge(sem("ln_centred"), 2 * n + hf + 1)
                act.activation(halves(sq, hf), banks(2 * hf), ACT.Square).then_inc(sem("ln_squared"), 1)
            for hf in range(2):
                act.wait_ge(sem("ln_variance"), 2 * n + hf + 1)
                act.activation(dev[:, hf, :], B[:, 4 + 2 * hf, 0:EIGHTH], ACT.Sqrt, bias=col("eps")) \
                   .then_inc(sem("ln_std"), 1)

        def ln_vector(dve, n, out):
            for hf in range(2):
                dve.wait_ge(sem("ln_squared"), 2 * n + hf + 1)
                dve.tensor_copy(halves(out, hf), banks(2 * hf)).then_inc(sem("ln_out"), 1)
            for hf in range(2):
                dve.wait_ge(sem("ln_std"), 2 * n + hf + 1)
                dve.reciprocal(inv[:, hf, :], dev[:, hf, :]).then_inc(sem("ln_inverse"), 1)
            for hf in range(2):
                dve.wait_ge(sem("ln_rstd"), 2 * n + hf + 1)
                dve.wait_ge(sem("ln_out"), 2 * n + hf + 1)
                dve.tensor_tensor(halves(out, hf), halves(out, hf), banks(4 + 2 * hf), ALU.mult) \
                   .then_inc(sem("ln_done"), 1)

        LN_GAU, LN_KEYS, LN_BLOCK, LN_POST1, LN_POST2, LN_MOE = range(6)

        def ln_count(n):
            return lambda hf: 2 * n + hf + 1

        @block.sync
        def _(sp):
            for name in group_of:
                if name == "mw1":
                    sp.wait_ge(sem("pk_scattered"), NT)
                sp.dma_start(L[name][tuple(slice(None) for _ in I[name].shape)], I[name]).then_inc(sem("in_" + group_of[name]), 16)
            sp.wait_ge(sem("out_ready"), 4)
            sp.dma_start(y, h[:, :]).then_inc(sem("out_stored"), 16)
            sp.wait_ge(sem("out_stored"), 16)

        @block.gpsimd
        def _(pool):
            for c in range(4):
                u = c % 2
                pool.wait_ge(sem("tok_num"), c + 1)
                pool.tensor_scalar(gden[:, u, :], gnum[:, u, :], 2.0, None, ALU.add).then_inc(sem("tok_den"), 1)
                pool.wait_ge(sem("tok_rec"), c + 1)
                pool.tensor_tensor(gact[:, u, :], gnum[:, u, :], grec[:, u, :], ALU.mult).then_inc(sem("tok_tanh"), 1)
                pool.wait_ge(sem("tok_tanh"), c + 1)
                pool.tensor_tensor(gmul[:, u, :], gact[:, u, :], gate[:, u, :], ALU.mult).then_inc(sem("tok_mish"), 1)
            for c in range(4):
                pool.wait_ge(sem("gau_relu"), c + 1)
                pool.tensor_tensor(kern[:, c % 2], relu[:, c % 2], relu[:, c % 2], ALU.mult) \
                    .then_inc(sem("gau_kernel"), 1)

            def onehot_weights(first=0):
                for a in range(first, EA):
                    last = pool.tensor_tensor(
                        aw[:, a].rearrange("p q c t -> p q (c t)"),
                        ah[:, a].rearrange("p c t -> p (c t)").unsqueeze(1).to_broadcast([PAIR, PARTS, PAIRS * TILE]),
                        xt[:, 0:PARTS * PAIRS, :].rearrange("p (q c) t -> p q (c t)", q=PARTS), ALU.mult)
                last.then_inc(sem("pk_aw"), 1)

            def scaled_values(i):
                hold(pool, sem("pk_index"), i + 1)
                pool.tensor_tensor(vi[:, 0], vi[:, 0], rn[:, bass.ds(i * LISTS, LISTS)].unsqueeze(2)
                                   .to_broadcast([TILE, LISTS, TOP]), ALU.mult).then_inc(sem("pk_values"), 1)

            def onehots(i):
                hold(pool, sem("pk_ab"), i * 3 + 3)
                for b in range(DVE_B, EB):
                    last = pool.tensor_scalar(bt[:, :, :, b, :], eb.rearrange("p (c j g) -> p c j g", c=PAIRS, j=QUAD),
                                              float(b), None, ALU.is_equal)
                last.then_inc(sem("pk_bt_pool"), 1)

            def weight_parts(i):
                parts = x4b[:, :, :].rearrange("p k (h c) -> p k h c", h=HEADS)
                hold(pool, sem("pk_sum"), i * 3 + 3)
                pool.tensor_tensor(wn[:, :, :], wu[:, :, :], wr[:, :].unsqueeze(2).to_broadcast([TILE, HEADS, CAND]),
                                   ALU.mult).then_inc(sem("pk_weights"), 1)
                hold(pool, sem("pk_part0"), i + 1)
                pool.tensor_tensor(rem[:, :, :], wn[:, :, :], parts[:, 0], ALU.subtract).then_inc(sem("pk_rem"), 1)
                hold(pool, sem("pk_part1"), i + 1)
                pool.tensor_tensor(parts[:, 2], rem[:, :, :], parts[:, 1], ALU.subtract).then_inc(sem("pk_part2"), 1)

            def pool_tile(i, prev):
                scaled_values(i)
                if prev:
                    pool.wait_ge(sem("pk_ah"), i)
                    onehot_weights()
                    onehots(i - 1)
                weight_parts(i)

            pool.wait_ge(sem("q_inorm"), 2)
            pool_tile(0, False)
            with pool.Fori(1, NT) as i:
                pool_tile(i, True)
            pool.wait_ge(sem("pk_ah"), NT)
            onehot_weights(DVE_A)

            for hf in range(2):
                for k, out in ((0, qr), (1, kr1)):
                    pool.wait_ge(sem("rot_parts"), 4 * hf + 2 * k + 2)
                    pool.tensor_tensor(out[:, hf * HALF:(hf + 1) * HALF], rot[:, k, 0], rot[:, k, 1], ALU.add) \
                        .then_inc(sem("rot_done"), 1)

            def head_keys(i, u):
                pool.tensor_copy(qb[:, u, :], qr[:, bass.ds(i * SEQ, SEQ)]).then_inc(sem("at_operands"), 1)
                pool.tensor_tensor(
                    km[:, u, :, :], kr1[:, bass.ds(i * SEQ, SEQ)].unsqueeze(1).to_broadcast([P, HEADS, SEQ]),
                    L["headmask"][:, :].unsqueeze(2).to_broadcast([P, HEADS, SEQ]), ALU.mult) \
                    .then_inc(sem("at_operands"), 1)

            pool.wait_ge(sem("rot_done"), 4)
            loaded(pool, "headmask")
            head_keys(0, 0)
            head_keys(1, 1)
            with pool.Fori(1, IMAGES // 2) as p:
                for u in range(2):
                    hold(pool, sem("at_scores"), p * 2 + u - 1)
                    head_keys(p * 2 + u, u)

        @block.scalar
        def _(act):
            loaded(act, "eps")
            act.activation(noise[:, :], L["eps"][:, :], ACT.Abs).then_inc(sem("noise_root"), 1)
            act.activation(nsign[:, :], L["eps"][:, :], ACT.Sign).then_inc(sem("noise_root"), 1)
            act.wait_ge(sem("noise_root"), 1)
            act.activation(noise[:, :], noise[:, :], ACT.Sqrt).then_inc(sem("noise_root"), 1)
            act.wait_ge(sem("key_steps"), 2)
            act.activation(kn[:, :], kn[:, :], ACT.Sqrt).then_inc(sem("key_norm"), 1)
            for c in range(4):
                act.wait_ge(sem("tok_gate"), 2 * c + 2)
                act.activation(gexp[:, c % 2, :], gcap[:, c % 2, :], ACT.Exp).then_inc(sem("tok_exp"), 1)

            ln_scalar(act, LN_GAU)
            for hf in range(2):
                act.wait_ge(sem("ln_done"), 2 * LN_GAU + hf + 1)
                act.activation(halves(sq, hf), halves(xn, hf), ACT.Square).then_inc(sem("l2_squared"), 1)
            for hf in range(2):
                act.wait_ge(sem("l2_sum"), hf + 1)
                act.activation(dev[:, hf, :], B[:, 4 + 2 * hf, 0:EIGHTH], ACT.Sqrt).then_inc(sem("l2_norm"), 1)
            def gau_silu(c):
                u = c % 2
                k = 4 * u
                for blk in range(2):
                    act.wait_ge(sem("gau_uv"), 3 * c + blk + 1)
                    act.activation(ug[:, u, blk, :], B[:, k + blk, 0:Q], ACT.Silu).then_inc(sem("gau_u"), 1)
                act.wait_ge(sem("gau_uv"), 3 * c + 3)
                act.activation(base[:, u, :], B[:, k + 2, 0:Q], ACT.Silu).then_inc(sem("gau_base"), 1)
                for pr in range(2):
                    act.wait_ge(sem("gau_v"), 2 * c + pr + 1)
                    act.activation(vtok[:, u, 2 * pr:2 * pr + 2, :],
                                   B[0:SEQ, k + (3 if pr == 0 else 0), :].rearrange("p (i n) -> p i n", i=2),
                                   ACT.Silu).then_inc(sem("gau_vtok"), 1)

            def gau_relu(c):
                act.wait_ge(sem("gau_biased"), c + 1)
                act.activation(relu[:, c % 2], biased[:, c % 2], ACT.Relu, scale=float(1.0 / np.sqrt(np.float32(P)))) \
                   .then_inc(sem("gau_relu"), 1)

            for c in range(0, 4, 2):
                gau_silu(c)
                gau_silu(c + 1)
                gau_relu(c)
                gau_relu(c + 1)

            ln_scalar(act, LN_KEYS)
            for m in range(8):
                def squares(m):
                    act.wait_ge(sem("q_centred"), m + 1)
                    act.activation(halves(sq, m % 2), banks(2 * (m % 2)), ACT.Square, bias=bqc[:, m // 2:m // 2 + 1]) \
                       .then_inc(sem("q_squared"), 1)

                def affine(m):
                    hf = m % 2
                    act.wait_ge(sem("q_z"), m + 1)
                    zz = z[:, hf, :]
                    act.activation(qln[:, m // 2, hf * HALF:(hf + 1) * HALF], zz, ACT.Identity,
                                   bias=col("lnb"), scale=col("lng")).then_inc(sem("q_ln"), 1)
                    act.activation(sq2[:, m // 2, hf * HALF:(hf + 1) * HALF], zz, ACT.Square,
                                   bias=col("lnb"), scale=col("lng")).then_inc(sem("q_ln"), 1)
                if m == 0:
                    squares(0)
                if m + 1 < 8:
                    squares(m + 1)
                act.wait_ge(sem("q_variance"), m + 1)
                act.activation(dev[:, m % 2, :], B[:, 4 + 2 * (m % 2), 0:EIGHTH], ACT.Sqrt, bias=col("eps")) \
                   .then_inc(sem("q_std"), 1)
                if m:
                    affine(m - 1)
            affine(7)
            def queries(i):
                act.activation(qt[:, :, :], qln[:, :, bass.ds(i * TILE, TILE)], ACT.Copy).then_inc(sem("pk_qt"), 1)

            def scores_out(i):
                act.wait_ge(sem("pk_scores"), i + 1)
                act.activation(s1[:, :, :].rearrange("p l e -> p (l e)"), PS[0:TILE, 0:LISTS * KEYS], ACT.Copy) \
                   .then_inc(sem("pk_s1"), 1)

            def indices_out(i):
                act.wait_ge(sem("pk_index"), i + 1)
                act.activation(vi[:, 1].rearrange("p l r -> p (l r)"), iu[:, :, :].rearrange("p l r -> p (l r)"),
                               ACT.Copy).then_inc(sem("pk_indices"), 1)

            def transposed_out(i):
                for k in range(2):
                    act.wait_ge(sem("pk_turned"), i * 2 + k + 1)
                    act.activation(xt[:, 8 * k:8 * k + 8, :].rearrange("p k t -> p (k t)"),
                                   PS[0:PAIR, (2 + k) * 512:(3 + k) * 512].bitcast(BF16)[:, 0:8 * TILE], ACT.Copy) \
                       .then_inc(sem("pk_xt"), 1)

            def softmax_terms(i):
                act.wait_ge(sem("pk_cand"), i * 7 + 7)
                act.activation(x4b[:, PARTS, :], cc[:, HEADS:, :].rearrange("p h c -> p (h c)"), ACT.Copy) \
                   .then_inc(sem("pk_expert"), 1)
                act.wait_ge(sem("pk_mneg"), i + 1)
                for k in range(HEADS):
                    last = act.activation(ex[:, k, :], cc[:, k, :], ACT.Exp, bias=mneg[:, k:k + 1])
                last.then_inc(sem("pk_exp"), 1)

            def weight_parts(i):
                act.wait_ge(sem("pk_weights"), i + 1)
                act.activation(x4b[:, 0, :], wn[:, :, :].rearrange("p h c -> p (h c)"), ACT.Copy) \
                   .then_inc(sem("pk_part0"), 1)
                act.wait_ge(sem("pk_rem"), i + 1)
                act.activation(x4b[:, 1, :], rem[:, :, :].rearrange("p h c -> p (h c)"), ACT.Copy) \
                   .then_inc(sem("pk_part1"), 1)

            def act_tile(i, prev, more):
                if more:
                    act.wait_ge(sem("pk_scores"), i + 1)
                    queries(i + 1)
                if prev:
                    transposed_out(i - 1)
                if more:
                    act.wait_ge(sem("pk_lists"), i + 1)
                    scores_out(i + 1)
                indices_out(i)
                softmax_terms(i)
                weight_parts(i)

            act.wait_ge(sem("q_ln"), 16)
            queries(0)
            scores_out(0)
            for c in range(NT // 2):
                act.wait_ge(sem("pk_inner"), c + 1)
                for j in range(QUAD):
                    r = slice(EB * j, EB * (j + 1))
                    src = B[r, 4:8, 0:2 * TILE].rearrange("p a (i j g) -> p a i j g", i=2, j=QUAD)[:, :, :, j, :]
                    last = act.activation(gelu[r, :, 2 * c * GROUPS:2 * (c + 1) * GROUPS]
                                          .rearrange("p a (i g) -> p a i g", i=2), src, ACT.Gelu)
                last.then_inc(sem("pk_gelu"), 1)
            act.wait_ge(sem("q_norm2"), 1)
            act.activation(qn[:, :], B[0:TILE, 2, 0:NT * LISTS], ACT.Sqrt).then_inc(sem("q_norm"), 1)
            act_tile(0, False, True)
            with act.Fori(1, NT - 1) as i:
                act_tile(i, True, True)
            act_tile(NT - 1, True, False)
            transposed_out(NT - 1)

            ln_scalar(act, LN_BLOCK)
            for g in range(4):
                act.wait_ge(sem("at_v"), g + 1)
                act.activation(vaug[:, 4 * g:4 * g + 4, :, 0:HD],
                               B[0:SEQ, g, :].rearrange("p (i h d) -> p i h d", i=4, h=HEADS),
                               ACT.Copy).then_inc(sem("at_vaug"), 1)

            def exps(i, u):
                act.wait_ge(sem("at_dif"), i + 1)
                act.activation(pe_[:, u, :, :], sd[:, u, :, :], ACT.Exp, scale=float(HD) ** -0.5) \
                   .then_inc(sem("at_exp"), 1)

            def probs_out(i, u):
                act.wait_ge(sem("at_turned"), i + 1)
                act.activation(pt[:, u, :, :].rearrange("p (b h) n -> p b (h n)", b=2),
                               B[0:SEQ, 4:6, 0:4 * SEQ], ACT.Copy).then_inc(sem("at_pt"), 1)

            def context_out(i):
                act.wait_ge(sem("at_cturned"), i + 1)
                act.activation(ct[:, bass.ds(i * SEQ, SEQ)], B[:, 7, 0:SEQ], ACT.Copy).then_inc(sem("at_ct"), 1)

            exps(0, 0)
            probs_out(0, 0)
            exps(1, 1)
            with act.Fori(1, IMAGES // 2) as p:
                for u in range(2):
                    probs_out(p * 2 + u - 1, 1 - u)
                    exps(p * 2 + u, u)
                    context_out(p * 2 + u - 2)
            probs_out(IMAGES - 1, 1)
            context_out(IMAGES - 2)
            context_out(IMAGES - 1)

            ln_scalar(act, LN_POST1)
            for hf in range(2):
                act.wait_ge(sem("ln_done"), 2 * LN_POST1 + hf + 1)
                act.activation(halves(x4, hf), halves(x2, hf), ACT.Identity, bias=col("be1"), scale=col("g1")) \
                   .then_inc(sem("post1"), 1)
            for hf in range(2):
                for k in range(4):
                    act.wait_ge(sem("ff_up"), 4 * hf + k + 1)
                    act.activation(hid[:, k, :].rearrange("p (q n) -> p q n", q=2), banks(2 * (k % 2)), ACT.Relu,
                                   bias=col("b1", k)).then_inc(sem("ff_hid"), 1)
            ln_scalar(act, LN_POST2)
            for hf in range(2):
                act.wait_ge(sem("ln_done"), 2 * LN_POST2 + hf + 1)
                act.activation(halves(x4, hf), halves(x2, hf), ACT.Identity, bias=col("be2"), scale=col("g2")) \
                   .then_inc(sem("post2"), 1)

            ln_scalar(act, LN_MOE)
            act.wait_ge(sem("moe_gdif"), 1)
            act.activation(ge[:, :], gd[:, :], ACT.Exp).then_inc(sem("moe_gexp"), 1)
            for k in range(3):
                n = min(4, NT - 4 * k)
                act.wait_ge(sem("moe_turned"), k + 1)
                act.activation(mt[:, 4 * k * TILE:(4 * k + n) * TILE], B[0:EXPERTS, k, 0:n * TILE], ACT.Copy) \
                   .then_inc(sem("moe_mt"), 1)
            act.sem_inc(sem("moe_hid"), 4)
            act.sem_inc(sem("moe_mb"), 2)
            with act.Fori(0, 4) as c:
                for e in range(EXPERTS):
                    act.wait_ge(sem("moe_down"), c * 8 + e + 1)
                    for k in range(4):
                        act.wait_ge(sem("moe_up"), c * 32 + 4 * e + k + 1)
                        act.activation(mhid[:, e % 2, k, :], B[:, k, 0:Q], ACT.Relu, bias=col("mb1", 4 * e + k)) \
                           .then_inc(sem("moe_hid"), 1)
                    act.wait_ge(sem("moe_tmp"), c * 8 + e + 1)
                    act.wait_ge(sem("moe_mask"), c * 8 + e + 1)
                    act.activation(mb[:, e % 2, :], B[:, 6 + e % 2, 0:Q], ACT.Copy).then_inc(sem("moe_mb"), 1)

        @block.tensor
        def _(pe):
            def tok_out(pe, c):
                if c == 0:
                    loaded(pe, "w3")
                pe.wait_ge(sem("tok_prod"), c + 1)
                if c >= 2:
                    pe.wait_ge(sem("tok_h"), c)
                pe.matmul(B[:, 4 + c % 2, 0:256], L["w3"][:, :], prod[:, c % 2, :], start=True, stop=True) \
                  .then_inc(sem("tok_third"), 1)

            loaded(pe, "ident")
            pe.wait_ge(sem("key_unit"), 2)
            pe.transpose(B[:, 7, 0:KEYS], kk[:, :, :, :].rearrange("p a b c -> p (a b c)"), L["ident"][0:KEYS, 0:KEYS]) \
              .then_inc(sem("key_turned"), 1)
            loaded(pe, "wq")
            loaded(pe, "centre64")
            loaded(pe, "cols")
            for k in range(4):
                pe.matmul(B[:, 6, k * P:(k + 1) * P], L["wq"][:, k, :], L["centre64"][:, :], start=True, stop=True)
            last = pe.matmul(B[:, 5, 0:4], L["centre64"][:, :], cols[:, COLS["bq"][0]:COLS["bq"][0] + 4],
                             start=True, stop=True)
            last.then_inc(sem("wq_centred"), 1)

            pe.wait_ge(sem("tok_weights"), 4)
            loaded(pe, "pat")
            for c in range(4):
                if c >= 2:
                    pe.wait_ge(sem("tok_gate"), 2 * (c - 2) + 2)
                    pe.wait_ge(sem("tok_prod"), c - 1)
                for br in range(2):
                    for k in range(2):
                        last = pe.matmul(B[:, 2 * (c % 2) + br, 0:256], wnt[:, br, k, :],
                                         L["pat"][:, k, c * 256:(c + 1) * 256], start=(k == 0), stop=(k == 1))
                    last.then_inc(sem("tok_linear"), 1)
                if c >= 1:
                    tok_out(pe, c - 1)
            tok_out(pe, 3)

            loaded(pe, "centre")
            ln_tensor(pe, LN_GAU, h, "tok_h", lambda hf: 2 * hf + 3)
            for hf in range(2):
                pe.wait_ge(sem("l2_squared"), hf + 1)
                spread(pe, "ones", sq, hf, 4 + 2 * hf).then_inc(sem("l2_sum"), 1)
            for hf in range(2):
                pe.wait_ge(sem("l2_rec"), hf + 1)
                gathered(pe, inv[:, hf, :], 4 + 2 * hf).then_inc(sem("l2_inverse"), 1)

            def gau_in(c):
                k = 4 * (c % 2)
                pe.wait_ge(sem("l2_done"), min(c + 1, 2))
                if c >= 2:
                    pe.wait_ge(sem("gau_h"), c - 1)
                x = x2[:, c * Q:(c + 1) * Q]
                for n, at in ((0, 0), (1, P), (2, 4 * P)):
                    pe.matmul(B[:, k + n, 0:Q], L["uvw"][:, at:at + P], x, start=True, stop=True) \
                      .then_inc(sem("gau_uv"), 1)
                for pr in range(2):
                    if pr:
                        pe.wait_ge(sem("gau_u"), 2 * c + 1)
                    for m in range(2):
                        at = c * Q + (2 * pr + m) * SEQ
                        last = pe.matmul(B[0:SEQ, k + (3 if pr == 0 else 0), m * 256:(m + 1) * 256],
                                         x2[:, at:at + SEQ], L["uvw"][:, 2 * P:4 * P], start=True, stop=True)
                    last.then_inc(sem("gau_v"), 1)

            def gau_scores(c):
                k = 4 * (c % 2)
                pe.wait_ge(sem("gau_qk"), 2 * c + 2)
                for m in range(4):
                    last = pe.matmul(B[0:SEQ, k + 2, m * SEQ:(m + 1) * SEQ], kg[:, c % 2, m * SEQ:(m + 1) * SEQ],
                                     qg[:, c % 2, m * SEQ:(m + 1) * SEQ], start=True, stop=True)
                last.then_inc(sem("gau_scores"), 1)

            def gau_mix(c):
                u, k = c % 2, 4 * (c % 2)
                pe.wait_ge(sem("gau_kernel"), c + 1)
                pe.wait_ge(sem("gau_vtok"), 2 * c + 2)
                for blk in range(2):
                    for m in range(4):
                        last = pe.matmul(B[:, k + (1, 3)[blk], m * SEQ:(m + 1) * SEQ],
                                         vtok[:, u, m, blk * P:(blk + 1) * P], kern[:, u, m, :], start=True, stop=True)
                    last.then_inc(sem("gau_mixed"), 1)
                pe.wait_ge(sem("gau_uo"), 2 * c + 2)
                for blk in range(2):
                    last = pe.matmul(B[:, k + 2, 0:Q], L["ow"][:, blk, :], uo[:, u, blk, :],
                                     start=(blk == 0), stop=(blk == 1))
                last.then_inc(sem("gau_out"), 1)

            loaded(pe, "uvw")
            loaded(pe, "ow")
            for c in range(0, 4, 2):
                gau_in(c)
                gau_in(c + 1)
                gau_scores(c)
                gau_scores(c + 1)
                gau_mix(c)
                gau_mix(c + 1)

            ln_tensor(pe, LN_KEYS, h, "gau_h", lambda hf: 2 * hf + 2)
            pe.wait_ge(sem("wqc_ready"), 2)
            loaded(pe, "mean64")

            def q_centre(m):
                if m >= 2:
                    pe.wait_ge(sem("q_shifted"), m - 1)
                for q in range(2):
                    at = (2 * (m % 2) + q) * Q
                    last = pe.matmul(B[:, 2 * (m % 2) + q, 0:Q], wqc[:, m // 2, :], x2[:, at:at + Q],
                                     start=True, stop=True)
                last.then_inc(sem("q_centred"), 1)

            pe.wait_ge(sem("ln_done"), 2 * LN_KEYS + 2)
            q_centre(0)
            q_centre(1)
            for m in range(8):
                pe.wait_ge(sem("q_squared"), m + 1)
                if m >= 2:
                    pe.wait_ge(sem("q_z"), m - 1)
                spread(pe, "mean64", sq, m % 2, 4 + 2 * (m % 2)).then_inc(sem("q_variance"), 1)
                if 1 <= m < 7:
                    q_centre(m + 1)
                pe.wait_ge(sem("q_inverse"), m + 1)
                gathered(pe, inv[:, m % 2, :], 4 + 2 * (m % 2)).then_inc(sem("q_rstd"), 1)
            def pk_scores(i):
                pe.wait_ge(sem("pk_qt"), i + 1)
                for k in range(PAIRS):
                    last = pe.matmul(PS[0:TILE, k * 256:(k + 1) * 256], qt[:, k, :], kbd[:, :], start=True, stop=True)
                last.then_inc(sem("pk_scores"), 1)

            def pk_turn(i):
                pe.wait_ge(sem("pk_part2"), i + 1)
                pe.wait_ge(sem("pk_expert"), i + 1)
                for k in range((PARTS + 1) * PAIRS):
                    bank = PS[0:PAIR, (2 + k // 8) * 512:(3 + k // 8) * 512].bitcast(BF16)
                    arr, pr = k // PAIRS, k % PAIRS
                    last = pe.transpose(bank[:, (k % 8) * TILE:(k % 8 + 1) * TILE],
                                        x4b[:, arr, pr * PAIR:(pr + 1) * PAIR], L["identb"][0:TILE, 0:TILE])
                    if k % 8 == 7:
                        last.then_inc(sem("pk_turned"), 1)

            def pk_scatter(i):
                pe.wait_ge(sem("pk_bt"), i + 1)
                pe.wait_ge(sem("pk_bt_pool"), i + 1)
                pe.wait_ge(sem("pk_aw"), i + 1)
                for g in range(GROUPS):
                    for k in range(PAIRS):
                        last = pe.matmul(
                            B[:, 5 + g // PER_BANK, (g % PER_BANK) * 48:(g % PER_BANK + 1) * 48],
                            bt[:, k, :, :, g].rearrange("p j b -> p (j b)"),
                            aw[:, :, :, k, :].rearrange("p a q (j g) -> p j a q g", j=QUAD)[:, :, :, :, g],
                            start=(k == 0), stop=(k == PAIRS - 1))
                last.then_inc(sem("pk_scattered"), 1)

            def pk_up(i):
                pe.wait_ge(sem("pk_wg"), i * 4 + 4)
                pe.wait_ge(sem("pk_h"), i + 1)
                for a in range(EA):
                    last = pe.matmul(B[:, 4, 0:TILE], L["up"][:, a, :], wg[:, a, :], start=(a == 0), stop=(a == EA - 1))
                last.then_inc(sem("pk_out"), 1)

            def pe_tile(i, prev, more):
                if prev:
                    pk_turn(i - 1)
                if more:
                    pe.wait_ge(sem("pk_s1"), i + 1)
                    pk_scores(i + 1)
                if prev == 2:
                    pk_up(i - 2)
                if prev:
                    pk_scatter(i - 1)

            pe.wait_ge(sem("kbd_ready"), 5)
            loaded(pe, "identb")
            loaded(pe, "up")
            pk_scores(0)
            loaded(pe, "down")
            pe.wait_ge(sem("q_ln"), 16)
            loaded(pe, "blk32")
            for c in range(NT // 2):
                if c:
                    pe.wait_ge(sem("pk_gelu"), c)
                for a in range(EA):
                    last = pe.matmul(B[:, 4 + a, 0:2 * TILE], L["down"][:, a, :],
                                     x2[:, 2 * c * TILE:2 * (c + 1) * TILE],
                                     start=True, stop=True)
                last.then_inc(sem("pk_inner"), 1)
                for t in range(2 * c, 2 * c + 2):
                    for k in range(4):
                        at = t * LISTS + 4 * k
                        last = pe.matmul(B[0:TILE, 2, at:at + 4], sq2[:, k, t * TILE:(t + 1) * TILE], L["blk32"][:, :],
                                         start=True, stop=True)
            last.then_inc(sem("q_norm2"), 1)
            pe_tile(0, 0, True)
            pe.wait_ge(sem("q_norm"), 1)
            pe.wait_ge(sem("pk_gelu"), NT // 2)
            pe_tile(1, 1, True)
            with pe.Fori(2, NT - 1) as i:
                pe_tile(i, 2, True)
            pe_tile(NT - 1, 2, False)
            pk_turn(NT - 1)
            pk_up(NT - 2)
            pk_scatter(NT - 1)
            pk_up(NT - 1)

            ln_tensor(pe, LN_BLOCK, h, "pk_h", lambda hf: NT + 1)
            loaded(pe, "qkv")
            pe.wait_ge(sem("ln_done"), 2 * LN_BLOCK + 2)
            for hf in range(2):
                for k in range(4):
                    if hf:
                        pe.wait_ge(sem("rot_parts"), k + 1)
                    for q in range(2):
                        at = (2 * hf + q) * Q
                        last = pe.matmul(B[:, 2 * k + q, 0:Q], L["qkv"][:, k, :], x2[:, at:at + Q],
                                         start=True, stop=True)
                    last.then_inc(sem("rot_linear"), 1)
            for g in range(4):
                pe.wait_ge(sem("rot_parts"), 4 + g // 2 + 1)
                for m in range(4):
                    at = (4 * g + m) * SEQ
                    last = pe.matmul(B[0:SEQ, g, m * P:(m + 1) * P], x2[:, at:at + SEQ], L["qkv"][:, 4, :],
                                     start=True, stop=True)
                last.then_inc(sem("at_v"), 1)

            def at_scores(i, u):
                pe.wait_ge(sem("at_operands"), i * 2 + 2)
                for b in range(2):
                    last = pe.matmul(B[0:SEQ, 2 * u + b, 0:4 * SEQ], qb[:, u, :],
                                     km[:, u, 4 * b:4 * b + 4, :].rearrange("p h n -> p (h n)"), start=True, stop=True)
                last.then_inc(sem("at_scores"), 1)

            def at_turn(i, u):
                pe.wait_ge(sem("at_exp"), i + 1)
                for hh in range(HEADS):
                    last = pe.transpose(B[0:SEQ, 4 + hh // 4, (hh % 4) * SEQ:(hh % 4 + 1) * SEQ], pe_[:, u, hh, :],
                                        L["ident"][0:SEQ, 0:SEQ])
                last.then_inc(sem("at_turned"), 1)

            def at_context(i, u):
                pe.wait_ge(sem("at_pt"), i + 1)
                for hh in range(HEADS):
                    last = pe.matmul(B[0:SEQ, 6, hh * (HD + 1):(hh + 1) * (HD + 1)], pt[:, u, hh, :],
                                     vaug[:, bass.ds(i, 1), hh, :].rearrange("p i d -> p (i d)"),
                                     start=True, stop=True)
                last.then_inc(sem("at_context"), 1)

            def at_cturn(i, u, first=False):
                pe.wait_ge(sem("at_cn"), i + 1)
                if not first:
                    pe.wait_ge(sem("at_ct"), i)
                pe.transpose(B[:, 7, 0:SEQ], cn[:, u, :, :].rearrange("p h d -> p (h d)"), L["ident"][0:SEQ, 0:SEQ]) \
                  .then_inc(sem("at_cturned"), 1)

            def at_step(i, u, stages):
                if "scores" in stages:
                    if "later" in stages:
                        pe.wait_ge(sem("at_dif"), i)
                    at_scores(i + 1, 1 - u)
                if "context" in stages:
                    at_context(i - 1, 1 - u)
                if "turn" in stages:
                    at_turn(i, u)
                if "context" in stages:
                    at_cturn(i - 1, 1 - u, "first" in stages)

            pe.wait_ge(sem("at_vaug"), 4)
            pe.wait_ge(sem("vaug_ones"), 1)
            at_scores(0, 0)
            at_step(0, 0, ("scores", "turn"))
            at_step(1, 1, ("scores", "later", "context", "turn", "first"))
            with pe.Fori(1, IMAGES // 2 - 1) as p:
                for u in range(2):
                    at_step(p * 2 + u, u, ("scores", "later", "context", "turn"))
            at_step(IMAGES - 2, 0, ("scores", "later", "context", "turn"))
            at_step(IMAGES - 1, 1, ("context", "turn"))
            at_context(IMAGES - 1, 1)
            at_cturn(IMAGES - 1, 1)

            loaded(pe, "wo")
            pe.wait_ge(sem("at_ct"), IMAGES)
            for hf in range(2):
                for q in range(2):
                    at = (2 * hf + q) * Q
                    last = pe.matmul(B[:, 2 * hf + q, 0:Q], L["wo"][:, :], ct[:, at:at + Q], start=True, stop=True)
                last.then_inc(sem("wo_out"), 1)
            ln_tensor(pe, LN_POST1, xn, "wo_res", lambda hf: hf + 1)
            loaded(pe, "w1")
            loaded(pe, "w2")
            for hf in range(2):
                pe.wait_ge(sem("post1"), 2)
                for k in range(4):
                    if 4 * hf + k >= 2:
                        pe.wait_ge(sem("ff_hid"), 4 * hf + k - 1)
                    for q in range(2):
                        at = (2 * hf + q) * Q
                        last = pe.matmul(B[:, 2 * (k % 2) + q, 0:Q], L["w1"][:, k, :], x4[:, at:at + Q],
                                         start=True, stop=True)
                    last.then_inc(sem("ff_up"), 1)
                pe.wait_ge(sem("ff_hid"), 4 * hf + 4)
                for q in range(2):
                    for k in range(4):
                        last = pe.matmul(B[:, 4 + 2 * hf + q, 0:Q], L["w2"][:, k, :], hid[:, k, q * Q:(q + 1) * Q],
                                         start=(k == 0), stop=(k == 3))
                last.then_inc(sem("ff_down"), 1)
            ln_tensor(pe, LN_POST2, xn, "ff_res", lambda hf: hf + 1)

            ln_tensor(pe, LN_MOE, h, "post_h", lambda hf: hf + 1)
            loaded(pe, "wr")
            pe.wait_ge(sem("ln_done"), 2 * LN_MOE + 2)
            for t in range(NT):
                last = pe.matmul(B[0:TILE, 4, t * EXPERTS:(t + 1) * EXPERTS], x2[:, t * TILE:(t + 1) * TILE],
                                 L["wr"][:, :], start=True, stop=True)
            last.then_inc(sem("moe_logits"), 1)
            pe.wait_ge(sem("moe_gate"), 1)
            for t in range(NT):
                last = pe.transpose(B[0:EXPERTS, t // 4, (t % 4) * TILE:(t % 4 + 1) * TILE], mgate[:, t, :],
                                    L["ident"][0:TILE, 0:TILE])
                if t % 4 == 3 or t == NT - 1:
                    last.then_inc(sem("moe_turned"), 1)
            pe.wait_ge(sem("moe_mt"), 3)
            for name in ("sel8", "mw1", "mw2"):
                loaded(pe, name)
            pe.sem_inc(sem("moe_down"), 2)

            def moe_down(c, e):
                pe.wait_ge(sem("moe_hid"), c * 32 + 4 * e + 8)
                pe.wait_ge(sem("moe_tmp"), c * 8 + e + 1)
                for k in range(4):
                    last = pe.matmul(B[:, 4 + e % 2, 0:Q], L["mw2"][:, e, k, :], mhid[:, e % 2, k, :],
                                     start=(k == 0), stop=(k == 3))
                last.then_inc(sem("moe_down"), 1)

            with pe.Fori(0, 4) as c:
                for e in range(EXPERTS):
                    hold(pe, sem("moe_mb"), c * 8 + e + 1)
                    pe.matmul(B[:, 6 + e % 2, 0:Q], L["sel8"][:, e, :], mt[:, bass.ds(c * Q, Q)],
                              start=True, stop=True).then_inc(sem("moe_mask"), 1)
                    for k in range(4):
                        pe.wait_ge(sem("moe_hid"), c * 32 + 4 * e + k + 1)
                        pe.matmul(B[:, k, 0:Q], L["mw1"][:, e, k * P:(k + 1) * P], x2[:, bass.ds(c * Q, Q)],
                                  start=True, stop=True).then_inc(sem("moe_up"), 1)
                    if e:
                        moe_down(c, e - 1)
                moe_down(c, EXPERTS - 1)

        @block.vector
        def _(dve):
            loaded(dve, "keys")
            dve.tensor_tensor(ksq[:, :, :], L["keys"][:, :, :], L["keys"][:, :, :], ALU.mult).then_inc(sem("key_steps"), 1)
            dve.wait_ge(sem("key_steps"), 1)
            dve.tensor_reduce(kn[:, :], ksq[:, :, :], AX.X, ALU.add).then_inc(sem("key_steps"), 1)
            dve.wait_ge(sem("noise_root"), 3)
            dve.wait_ge(sem("noise_root"), 2)
            dve.tensor_tensor(noise[:, :], noise[:, :], nsign[:, :], ALU.mult).then_inc(sem("noise_done"), 1)
            dve.wait_ge(sem("noise_done"), 1)
            loaded(dve, "tokw")
            loaded(dve, "cols")
            for br in range(2):
                for k in range(2):
                    dve.scalar_tensor_tensor(wnt[:, br, k, :], noise[:, 6 + br * P:6 + (br + 1) * P],
                                             noise[:, 2 * br + k:2 * br + k + 1], L["tokw"][:, br, 1, k, :],
                                             ALU.mult, ALU.mult).then_inc(sem("tok_sw"), 1)
                dve.scalar_tensor_tensor(bn[:, br:br + 1], col(("w1sb", "w2sb")[br]), noise[:, 4 + br:5 + br],
                                         col(("w1b", "w2b")[br]), ALU.mult, ALU.add).then_inc(sem("tok_bias"), 1)
            for br in range(2):
                for k in range(2):
                    dve.wait_ge(sem("tok_sw"), 2 * br + k + 1)
                    dve.tensor_tensor(wnt[:, br, k, :], wnt[:, br, k, :], L["tokw"][:, br, 0, k, :], ALU.add) \
                       .then_inc(sem("tok_weights"), 1)
            dve.wait_ge(sem("key_norm"), 1)
            dve.tensor_scalar(knc[:, :], kn[:, :], 1e-12, None, ALU.max).then_inc(sem("key_steps"), 1)
            dve.wait_ge(sem("key_steps"), 3)
            dve.reciprocal(kr[:, :], knc[:, :]).then_inc(sem("key_steps"), 1)
            dve.wait_ge(sem("key_steps"), 4)
            for d in range(2):
                dve.tensor_tensor(kk[:, d], L["keys"][:, :, :], kr[:, :].unsqueeze(2).to_broadcast([KEYS, 2, 32]),
                                  ALU.mult).then_inc(sem("key_unit"), 1)
            dve.memset(kbd[:, :], 0.0).then_inc(sem("kbd_ready"), 1)
            dve.memset(wg[:, :, :], 0.0).then_inc(sem("wg_zero"), 1)
            dve.wait_ge(sem("kbd_ready"), 1)
            dve.wait_ge(sem("key_turned"), 1)
            for j in range(4):
                dve.tensor_copy(kbd[32 * j:32 * j + 32, j * KEYS:(j + 1) * KEYS], B[32 * j:32 * j + 32, 7, 0:KEYS]) \
                   .then_inc(sem("kbd_ready"), 1)
            dve.wait_ge(sem("wq_centred"), 1)
            dve.tensor_copy(wqc[:, :, :].rearrange("p k n -> p (k n)"), B[:, 6, :]).then_inc(sem("wqc_ready"), 1)
            dve.tensor_copy(bqc[:, :], B[:, 5, 0:4]).then_inc(sem("wqc_ready"), 1)

            hv = h[:, :].rearrange("p (i s) -> p i s", i=IMAGES)
            dve.tensor_copy(hv[:, :, 0:1], col("cls").unsqueeze(1).to_broadcast([P, IMAGES, 1])) \
               .then_inc(sem("tok_h"), 1)
            dve.wait_ge(sem("tok_bias"), 2)
            loaded(dve, "pos")

            def tok_gate(c):
                u = c % 2
                dve.wait_ge(sem("tok_linear"), 2 * c + 2)
                if c >= 2:
                    dve.wait_ge(sem("tok_mish"), c - 1)
                dve.tensor_scalar(gate[:, u, :], B[:, 2 * u, 0:256], bn[:, 0:1], None, ALU.add) \
                   .then_inc(sem("tok_gate"), 1)
                dve.tensor_scalar(gcap[:, u, :], B[:, 2 * u, 0:256], bn[:, 0:1], 20.0, ALU.add, ALU.min) \
                   .then_inc(sem("tok_gate"), 1)

            def tok_mid(c):
                u = c % 2
                dve.wait_ge(sem("tok_exp"), c + 1)
                dve.scalar_tensor_tensor(gnum[:, u, :], gexp[:, u, :], 2.0, gexp[:, u, :], ALU.add, ALU.mult) \
                   .then_inc(sem("tok_num"), 1)
                dve.wait_ge(sem("tok_den"), c + 1)
                dve.reciprocal(grec[:, u, :], gden[:, u, :]).then_inc(sem("tok_rec"), 1)

            def tok_end(c):
                u = c % 2
                dve.wait_ge(sem("tok_mish"), c + 1)
                dve.scalar_tensor_tensor(prod[:, u, :], B[:, 2 * u + 1, 0:256], bn[:, 1:2], gmul[:, u, :],
                                         ALU.add, ALU.mult).then_inc(sem("tok_prod"), 1)
                dve.wait_ge(sem("tok_third"), c + 1)
                dve.scalar_tensor_tensor(
                    hv[:, 4 * c:4 * c + 4, 1:SEQ], B[:, 4 + u, 0:256].rearrange("p (i s) -> p i s", i=4), col("w3b"),
                    L["pos"][:, :].unsqueeze(1).to_broadcast([P, 4, PATCHES]), ALU.add, ALU.add) \
                    .then_inc(sem("tok_h"), 1)

            tok_gate(0)
            for c in range(4):
                if c + 1 < 4:
                    tok_gate(c + 1)
                tok_mid(c)
                tok_end(c)

            ln_vector(dve, LN_GAU, xn)
            for hf in range(2):
                dve.wait_ge(sem("l2_norm"), hf + 1)
                dve.tensor_scalar(dev[:, hf, :], dev[:, hf, :], 1e-5, None, ALU.max).then_inc(sem("l2_floor"), 1)
                dve.wait_ge(sem("l2_floor"), hf + 1)
                dve.reciprocal(inv[:, hf, :], dev[:, hf, :]).then_inc(sem("l2_rec"), 1)
            for hf in range(2):
                dve.wait_ge(sem("l2_inverse"), hf + 1)
                dve.scalar_tensor_tensor(halves(x2, hf), halves(xn, hf), col("g"), banks(4 + 2 * hf),
                                         ALU.mult, ALU.mult) \
                   .then_inc(sem("l2_done"), 1)
            loaded(dve, "relpos")

            def gau_qk(c):
                u = c % 2
                dve.wait_ge(sem("gau_base"), c + 1)
                for k, out in enumerate((qg, kg)):
                    dve.tensor_scalar(out[:, u, :], base[:, u, :], col("gamma", k), col("beta", k), ALU.mult, ALU.add) \
                       .then_inc(sem("gau_qk"), 1)

            def gau_bias(c):
                dve.wait_ge(sem("gau_scores"), c + 1)
                dve.tensor_tensor(biased[:, c % 2], B[0:SEQ, 4 * (c % 2) + 2, 0:Q].rearrange("p (i s) -> p i s", i=4),
                                  L["relpos"][:, :].unsqueeze(1).to_broadcast([SEQ, 4, SEQ]), ALU.add) \
                   .then_inc(sem("gau_biased"), 1)

            def gau_gate(c):
                u, k = c % 2, 4 * (c % 2)
                for blk in range(2):
                    dve.wait_ge(sem("gau_mixed"), 2 * c + blk + 1)
                    dve.tensor_tensor(uo[:, u, blk, :], B[:, k + (1, 3)[blk], 0:Q], ug[:, u, blk, :], ALU.mult) \
                       .then_inc(sem("gau_uo"), 1)

            def gau_add(c):
                u, at = c % 2, c * Q
                dve.wait_ge(sem("gau_out"), c + 1)
                dve.scalar_tensor_tensor(gres[:, u, :], xn[:, at:at + Q], col("res"), B[:, 4 * u + 2, 0:Q],
                                         ALU.mult, ALU.add).then_inc(sem("gau_res"), 1)
                dve.wait_ge(sem("gau_res"), c + 1)
                dve.tensor_tensor(h[:, at:at + Q], h[:, at:at + Q], gres[:, u, :], ALU.add).then_inc(sem("gau_h"), 1)

            for c in range(0, 4, 2):
                gau_qk(c)
                gau_qk(c + 1)
                gau_bias(c)
                gau_bias(c + 1)
                gau_gate(c)
                gau_add(c)
                gau_gate(c + 1)
                gau_add(c + 1)

            ln_vector(dve, LN_KEYS, x2)
            def q_shift(m):
                dve.wait_ge(sem("q_squared"), m + 1)
                if m >= 2:
                    dve.wait_ge(sem("q_ln"), 2 * (m - 2) + 2)
                dve.tensor_scalar(halves(z.rearrange("p f n -> p (f n)"), m % 2), banks(2 * (m % 2)),
                                  bqc[:, m // 2:m // 2 + 1], None, ALU.add).then_inc(sem("q_shifted"), 1)

            q_shift(0)
            for m in range(8):
                hf = m % 2
                dve.wait_ge(sem("q_std"), m + 1)
                dve.reciprocal(inv[:, hf, :], dev[:, hf, :]).then_inc(sem("q_inverse"), 1)
                if m + 1 < 8:
                    q_shift(m + 1)
                dve.wait_ge(sem("q_rstd"), m + 1)
                zz = halves(z.rearrange("p f n -> p (f n)"), hf)
                dve.tensor_tensor(zz, zz, banks(4 + 2 * hf), ALU.mult).then_inc(sem("q_z"), 1)
            vals = vi[:, 0]

            def top_lists(i):
                hold(dve, sem("pk_s1"), i + 1)
                for l in range(LISTS):
                    last = dve.max(vals[:, l, 0:8], s1[:, l, :])
                last.then_inc(sem("pk_top8"), 1)
                hold(dve, sem("pk_top8"), i * 2 + 1)
                for l in range(LISTS):
                    dve.max_index(iu[:, l, 0:8], vals[:, l, 0:8], s1[:, l, :])
                    last = dve.match_replace(s2[:, l, :], vals[:, l, 0:8], s1[:, l, :], BIG)
                last.then_inc(sem("pk_lists"), 1)
                hold(dve, sem("pk_lists"), i + 1)
                for l in range(LISTS):
                    last = dve.max(vals[:, l, 8:16], s2[:, l, :])
                last.then_inc(sem("pk_top8"), 1)
                hold(dve, sem("pk_top8"), i * 2 + 2)
                for l in range(LISTS):
                    last = dve.max_index(iu[:, l, 8:16], vals[:, l, 8:16], s2[:, l, :])
                last.then_inc(sem("pk_index"), 1)

            def onehots(i, last_tile=False):
                dve.wait_ge(sem("pk_xt"), i * 2 + 2)
                expert = xt[:, PARTS * PAIRS:, :].rearrange("p c t -> p (c t)")
                dve.tensor_scalar(ebf[:, :], expert, -15.5, 1.0 / EB, ALU.add, ALU.mult).then_inc(sem("pk_ab"), 1)
                dve.wait_ge(sem("pk_ab"), i * 3 + 1)
                dve.tensor_scalar(ea[:, :], ebf[:, :], ROUND, ROUND, ALU.add, ALU.subtract).then_inc(sem("pk_ab"), 1)
                dve.wait_ge(sem("pk_ab"), i * 3 + 2)
                dve.scalar_tensor_tensor(eb[:, :], ea[:, :], -float(EB), expert, ALU.mult, ALU.add) \
                   .then_inc(sem("pk_ab"), 1)
                for a in range(EA):
                    last = dve.tensor_scalar(ah[:, a].rearrange("p c t -> p (c t)"), ea[:, :], float(a), None,
                                             ALU.is_equal)
                last.then_inc(sem("pk_ah"), 1)
                dve.wait_ge(sem("pk_ab"), i * 3 + 3)
                for b in range(EB if last_tile else DVE_B):
                    last = dve.tensor_scalar(bt[:, :, :, b, :], eb.rearrange("p (c j g) -> p c j g", c=PAIRS, j=QUAD),
                                             float(b), None, ALU.is_equal)
                last.then_inc(sem("pk_bt"), 1)
                if last_tile:
                    dve.wait_ge(sem("pk_ah"), i + 1)
                    for a in range(DVE_A):
                        last = dve.tensor_tensor(
                            aw[:, a].rearrange("p q c t -> p q (c t)"),
                            ah[:, a].rearrange("p c t -> p (c t)").unsqueeze(1).to_broadcast([PAIR, PARTS, PAIRS * TILE]),
                            xt[:, 0:PARTS * PAIRS, :].rearrange("p (q c) t -> p q (c t)", q=PARTS), ALU.mult)
                    last.then_inc(sem("pk_bt_pool"), 1)

            def candidates(i):
                v = vi[:, :, :, :].rearrange("p k (h l) r -> p (k h) l r", l=2)
                first, second = v[:, :, 0, :], v[:, :, 1, :]
                dve.wait_ge(sem("pk_values"), i + 1)
                dve.wait_ge(sem("pk_indices"), i + 1)
                for r in range(5):
                    n = ROW_LEN[r]
                    dve.tensor_tensor(cc[:, :, ROW_AT[r]:ROW_AT[r] + n],
                                      first[:, :, r:r + 1].to_broadcast([TILE, LISTS, n]), second[:, :, 0:n],
                                      ALU.add).then_inc(sem("pk_cand"), 1)
                dve.tensor_tensor(cc[:, :, ROW_AT[5]:ROW_AT[8]].rearrange("p k (r c) -> p k r c", c=2),
                                  first[:, :, 5:8].unsqueeze(3).to_broadcast([TILE, LISTS, 3, 2]),
                                  second[:, :, 0:2].unsqueeze(2).to_broadcast([TILE, LISTS, 3, 2]),
                                  ALU.add).then_inc(sem("pk_cand"), 1)
                dve.tensor_tensor(cc[:, :, ROW_AT[8]:CAND], first[:, :, 8:16],
                                  second[:, :, 0:1].to_broadcast([TILE, LISTS, 8]), ALU.add) \
                   .then_inc(sem("pk_cand"), 1)
                hold(dve, sem("pk_cand"), i * 7 + 7)
                for k in range(HEADS):
                    last = dve.max(m8[:, k, :], cc[:, k, :])
                last.then_inc(sem("pk_m"), 1)
                hold(dve, sem("pk_m"), i * 3 + 1)
                dve.tensor_scalar(mneg[:, :], m8[:, :, 0], -1.0, None, ALU.mult).then_inc(sem("pk_mneg"), 1)
                for k in range(HEADS):
                    last = dve.match_replace(c2[:, k, :], m8[:, k, :], cc[:, k, :], BIG)
                last.then_inc(sem("pk_m"), 1)
                hold(dve, sem("pk_m"), i * 3 + 2)
                for k in range(HEADS):
                    last = dve.max(m16[:, k, :], c2[:, k, :])
                last.then_inc(sem("pk_m"), 1)
                hold(dve, sem("pk_m"), i * 3 + 3)
                for k in range(HEADS):
                    last = dve.match_replace(c2[:, k, :], m16[:, k, :], c2[:, k, :], BIG)
                last.then_inc(sem("pk_taken"), 1)

            def weights(i):
                dve.wait_ge(sem("pk_exp"), i + 1)
                dve.wait_ge(sem("pk_taken"), i + 1)
                dve.scalar_tensor_tensor(wu[:, :, :], c2[:, :, :], 0.1 * BIG, ex[:, :, :], ALU.is_lt, ALU.mult) \
                   .then_inc(sem("pk_sum"), 1)
                dve.wait_ge(sem("pk_sum"), i * 3 + 1)
                dve.tensor_reduce(wz[:, :], wu[:, :, :], AX.X, ALU.add).then_inc(sem("pk_sum"), 1)
                dve.wait_ge(sem("pk_sum"), i * 3 + 2)
                dve.reciprocal(wr[:, :], wz[:, :]).then_inc(sem("pk_sum"), 1)

            def gather_weights(i):
                dve.wait_ge(sem("pk_scattered"), i + 1)
                for j in range(QUAD):
                    r = slice(EB * j, EB * (j + 1))
                    src = B[r, 5:8, 0:PER_BANK * 48].rearrange("p k (g t a q) -> p k g t a q", g=PER_BANK, t=QUAD, q=PARTS)
                    dve.tensor_reduce(wt[r, :, :].rearrange("p (k g) a -> p k g a", k=3), src[:, :, :, j], AX.X,
                                      ALU.add).then_inc(sem("pk_wt"), 1)
                for j in range(QUAD):
                    r = slice(EB * j, EB * (j + 1))
                    dve.wait_ge(sem("pk_wt"), i * 4 + j + 1)
                    dve.tensor_tensor(wg[r, :, j * GROUPS:(j + 1) * GROUPS],
                                      wt[r, 0:GROUPS, :].rearrange("p g a -> p a g"),
                                      gelu[r, :, bass.ds(i * GROUPS, GROUPS)], ALU.mult).then_inc(sem("pk_wg"), 1)

            def add_experts(i):
                dve.wait_ge(sem("pk_out"), i + 1)
                at = bass.ds(i * TILE, TILE)
                dve.tensor_tensor(h[:, at], h[:, at], B[:, 4, 0:TILE], ALU.add).then_inc(sem("pk_h"), 1)

            def dve_tile(i, prev):
                top_lists(i)
                if prev == 0:
                    dve.wait_ge(sem("q_norm"), 1)
                    dve.tensor_scalar(qnc[:, :], qn[:, :], 1e-12, None, ALU.max).then_inc(sem("q_inorm"), 1)
                    dve.wait_ge(sem("q_inorm"), 1)
                    dve.reciprocal(rn[:, :], qnc[:, :]).then_inc(sem("q_inorm"), 1)
                if prev == 2:
                    gather_weights(i - 2)
                if prev:
                    onehots(i - 1)
                candidates(i)
                weights(i)
                if prev == 2:
                    add_experts(i - 2)

            dve.sem_inc(sem("pk_h"), 1)
            dve_tile(0, 0)
            dve.wait_ge(sem("pk_gelu"), NT // 2)
            dve.memset(B[:, 7, (GROUPS - 2 * PER_BANK) * 48:PER_BANK * 48], 0.0).then_inc(sem("pad_zero"), 1)
            dve_tile(1, 1)
            dve.wait_ge(sem("pad_zero"), 1)
            dve.wait_ge(sem("wg_zero"), 1)
            with dve.Fori(2, NT) as i:
                dve_tile(i, 2)
            gather_weights(NT - 2)
            onehots(NT - 1, True)
            add_experts(NT - 2)
            gather_weights(NT - 1)
            add_experts(NT - 1)

            dve.memset(vaug[:, :, :, HD:HD + 1], 1.0).then_inc(sem("vaug_ones"), 1)
            ln_vector(dve, LN_BLOCK, x2)
            loaded(dve, "rope")
            for hf in range(2):
                for k in range(4):
                    dve.wait_ge(sem("rot_linear"), 4 * hf + k + 1)
                    if hf and k % 2 == 0:
                        dve.wait_ge(sem("rot_done"), k // 2 + 1)
                    dve.tensor_tensor(rot[:, k // 2, k % 2, :].rearrange("p (q i s) -> p q i s", q=2, i=4),
                                      B[:, 2 * k:2 * k + 2, 0:Q].rearrange("p q (i s) -> p q i s", i=4),
                                      L["rope"][:, k % 2, :].unsqueeze(1).unsqueeze(1).to_broadcast([P, 2, 4, SEQ]),
                                      ALU.mult).then_inc(sem("rot_parts"), 1)

            def at_shift(i, u):
                dve.wait_ge(sem("at_scores"), i + 1)
                sc = B[0:SEQ, 2 * u:2 * u + 2, 0:4 * SEQ].rearrange("p b (h n) -> p b h n", h=4)
                dve.tensor_reduce(mx[:, u, :].rearrange("p (b h) -> p b h", b=2), sc, AX.X, ALU.max) \
                   .then_inc(sem("at_max"), 1)
                dve.wait_ge(sem("at_max"), i + 1)
                dve.tensor_tensor(sd[:, u, :, :].rearrange("p (b h) n -> p b h n", b=2), sc,
                                  mx[:, u, :].rearrange("p (b h) -> p b h", b=2).unsqueeze(3)
                                  .to_broadcast([SEQ, 2, 4, SEQ]), ALU.subtract).then_inc(sem("at_dif"), 1)

            def at_normalise(i, u):
                cx = B[0:SEQ, 6, 0:HEADS * (HD + 1)].rearrange("p (h d) -> p h d", h=HEADS)
                dve.wait_ge(sem("at_context"), i + 1)
                dve.reciprocal(rs[:, u, :], cx[:, :, HD]).then_inc(sem("at_rs"), 1)
                dve.wait_ge(sem("at_rs"), i + 1)
                dve.tensor_tensor(cn[:, u, :, :], cx[:, :, 0:HD],
                                  rs[:, u, :].unsqueeze(2).to_broadcast([SEQ, HEADS, HD]),
                                  ALU.mult).then_inc(sem("at_cn"), 1)

            at_shift(0, 0)
            at_shift(1, 1)
            with dve.Fori(1, IMAGES // 2) as p:
                for u in range(2):
                    dve.wait_ge(sem("at_exp"), p * 2 + u - 1)
                    at_normalise(p * 2 + u - 2, u)
                    at_shift(p * 2 + u, u)
            at_normalise(IMAGES - 2, 0)
            at_normalise(IMAGES - 1, 1)

            for hf in range(2):
                dve.wait_ge(sem("wo_out"), hf + 1)
                dve.tensor_tensor(halves(xn, hf), banks(2 * hf), halves(x2, hf), ALU.add).then_inc(sem("wo_res"), 1)
            ln_vector(dve, LN_POST1, x2)
            for hf in range(2):
                dve.wait_ge(sem("ff_down"), hf + 1)
                dve.scalar_tensor_tensor(halves(xn, hf), banks(4 + 2 * hf), col("b2"), halves(x4, hf),
                                         ALU.add, ALU.add).then_inc(sem("ff_res"), 1)
            ln_vector(dve, LN_POST2, x2)
            for hf in range(2):
                dve.wait_ge(sem("post2"), hf + 1)
                dve.tensor_tensor(halves(h, hf), halves(h, hf), halves(x4, hf), ALU.add).then_inc(sem("post_h"), 1)

            ln_vector(dve, LN_MOE, x2)
            loaded(dve, "br")
            loaded(dve, "order")
            dve.wait_ge(sem("moe_logits"), 1)
            wide = [TILE, NT, EXPERTS]
            dve.tensor_tensor(lg[:, :, :], B[0:TILE, 4, 0:NT * EXPERTS].rearrange("p (t e) -> p t e", t=NT),
                              L["br"][:, :].unsqueeze(1).to_broadcast(wide), ALU.add).then_inc(sem("moe_route"), 1)
            dve.wait_ge(sem("moe_route"), 1)
            dve.tensor_reduce(lm[:, :], lg[:, :, :], AX.X, ALU.max).then_inc(sem("moe_route"), 1)
            dve.wait_ge(sem("moe_route"), 2)
            dve.tensor_tensor(gd[:, :], lm[:, :], lm[:, :], ALU.subtract).then_inc(sem("moe_gdif"), 1)
            dve.tensor_tensor(leq[:, :, :], lg[:, :, :], lm[:, :].unsqueeze(2).to_broadcast(wide), ALU.is_equal) \
               .then_inc(sem("moe_route"), 1)
            dve.wait_ge(sem("moe_route"), 3)
            dve.tensor_tensor(lord[:, :, :], leq[:, :, :], L["order"][:, :].unsqueeze(1).to_broadcast(wide),
                              ALU.mult).then_inc(sem("moe_route"), 1)
            dve.wait_ge(sem("moe_route"), 4)
            dve.tensor_reduce(lfirst[:, :], lord[:, :, :], AX.X, ALU.max).then_inc(sem("moe_route"), 1)
            dve.wait_ge(sem("moe_route"), 5)
            dve.tensor_tensor(lmask[:, :, :], L["order"][:, :].unsqueeze(1).to_broadcast(wide),
                              lfirst[:, :].unsqueeze(2).to_broadcast(wide), ALU.is_equal).then_inc(sem("moe_route"), 1)
            dve.wait_ge(sem("moe_gexp"), 1)
            dve.reciprocal(gr[:, :], ge[:, :]).then_inc(sem("moe_route"), 1)
            dve.wait_ge(sem("moe_route"), 7)
            dve.tensor_tensor(gg[:, :], ge[:, :], gr[:, :], ALU.mult).then_inc(sem("moe_route"), 1)
            dve.wait_ge(sem("moe_route"), 8)
            dve.tensor_tensor(mgate[:, :, :], lmask[:, :, :], gg[:, :].unsqueeze(2).to_broadcast(wide), ALU.mult) \
               .then_inc(sem("moe_gate"), 1)

            dve.sem_inc(sem("moe_tmp"), 2)
            with dve.Fori(0, 4) as c:
                for e in range(EXPERTS):
                    dve.wait_ge(sem("moe_down"), c * 8 + e + 3)
                    dve.wait_ge(sem("moe_mb"), c * 8 + e + 3)
                    if e:
                        dve.wait_ge(sem("moe_acc"), c * 8 + e)
                    dve.scalar_tensor_tensor((mtmp if e else macc)[:, :], B[:, 4 + e % 2, 0:Q], col("mb2", e),
                                             mb[:, e % 2, :], ALU.add, ALU.mult).then_inc(sem("moe_tmp"), 1)
                    if e:
                        dve.wait_ge(sem("moe_tmp"), c * 8 + e + 3)
                        dve.tensor_tensor(macc[:, :], macc[:, :], mtmp[:, :], ALU.add).then_inc(sem("moe_acc"), 1)
                    else:
                        dve.wait_ge(sem("moe_tmp"), c * 8 + 3)
                        dve.sem_inc(sem("moe_acc"), 1)
                dve.wait_ge(sem("moe_acc"), c * 8 + 8)
                at = bass.ds(c * Q, Q)
                dve.tensor_tensor(h[:, at], h[:, at], macc[:, :], ALU.add).then_inc(sem("out_ready"), 1)
                dve.wait_ge(sem("out_ready"), c + 1)


def layouts(x, cls_tok, **w):
    f = np.float32
    a = {k: np.asarray(v) for k, v in w.items()}
    x = np.asarray(x)
    out = {}
    out["eps"] = np.concatenate(
        [a["L0_tok_eps_in1"].reshape(2, P).T, a["L0_tok_eps_in2"].reshape(2, P).T,
         a["L0_tok_eps_out1"][:, None], a["L0_tok_eps_out2"][:, None],
         np.broadcast_to(a["L0_tok_eps_out1"], (P, P)), np.broadcast_to(a["L0_tok_eps_out2"], (P, P))], axis=1)
    out["keys"] = np.stack([a["L0_ffn_keys0"], a["L0_ffn_keys1"]], axis=1)
    cols = {
        "w1b": a["L0_tok_W1_b"], "w1sb": a["L0_tok_W1_sb"], "w2b": a["L0_tok_W2_b"], "w2sb": a["L0_tok_W2_sb"],
        "w3b": a["L0_tok_W3_b"], "gamma": a["L0_attn_gamma"].T, "beta": a["L0_attn_beta"].T,
        "res": a["L0_attn_res_scale"], "g": np.broadcast_to(a["L0_attn_g"].reshape(1), (P,)),
        "bq": a["L0_ffn_bq"].reshape(4, P).T,
        "lng": np.concatenate([a["L0_ffn_ln_g"]] * 2), "lnb": np.concatenate([a["L0_ffn_ln_b"]] * 2),
        "b1": a["L1_attn_b1"].reshape(4, P).T, "b2": a["L1_attn_b2"], "g1": a["L1_attn_g1"], "be1": a["L1_attn_be1"],
        "g2": a["L1_attn_g2"], "be2": a["L1_attn_be2"], "mb1": a["L1_ffn_b1"].reshape(32, P).T,
        "mb2": a["L1_ffn_b2"].T, "cls": np.asarray(cls_tok).reshape(P), "eps": np.full((P,), 1e-5, f),
    }
    out["cols"] = np.concatenate([cols[k].reshape(P, n) for k, (_, n) in COLS.items()], axis=1)
    out["tokw"] = np.stack([np.stack([a[f"L0_tok_W{br}_{k}"].T.reshape(2, P, P).transpose(1, 0, 2)
                                      for k in ("w", "sw")], axis=1) for br in (1, 2)], axis=1)
    out["pat"] = x.reshape(IMAGES, 8, 16, 8, 16).transpose(2, 4, 0, 1, 3).reshape(2, P, IMAGES * PATCHES) \
        .transpose(1, 0, 2)
    out["ident"] = np.eye(P, dtype=f)
    head = np.arange(P) // 64
    out["centre64"] = (np.eye(P) - (head[:, None] == head) / 64).astype(f)
    out["wq"] = a["L0_ffn_Wq"].reshape(4, P, P).transpose(1, 0, 2)
    out["w3"] = a["L0_tok_W3_w"].T
    div = np.exp(np.arange(0, P, 2, dtype=f) * f(-np.log(10000.0) / P)).astype(f)
    ang = (np.arange(PATCHES, dtype=f)[:, None] * div).astype(f)
    out["pos"] = np.stack([np.sin(ang), np.cos(ang)], axis=-1).reshape(PATCHES, P).T.astype(f)
    out["centre"] = (np.eye(P) - 1.0 / P).astype(f)
    out["mean"] = np.full((P, 32), 1.0 / P, f)
    out["ones"] = np.ones((P, 32), f)
    row, feat = np.arange(P)[:, None, None], np.arange(P)[None, None, :]
    out["back"] = (row == 32 * np.arange(4)[None, :, None] + 8 * (feat // 32)).astype(f)
    out["uvw"] = a["L0_attn_uv_w"]
    out["relpos"] = a["L0_attn_w"][SEQ - 1 + np.arange(SEQ)[:, None] - np.arange(SEQ)[None, :]]
    out["ow"] = a["L0_attn_o_w"].reshape(2, P, P).transpose(1, 0, 2)
    out["mean64"] = ((head[:, None] == np.arange(32) // 16) / 64).astype(f)
    out["blk32"] = (np.arange(P)[:, None] // 32 == np.arange(4)).astype(f)
    out["down"] = np.tile(a["L0_ffn_expert_down"][:P].T.reshape(P, EA, 1, EB), (1, 1, QUAD, 1)).reshape(P, EA, P)
    out["identb"] = np.eye(P, dtype=mybir.dt.np(BF16))
    out["up"] = np.tile(a["L0_ffn_expert_up"][:P].reshape(EA, EB, P).transpose(1, 0, 2), (QUAD, 1, 1))
    swap = np.arange(P) ^ 8
    wq, wk = a["L1_attn_Wq"], a["L1_attn_Wk"]
    out["qkv"] = np.stack([wq.T, wq[swap].T, wk.T, wk[swap].T, a["L1_attn_Wv"].T], axis=1)
    inv = (1.0 / (f(10000.0) ** (np.arange(0, HD, 2, dtype=f) / f(HD)))).astype(f)
    fr = (np.arange(SEQ, dtype=f)[:, None] * inv).astype(f)
    d = np.arange(P) % HD
    out["rope"] = np.stack([np.cos(fr)[:, d % 8].T, np.where(d < 8, -1.0, 1.0)[:, None] * np.sin(fr)[:, d % 8].T],
                           axis=1).astype(f)
    out["headmask"] = (np.arange(P)[:, None] // HD == np.arange(HEADS)).astype(f)
    out["wo"] = a["L1_attn_Wo"].T
    out["w1"] = a["L1_attn_W1"].T.reshape(P, 4, P)
    out["w2"] = a["L1_attn_W2"].T.reshape(4, P, P).transpose(1, 0, 2)
    out["wr"] = a["L1_ffn_Wr"]
    out["br"] = np.broadcast_to(a["L1_ffn_br"], (TILE, EXPERTS))
    out["order"] = np.broadcast_to(np.arange(EXPERTS, 0, -1).astype(f), (TILE, EXPERTS))
    out["sel8"] = np.broadcast_to(np.eye(EXPERTS, dtype=f)[:, :, None], (EXPERTS, EXPERTS, P))
    out["mw2"] = a["L1_ffn_W2"].reshape(EXPERTS, 4, P, P).transpose(2, 0, 1, 3)
    out["mw1"] = a["L1_ffn_W1"].transpose(1, 0, 2)
    return out


def kernel(**inputs):
    import concourse.bacc as _bacc
    from concourse.bass_utils import run_bass_kernel_spmd as _run

    nc = _bacc.Bacc("TRN2", target_bir_lowering=False, num_devices=1)
    arrays, aps = {}, {}
    for name, v in layouts(**inputs).items():
        v = np.ascontiguousarray(v)
        arrays["in_" + name + "_dram"] = v
        aps[name] = nc.dram_tensor("in_" + name + "_dram", v.shape, mybir.dt.from_np(v.dtype), kind="ExternalInput").ap()
    y = nc.dram_tensor("out_dram", (P, T), F32, kind="ExternalOutput").ap()
    build(nc, aps, y)
    r = _run(nc, [arrays], core_ids=[0])
    return np.ascontiguousarray(r.results[0]["out_dram"].T.reshape(IMAGES, SEQ, P))
```

```python
from contextlib import ExitStack

import numpy as np

import concourse.bass as bass
from concourse import mybir

F32 = mybir.dt.float32
BF16 = mybir.dt.bfloat16
U32 = mybir.dt.uint32
F32R = mybir.dt.float32r
ALU = mybir.AluOpType
ACT = mybir.ActivationFunctionType
AX = mybir.AxisListType

P = 128
IMAGES = 16
PATCHES = 64
SEQ = PATCHES + 1
T = IMAGES * SEQ
Q = T // 4
HALF = 2 * Q
EIGHTH = Q // 2
NORMS = 320
CHUNK = IMAGES * PATCHES // 4
TILE = 104
NT = T // TILE
HEADS = 8
KEYS = 64
TOP = 16
LISTS = 2 * HEADS
DVE_A = 2
ACT_B = 7
ACT_EARLY = 5
DVE_B = 31
ROW_LEN = [TOP // (r + 1) for r in range(TOP)]
ROW_AT = [sum(ROW_LEN[:r]) for r in range(TOP)]
CAND = sum(ROW_LEN)
PAIR = 2 * CAND
PAIRS = HEADS // 2
QUAD = 4
GROUPS = TILE // QUAD
PER_BANK = 9
EA, EB = 4, 32
PARTS = 3
HD = 16
EXPERTS = 8
BIG = -1e30
ROUND = 12582912.0

COLS = {}
for _name, _n in (("w1b", 1), ("w1sb", 1), ("w2b", 1), ("w2sb", 1), ("w3b", 1), ("gamma", 2), ("beta", 2),
                  ("res", 1), ("g", 1), ("bq", 4), ("lng", 1), ("lnb", 1), ("b1", 4), ("b2", 1), ("g1", 1),
                  ("be1", 1), ("g2", 1), ("be2", 1), ("mb1", 32), ("mb2", 8), ("cls", 1), ("eps", 1),
                  ("minus", ACT_B)):
    COLS[_name] = (sum(n for _, n in COLS.values()), _n)
NCOLS = sum(n for _, n in COLS.values())


LOADS = {
    "first": ("eps", "cols", "keys"),
    "tokw": ("tokw",),
    "pat": ("pat",),
    "tok": ("ident", "centre64", "wq", "w3", "pos"),
    "gau": ("centre", "mean", "ones", "back", "uvw", "relpos", "ow"),
    "keys": ("mean64", "blk32", "down", "identb", "up"),
    "block": ("qkv", "rope", "headmask", "wo", "w1", "w2"),
    "moe": ("wr", "br", "order", "selm", "mw2"),
    "mw1": ("mw1",),
}
group_of = {name: group for group, names in LOADS.items() for name in names}


def build(nc, I, y):
    with ExitStack() as ctx:
        start = {}

        def sb(name, shape, dt=F32):
            start[name] = -(-nc.sbuf_base // 32) * 32
            return ctx.enter_context(nc.sbuf_tensor(name, shape, dt))

        def rounded(name, place, at, *shape):
            return nc.alloc_sbuf_tensor_at(name, [P, *shape], F32R, offset=start[place] + 4 * at)

        def view(arena, at, *shape):
            n = int(np.prod(shape))
            names = " ".join("abcd"[:len(shape)])
            v = arena[:, at:at + n]
            if len(shape) == 1:
                return v
            return v.rearrange(f"p ({names}) -> p {names}", **dict(zip("abcd", shape)))

        sems = {}

        def sem(name):
            if name not in sems:
                sems[name] = ctx.enter_context(nc.semaphore(name))
            return sems[name]

        PS = ctx.enter_context(nc.psum_tensor("PS", [P, 8 * 512], F32))
        B = PS[:, :].rearrange("p (b n) -> p b n", b=8)

        L = {}
        for name, ap in I.items():
            if name not in ("pat", "tokw", "mw1"):
                L[name] = sb("in_" + name, list(ap.shape), ap.dtype)
        cols = L["cols"]

        def col(name, k=0):
            at = COLS[name][0] + k
            return cols[:, at:at + 1]

        arena1 = sb("arena1", [P, 4 * T])
        arena2 = sb("arena2", [P, 4 * T])
        arena3 = sb("arena3", [P, EB * PAIRS * TILE // 2])
        qln = view(arena1, 0, 4, T)
        L["pat"] = view(arena1, 0, 2, IMAGES * PATCHES)
        L["tokw"] = view(arena1, 2 * IMAGES * PATCHES, 2, 2, 2, P)
        free = 2 * IMAGES * PATCHES + 8 * P
        wnt = view(arena1, free, 2, 2, P)
        noise, nsign = (view(arena1, free + 4 * P + k * (2 * P + 6), 2 * P + 6) for k in range(2))
        L["mw1"] = view(arena3, 0, EXPERTS, 4 * P)
        ct = view(arena1, 0, T)
        x4 = view(arena1, T, T)
        hid = view(arena1, 2 * T, 4, HALF)
        sq2 = view(arena2, 0, 4, T)
        grec, gact, gmul, prod = (view(arena2, 4 * CHUNK * k, 4, CHUNK) for k in range(4))
        rot = view(arena2, 0, 2, 2, HALF)
        qr = view(arena2, 2 * T, T)
        kr1 = view(arena2, 3 * T, T)
        bt = arena3[0:PAIR, :].bitcast(BF16).rearrange("p (c j b g) -> p c j b g", c=PAIRS, j=QUAD, b=EB)
        ug = view(arena3, 0, 2, 2, Q)
        uo = view(arena3, 4 * Q, 2, 2, Q)
        gres = view(arena3, 8 * Q, 2, Q)
        vtok = view(arena3, 10 * Q, 2, 4, 2 * P)[0:SEQ]
        biased = view(arena3, 10 * Q + 16 * P, 2, 4, SEQ)[0:SEQ]
        relu = view(arena3, 12 * Q + 16 * P, 2, 4, SEQ)[0:SEQ]
        sd, pt = (view(arena3, EXPERTS * 4 * P + 2 * HEADS * SEQ * k, 2, HEADS, SEQ)[0:SEQ] for k in range(2))
        kern = view(arena3, 14 * Q + 16 * P, 2, 4, SEQ)[0:SEQ]

        arena4 = sb("arena4", [P, 4608])
        arena5 = sb("arena5", [P, IMAGES * HEADS * (HD + 1)])
        arena6 = sb("arena6", [P, 6 * Q])
        gexp, gcap, gnum, gden = (view(arena4, 4 * CHUNK * k, 4, CHUNK) for k in range(4))
        s1 = view(arena4, 0, LISTS, KEYS)[0:TILE]
        s2 = view(arena4, LISTS * KEYS, LISTS, KEYS)[0:TILE]
        aw = arena4[0:PAIR, 2 * LISTS * KEYS:2 * LISTS * KEYS + EA * PARTS * PAIRS * TILE // 2].bitcast(BF16) \
            .rearrange("p (a q c t) -> p a q c t", a=EA, q=PARTS, c=PAIRS)
        z = view(arena5, 0, 2, HALF)
        km = view(arena4, 0, 2, HEADS, SEQ)
        mt = arena1[0:PARTS * EXPERTS, 0:T // 2].bitcast(BF16)
        mb = view(arena1, 2 * T, 2, Q)
        mtmp = view(arena1, 3 * T, Q)
        macc = view(arena1, 3 * T + Q, Q)
        vaug = view(arena5, 0, IMAGES, HEADS, HD + 1)[0:SEQ]
        mhid = view(arena5, 0, 2, 4, Q)
        qg, kg, base = (view(arena6, 2 * Q * k, 2, Q) for k in range(3))
        pe_ = view(arena6, 0, 2, HEADS, SEQ)[0:SEQ]

        h = sb("h", [P, T])
        xn = sb("xn", [P, T])
        x2 = sb("x2", [P, T])
        sq = sb("sq", [P, T])
        dev = sb("dev", [P, Q])
        inv = sb("inv", [P, Q])

        w1h = rounded("w1h", "arena4", 0, EXPERTS, 4 * P)
        w1l = rounded("w1l", "arena3", 0, EXPERTS, 4 * P)
        w2h = rounded("w2h", "arena2", 0, EXPERTS, 4, P)
        w2l = rounded("w2l", "in_mw2", 0, EXPERTS, 4, P)
        xh = rounded("xh", "xn", 0, T)
        xl = rounded("xl", "arena1", T, T)
        mhh = rounded("mhh", "arena3", EXPERTS * 4 * P, 2, 4, Q)
        mhl = rounded("mhl", "arena5", 0, 2, 4, Q)

        bn = sb("bn", [P, 2])


        warmed = sb("warmed", [P, 9])

        ksq = sb("ksq", [KEYS, 2, 32])
        kn = sb("kn", [KEYS, 2])
        knc = sb("knc", [KEYS, 2])
        kr = sb("kr", [KEYS, 2])
        kk = sb("kk", [KEYS, 2, 2, 32])
        kbd = sb("kbd", [P, 4 * KEYS])
        wqc = sb("wqc", [P, 4, P])
        bqc = sb("bqc", [P, 4])
        qn = sb("qn", [TILE, NT * LISTS])
        qnc = sb("qnc", [TILE, NT * LISTS])
        rn = sb("rn", [TILE, NT * LISTS])
        gelu = sb("gelu", [P, EA, T // QUAD + 1])
        qt = sb("qt", [P, PAIRS, TILE])
        vi = sb("vi", [TILE, 2, LISTS, TOP])
        iu = sb("iu", [TILE, LISTS, TOP], U32)
        cc = sb("cc", [TILE, LISTS, CAND])
        c2 = sb("c2", [TILE, HEADS, CAND])
        mm = sb("mm", [TILE, HEADS, TOP])
        me = sb("me", [TILE, HEADS, TOP])
        mneg = sb("mneg", [TILE, HEADS])
        ex = sb("ex", [TILE, HEADS, CAND])
        wu = sb("wu", [TILE, HEADS, CAND])
        wz = sb("wz", [TILE, HEADS])
        wr = sb("wr", [TILE, HEADS])
        wn = sb("wn", [TILE, HEADS, CAND])
        rem = sb("rem", [TILE, HEADS, CAND])
        x4b = sb("x4b", [TILE, PARTS + 1, HEADS * CAND], BF16)
        xt = sb("xt", [PAIR, (PARTS + 1) * PAIRS, TILE], BF16)
        ebf = sb("ebf", [PAIR, PAIRS * TILE], BF16)
        ea = sb("ea", [PAIR, PAIRS * TILE], BF16)
        eb = sb("eb", [PAIR, PAIRS * TILE], BF16)
        far = sb("far", [PAIR, ACT_B, PAIRS * TILE], BF16)
        ah = sb("ah", [PAIR, EA, PAIRS, TILE], BF16)
        wg = sb("wg", [P, QUAD, 3 * PER_BANK, EA, PARTS])

        qb = sb("qb", [P, 2, SEQ])
        mx = sb("mx", [SEQ, 2, HEADS])
        rs = sb("rs", [SEQ, 2, HEADS])
        cn = sb("cn", [SEQ, 2, HEADS, HD])

        lg = sb("lg", [TILE, NT, EXPERTS])
        lm = sb("lm", [TILE, NT])
        leq = sb("leq", [TILE, NT, EXPERTS])
        lord = sb("lord", [TILE, NT, EXPERTS])
        lfirst = sb("lfirst", [TILE, NT])
        gd = sb("gd", [TILE, NT])
        ge = sb("ge", [TILE, NT])
        gr = sb("gr", [TILE, NT])
        gg = sb("gg", [TILE, NT])
        lmask = sb("lmask", [TILE, NT, EXPERTS])
        mgate = sb("mgate", [TILE, NT, EXPERTS])
        mrest = sb("mrest", [TILE, NT, EXPERTS])
        mparts = sb("mparts", [TILE, NT, PARTS, EXPERTS], BF16)

        block = ctx.enter_context(nc.Block())

        def hold(eng, semaphore, value):
            eng.wait_ge(semaphore, value)
            eng.sem_inc(sem("held"), 1)

        def loaded(eng, name):
            eng.wait_ge(sem("in_" + group_of[name]), 16 * len(LOADS[group_of[name]]))

        def images(ap, n):
            return ap.rearrange("p (i s) -> p i s", i=n)

        def high_part(dve, out, x):
            return dve.tensor_copy(out, x)

        def halves(ap, hf):
            return ap[:, hf * HALF:(hf + 1) * HALF].rearrange("p (q n) -> p q n", q=2)

        def banks(first):
            return B[:, first:first + 2, 0:Q]

        def spread(pe, stat, x, at, n, bank):
            for q in range(4):
                last = pe.matmul(B[32 * q:32 * q + 32, bank, 0:n], L[stat][:, :], x[:, at + q * n:at + (q + 1) * n],
                                 start=True, stop=True)
            return last

        def gathered(pe, x, n, bank):
            for q in range(4):
                at = q * n % Q
                last = pe.matmul(B[:, bank + q * n // Q, at:at + n], L["back"][:, q, :], x, start=True, stop=True)
            return last

        def quarter(ap, c):
            return ap[:, c * Q:(c + 1) * Q]

        def ln_centre(pe, c, x):
            pe.matmul(B[:, 2 * c, 0:Q], L["centre"][:, :], quarter(x, c), start=True, stop=True) \
              .then_inc(sem("ln_centred"), 1)

        def ln_variance(pe, n, c):
            pe.wait_ge(sem("ln_squared"), 4 * n + c + 1)
            spread(pe, "mean", sq, c * Q, SEQ, 2 * c + 1).then_inc(sem("ln_variance"), 1)

        def ln_back(pe, n, c):
            pe.wait_ge(sem("ln_inverse"), 4 * n + c + 1)
            gathered(pe, inv[:, c * SEQ:(c + 1) * SEQ], SEQ, 2 * c + 1).then_inc(sem("ln_rstd"), 1)

        def ln_tensor(pe, n, x, ready, count):
            for c in range(4):
                pe.wait_ge(sem(ready), count(c))
                ln_centre(pe, c, x)
            for c in range(4):
                ln_variance(pe, n, c)
            for c in range(4):
                ln_back(pe, n, c)

        def ln_square(act, n, c):
            act.wait_ge(sem("ln_centred"), 4 * n + c + 1)
            act.activation(quarter(sq, c), B[:, 2 * c, 0:Q], ACT.Square).then_inc(sem("ln_squared"), 1)

        def ln_deviation(act, n, c):
            act.wait_ge(sem("ln_variance"), 4 * n + c + 1)
            act.activation(dev[:, c * SEQ:(c + 1) * SEQ], B[:, 2 * c + 1, 0:SEQ], ACT.Sqrt, bias=col("eps")) \
               .then_inc(sem("ln_std"), 1)

        def ln_scalar(act, n):
            warm(act, ACT.Sqrt, n)
            for c in range(4):
                ln_square(act, n, c)
            for c in range(4):
                ln_deviation(act, n, c)

        def ln_copy(dve, n, c, out):
            dve.wait_ge(sem("ln_squared"), 4 * n + c + 1)
            dve.tensor_copy(quarter(out, c), B[:, 2 * c, 0:Q]).then_inc(sem("ln_out"), 1)

        def ln_invert(dve, n, c):
            dve.wait_ge(sem("ln_std"), 4 * n + c + 1)
            dve.reciprocal(inv[:, c * SEQ:(c + 1) * SEQ], dev[:, c * SEQ:(c + 1) * SEQ]).then_inc(sem("ln_inverse"), 1)

        def ln_scale(dve, n, c, out):
            dve.wait_ge(sem("ln_rstd"), 4 * n + c + 1)
            dve.wait_ge(sem("ln_out"), 4 * n + c + 1)
            dve.tensor_tensor(quarter(out, c), quarter(out, c), B[:, 2 * c + 1, 0:Q], ALU.mult) \
               .then_inc(sem("ln_done"), 1)

        def ln_vector(dve, n, out):
            for c in range(4):
                ln_copy(dve, n, c, out)
            for c in range(4):
                ln_invert(dve, n, c)
            for c in range(4):
                ln_scale(dve, n, c, out)

        def warm(act, func, k):
            act.activation(warmed[:, k:k + 1], col("eps"), func)

        LN_GAU, LN_KEYS, LN_BLOCK, LN_POST1, LN_POST2, LN_MOE = range(6)

        @block.sync
        def _(sp):
            for name in group_of:
                if name == "mw1":
                    sp.wait_ge(sem("pk_scattered"), NT)
                sp.dma_start(L[name][tuple(slice(None) for _ in I[name].shape)], I[name]).then_inc(sem("in_" + group_of[name]), 16)
            sp.wait_ge(sem("out_ready"), 4)
            sp.dma_start(y, h[:, :]).then_inc(sem("out_stored"), 16)
            sp.wait_ge(sem("out_stored"), 16)

        @block.gpsimd
        def _(pool):
            for c in range(4):
                pool.wait_ge(sem("tok_rec"), c + 1)
                pool.tensor_tensor(gact[:, c, :], gnum[:, c, :], grec[:, c, :], ALU.mult).then_inc(sem("tok_tanh"), 1)
            for c in range(4):
                pool.wait_ge(sem("gau_relu"), c + 1)
                pool.tensor_tensor(kern[:, c % 2], relu[:, c % 2], relu[:, c % 2], ALU.mult) \
                    .then_inc(sem("gau_kernel"), 1)

            def onehot_weights(first=0):
                for a in range(first, EA):
                    last = pool.tensor_tensor(
                        aw[:, a].rearrange("p q c t -> p q (c t)"),
                        ah[:, a].rearrange("p c t -> p (c t)").unsqueeze(1).to_broadcast([PAIR, PARTS, PAIRS * TILE]),
                        xt[:, 0:PARTS * PAIRS, :].rearrange("p (q c) t -> p q (c t)", q=PARTS), ALU.mult)
                last.then_inc(sem("pk_aw"), 1)

            def scaled_values(i):
                hold(pool, sem("pk_index"), i + 1)
                pool.tensor_tensor(vi[:, 0], vi[:, 0], rn[:, bass.ds(i * LISTS, LISTS)].unsqueeze(2)
                                   .to_broadcast([TILE, LISTS, TOP]), ALU.mult).then_inc(sem("pk_values"), 1)

            def onehots(i):
                hold(pool, sem("pk_ab"), i * 3 + 3)
                for b in range(DVE_B, EB):
                    last = pool.tensor_scalar(bt[:, :, :, b, :], eb.rearrange("p (c j g) -> p c j g", c=PAIRS, j=QUAD),
                                              float(b), None, ALU.is_equal)
                last.then_inc(sem("pk_bt_pool"), 1)

            def weight_parts(i):
                parts = x4b[:, :, :].rearrange("p k (h c) -> p k h c", h=HEADS)
                hold(pool, sem("pk_sum"), i * 2 + 2)
                pool.tensor_tensor(wn[:, :, :], wu[:, :, :], wr[:, :].unsqueeze(2).to_broadcast([TILE, HEADS, CAND]),
                                   ALU.mult).then_inc(sem("pk_weights"), 1)
                hold(pool, sem("pk_part0"), i + 1)
                pool.tensor_tensor(rem[:, :, :], wn[:, :, :], parts[:, 0], ALU.subtract).then_inc(sem("pk_rem"), 1)
                hold(pool, sem("pk_part1"), i + 1)
                pool.tensor_tensor(parts[:, 2], rem[:, :, :], parts[:, 1], ALU.subtract).then_inc(sem("pk_part2"), 1)

            def pool_tile(i, prev):
                scaled_values(i)
                if prev:
                    pool.wait_ge(sem("pk_ah"), i)
                    onehot_weights()
                    onehots(i - 1)
                weight_parts(i)

            pool.wait_ge(sem("q_inorm"), 2)
            pool_tile(0, False)
            with pool.Fori(1, NT) as i:
                pool_tile(i, True)
            pool.wait_ge(sem("pk_ah"), NT)
            onehot_weights(DVE_A)

            def rotated(hf):
                for k, out in ((0, qr), (1, kr1)):
                    pool.wait_ge(sem("rot_parts"), 4 * hf + 2 * k + 2)
                    pool.tensor_tensor(out[:, hf * HALF:(hf + 1) * HALF], rot[:, k, 0], rot[:, k, 1], ALU.add) \
                        .then_inc(sem("rot_done"), 1)

            def head_keys(i, u):
                pool.tensor_copy(qb[:, u, :], qr[:, bass.ds(i * SEQ, SEQ)]).then_inc(sem("at_operands"), 1)
                pool.tensor_tensor(
                    km[:, u, :, :], kr1[:, bass.ds(i * SEQ, SEQ)].unsqueeze(1).to_broadcast([P, HEADS, SEQ]),
                    L["headmask"][:, :].unsqueeze(2).to_broadcast([P, HEADS, SEQ]), ALU.mult) \
                    .then_inc(sem("at_operands"), 1)

            rotated(0)
            loaded(pool, "headmask")
            pool.wait_ge(sem("rot_done"), 2)
            head_keys(0, 0)
            rotated(1)
            head_keys(1, 1)
            pool.wait_ge(sem("rot_done"), 4)
            with pool.Fori(1, IMAGES // 2) as p:
                for u in range(2):
                    hold(pool, sem("at_scores"), p * 2 + u - 1)
                    head_keys(p * 2 + u, u)

            for k in range(4):
                at = slice(2 * k, 2 * k + 2)
                pool.wait_ge(sem("moe_high"), 2 * k + 1)
                pool.tensor_tensor(w1l[:, at], L["mw1"][:, at], w1h[:, at], ALU.subtract) \
                    .then_inc(sem("moe_low"), 1)
                pool.wait_ge(sem("moe_high"), 2 * k + 2)
                pool.tensor_tensor(w2l[:, at], L["mw2"][:, at], w2h[:, at], ALU.subtract) \
                    .then_inc(sem("moe_low"), 1)
            for c in range(4):
                pool.wait_ge(sem("moe_high"), c + 9)
                pool.tensor_tensor(quarter(xl, c), quarter(x2, c), quarter(xh, c), ALU.subtract) \
                    .then_inc(sem("moe_low"), 1)
            with pool.Fori(0, 4) as c:
                for e in range(EXPERTS):
                    pool.wait_ge(sem("moe_split"), (c * 8 + e) * 3 + 2)
                    pool.tensor_tensor(mhl[:, e % 2, 2:4, :], mhid[:, e % 2, 2:4, :], mhh[:, e % 2, 2:4, :], ALU.subtract) \
                        .then_inc(sem("moe_hl_pool"), 1)

        @block.scalar
        def _(act):
            loaded(act, "eps")
            act.activation(noise[:, :], L["eps"][:, :], ACT.Abs).then_inc(sem("noise_root"), 1)
            act.activation(nsign[:, :], L["eps"][:, :], ACT.Sign).then_inc(sem("noise_root"), 1)
            act.wait_ge(sem("noise_root"), 1)
            act.activation(noise[:, :], noise[:, :], ACT.Sqrt).then_inc(sem("noise_root"), 1)
            act.wait_ge(sem("key_steps"), 2)
            act.activation(kn[:, :], kn[:, :], ACT.Sqrt).then_inc(sem("key_norm"), 1)
            warm(act, ACT.Exp, 7)
            act.wait_ge(sem("tok_weight_steps"), 2)
            for c in range(4):
                act.wait_ge(sem("tok_linear"), 2 * c + 2)
                act.activation(gexp[:, c, :], B[:, c, 0:CHUNK], ACT.Exp, bias=bn[:, 0:1]).then_inc(sem("tok_exp"), 1)

            ln_scalar(act, LN_GAU)
            for c in range(4):
                act.wait_ge(sem("ln_done"), 4 * LN_GAU + c + 1)
                act.activation(quarter(sq, c), quarter(xn, c), ACT.Square).then_inc(sem("l2_squared"), 1)
            for c in range(4):
                act.wait_ge(sem("l2_sum"), c + 1)
                act.activation(dev[:, c * SEQ:(c + 1) * SEQ], B[:, 2 * c + 1, 0:SEQ], ACT.Sqrt) \
                   .then_inc(sem("l2_norm"), 1)
            warm(act, ACT.Silu, 6)

            def gau_silu(c):
                u = c % 2
                k = 4 * u
                for blk in range(2):
                    act.wait_ge(sem("gau_uv"), 3 * c + blk + 1)
                    act.activation(ug[:, u, blk, :], B[:, k + blk, 0:Q], ACT.Silu).then_inc(sem("gau_u"), 1)
                act.wait_ge(sem("gau_uv"), 3 * c + 3)
                act.activation(base[:, u, :], B[:, k + 2, 0:Q], ACT.Silu).then_inc(sem("gau_base"), 1)
                for pr in range(2):
                    act.wait_ge(sem("gau_v"), 2 * c + pr + 1)
                    act.activation(vtok[:, u, 2 * pr:2 * pr + 2, :],
                                   B[0:SEQ, k + (3 if pr == 0 else 0), :].rearrange("p (i n) -> p i n", i=2),
                                   ACT.Silu).then_inc(sem("gau_vtok"), 1)

            def gau_relu(c):
                act.wait_ge(sem("gau_biased"), c + 1)
                act.activation(relu[:, c % 2], biased[:, c % 2], ACT.Relu, scale=float(1.0 / np.sqrt(np.float32(P)))) \
                   .then_inc(sem("gau_relu"), 1)

            for c in range(0, 4, 2):
                gau_silu(c)
                gau_silu(c + 1)
                gau_relu(c)
                gau_relu(c + 1)

            ln_scalar(act, LN_KEYS)
            def queries(i):
                act.activation(qt[:, :, :], qln[:, :, bass.ds(i * TILE, TILE)], ACT.Copy).then_inc(sem("pk_qt"), 1)

            def squares(m):
                act.wait_ge(sem("q_centred"), m + 1)
                act.activation(halves(sq, m % 2), banks(2 * (m % 2)), ACT.Square, bias=bqc[:, m // 2:m // 2 + 1]) \
                   .then_inc(sem("q_squared"), 1)

            def deviation(m):
                act.wait_ge(sem("q_variance"), m + 1)
                act.activation(dev[:, m % 2 * EIGHTH:(m % 2 + 1) * EIGHTH], B[:, 4 + 2 * (m % 2), 0:EIGHTH], ACT.Sqrt, bias=col("eps")) \
                   .then_inc(sem("q_std"), 1)

            def affine(m, out, func):
                hf = m % 2
                act.wait_ge(sem("q_z"), m + 1)
                act.activation(out[:, m // 2, hf * HALF:(hf + 1) * HALF], z[:, hf, :], func,
                               bias=col("lnb"), scale=col("lng")).then_inc(sem("q_ln"), 1)

            squares(0)
            deviation(0)
            for m in range(8):
                if m + 1 < 8:
                    squares(m + 1)
                if m:
                    affine(m - 1, qln, ACT.Identity)
                if m + 1 < 8:
                    deviation(m + 1)
                if m:
                    affine(m - 1, sq2, ACT.Square)
            act.wait_ge(sem("q_ln"), 14)
            queries(0)
            affine(7, qln, ACT.Identity)
            affine(7, sq2, ACT.Square)

            def scores_out(i):
                act.wait_ge(sem("pk_scores"), i + 1)
                act.activation(s1[:, :, :].rearrange("p l e -> p (l e)"), PS[0:TILE, 0:LISTS * KEYS], ACT.Copy) \
                   .then_inc(sem("pk_s1"), 1)

            def indices_out(i):
                act.wait_ge(sem("pk_index"), i + 1)
                act.activation(vi[:, 1].rearrange("p l r -> p (l r)"), iu[:, :, :].rearrange("p l r -> p (l r)"),
                               ACT.Copy).then_inc(sem("pk_indices"), 1)

            def transposed_out(i):
                for k in range(2):
                    act.wait_ge(sem("pk_turned"), i * 2 + k + 1)
                    act.activation(xt[:, 8 * k:8 * k + 8, :].rearrange("p k t -> p (k t)"),
                                   PS[0:PAIR, (2 + k) * 512:(3 + k) * 512].bitcast(BF16)[:, 0:8 * TILE], ACT.Copy) \
                       .then_inc(sem("pk_xt"), 1)

            def softmax_terms(i):
                act.wait_ge(sem("pk_mneg"), i + 1)
                for k in range(HEADS):
                    last = act.activation(ex[:, k, :], cc[:, k, :], ACT.Exp, bias=mneg[:, k:k + 1])
                last.then_inc(sem("pk_exp"), 1)
                act.wait_ge(sem("pk_m"), i * 3 + 3)
                for k in range(HEADS):
                    last = act.activation(me[:, k, :], mm[:, k, :], ACT.Exp, bias=mneg[:, k:k + 1],
                                          accum_out=wz[:, k:k + 1])
                last.then_inc(sem("pk_total"), 1)

            def expert_out(i):
                act.wait_ge(sem("pk_cand"), i * 7 + 7)
                act.activation(x4b[:, PARTS, :], cc[:, HEADS:, :].rearrange("p h c -> p (h c)"), ACT.Copy) \
                   .then_inc(sem("pk_expert"), 1)

            def weight_parts(i):
                act.wait_ge(sem("pk_weights"), i + 1)
                act.activation(x4b[:, 0, :], wn[:, :, :].rearrange("p h c -> p (h c)"), ACT.Copy) \
                   .then_inc(sem("pk_part0"), 1)
                act.wait_ge(sem("pk_rem"), i + 1)
                act.activation(x4b[:, 1, :], rem[:, :, :].rearrange("p h c -> p (h c)"), ACT.Copy) \
                   .then_inc(sem("pk_part1"), 1)

            def b_onehots(i, first, end):
                act.wait_ge(sem("pk_ab"), i * 3 + 3)
                at = COLS["minus"][0]
                for b in range(first, end):
                    last = act.activation(far[:, b, :], eb[:, :], ACT.Abs, bias=cols[0:PAIR, at + b:at + b + 1])
                last.then_inc(sem("pk_far"), 1)
                act.wait_ge(sem("pk_far"), i * 2 + (1 if first == 0 else 2))
                for b in range(first, end):
                    last = act.activation(bt[:, :, :, b, :], far[:, b, :].rearrange("p (c j g) -> p c j g", c=PAIRS, j=QUAD),
                                          ACT.Relu, scale=-1.0, bias=1.0)
                last.then_inc(sem("pk_bt_act"), 1)

            def act_tile(i, prev, more):
                if more and prev:
                    act.wait_ge(sem("pk_scores"), i + 1)
                    queries(i + 1)
                if prev:
                    transposed_out(i - 1)
                if more:
                    act.wait_ge(sem("pk_lists"), i + 1)
                    scores_out(i + 1)
                if prev:
                    indices_out(i)
                    b_onehots(i - 1, 0, ACT_EARLY)
                softmax_terms(i)
                if prev:
                    b_onehots(i - 1, ACT_EARLY, ACT_B)
                expert_out(i)
                weight_parts(i)

            scores_out(0)
            queries(1)
            act.wait_ge(sem("q_norm2"), 8)
            n = NT // 2 * LISTS
            for hf in range(2):
                act.activation(qn[:, hf * n:(hf + 1) * n], B[0:TILE, 7 - 2 * hf, NORMS:NORMS + n], ACT.Sqrt) \
                   .then_inc(sem("q_norm"), 1)
            for t in range(NT):
                act.wait_ge(sem("pk_inner"), t + 1)
                for j in range(QUAD):
                    r = slice(EB * j, EB * (j + 1))
                    src = B[r, 4 + t % 4, 0:EA * TILE].rearrange("p (a j g) -> p a j g", a=EA, j=QUAD)[:, :, j, :]
                    last = act.activation(gelu[r, :, t * GROUPS:(t + 1) * GROUPS], src, ACT.Gelu)
                last.then_inc(sem("pk_gelu"), 1)
            indices_out(0)
            warm(act, ACT.Exp, 0)
            act_tile(0, False, True)
            with act.Fori(1, NT - 1) as i:
                act_tile(i, True, True)
            act_tile(NT - 1, True, False)
            transposed_out(NT - 1)
            b_onehots(NT - 1, 0, ACT_EARLY)
            warm(act, ACT.Sqrt, LN_BLOCK)
            for c in range(2):
                ln_square(act, LN_BLOCK, c)
            for c in range(2):
                ln_deviation(act, LN_BLOCK, c)

            for c in range(2, 4):
                ln_square(act, LN_BLOCK, c)
            for c in range(2, 4):
                ln_deviation(act, LN_BLOCK, c)
            for g in range(4):
                act.wait_ge(sem("at_v"), g + 1)
                act.activation(vaug[:, 4 * g:4 * g + 4, :, 0:HD],
                               B[0:SEQ, 4 + g, :].rearrange("p (i h d) -> p i h d", i=4, h=HEADS),
                               ACT.Copy).then_inc(sem("at_vaug"), 1)

            warm(act, ACT.Exp, 8)
            act.sem_inc(sem("at_ct"), 1)

            def exps(i, u):
                act.wait_ge(sem("at_dif"), i + 1)
                act.activation(pe_[:, u, :, :], sd[:, u, :, :], ACT.Exp, scale=float(HD) ** -0.5) \
                   .then_inc(sem("at_exp"), 1)

            def probs_out(i, u):
                act.wait_ge(sem("at_turned"), i + 1)
                act.activation(pt[:, u, :, :].rearrange("p (b h) n -> p b (h n)", b=2),
                               B[0:SEQ, 4:6, 0:4 * SEQ], ACT.Copy).then_inc(sem("at_pt"), 1)

            def context_out(i):
                act.wait_ge(sem("at_cturned"), i + 1)
                act.activation(ct[:, bass.ds(i * SEQ, SEQ)], B[:, 7, 0:SEQ], ACT.Copy).then_inc(sem("at_ct"), 1)

            exps(0, 0)
            probs_out(0, 0)
            exps(1, 1)
            with act.Fori(1, IMAGES // 2) as p:
                for u in range(2):
                    probs_out(p * 2 + u - 1, 1 - u)
                    exps(p * 2 + u, u)
                    context_out(p * 2 + u - 2)
            probs_out(IMAGES - 1, 1)
            context_out(IMAGES - 2)
            context_out(IMAGES - 1)

            ln_scalar(act, LN_POST1)
            for c in range(4):
                act.wait_ge(sem("ln_done"), 4 * LN_POST1 + c + 1)
                act.activation(quarter(x4, c), quarter(x2, c), ACT.Identity, bias=col("be1"), scale=col("g1")) \
                   .then_inc(sem("post1"), 1)
            for hf in range(2):
                for k in range(4):
                    act.wait_ge(sem("ff_up"), 4 * hf + k + 1)
                    act.activation(hid[:, k, :].rearrange("p (q n) -> p q n", q=2), banks(2 * (k % 2)), ACT.Relu,
                                   bias=col("b1", k)).then_inc(sem("ff_hid"), 1)
            ln_scalar(act, LN_POST2)
            for c in range(4):
                act.wait_ge(sem("ln_done"), 4 * LN_POST2 + c + 1)
                act.activation(quarter(x4, c), quarter(x2, c), ACT.Identity, bias=col("be2"), scale=col("g2")) \
                   .then_inc(sem("post2"), 1)

            ln_scalar(act, LN_MOE)
            act.sem_inc(sem("moe_hid"), 4)
            act.wait_ge(sem("moe_route"), 3)
            act.activation(ge[:, :], gd[:, :], ACT.Exp).then_inc(sem("moe_gexp"), 1)
            for k in range(2):
                act.wait_ge(sem("moe_turned"), k + 1)
                act.activation(mt[:, k * HALF:(k + 1) * HALF],
                               B[0:PARTS * EXPERTS, 6 + k, 0:Q].bitcast(BF16), ACT.Copy).then_inc(sem("moe_mt"), 1)
            act.sem_inc(sem("moe_mb"), 2)
            with act.Fori(0, 4) as c:
                for e in range(EXPERTS):
                    act.wait_ge(sem("moe_down"), c * 8 + e + 1)
                    for k in range(4):
                        act.wait_ge(sem("moe_up"), c * 32 + 4 * e + k + 1)
                        act.activation(mhid[:, e % 2, k, :], B[:, k, 0:Q], ACT.Relu, bias=col("mb1", 4 * e + k)) \
                           .then_inc(sem("moe_hid"), 1)
                    act.wait_ge(sem("moe_tmp"), c * 8 + e + 1)
                    act.wait_ge(sem("moe_mask"), c * 8 + e + 1)
                    act.activation(mb[:, e % 2, :], B[:, 6 + e % 2, 0:Q], ACT.Copy).then_inc(sem("moe_mb"), 1)

        @block.tensor
        def _(pe):
            loaded(pe, "pat")
            pe.wait_ge(sem("tok_weight_steps"), 10)
            for c in range(4):
                for br in range(2):
                    for k in range(2):
                        last = pe.matmul(B[:, c, br * CHUNK:(br + 1) * CHUNK], wnt[:, br, k, :],
                                         L["pat"][:, k, c * CHUNK:(c + 1) * CHUNK], start=(k == 0), stop=(k == 1))
                    last.then_inc(sem("tok_linear"), 1)

            loaded(pe, "wq")
            for k in range(4):
                pe.matmul(B[:, 6, k * P:(k + 1) * P], L["wq"][:, k, :], L["centre64"][:, :], start=True, stop=True)
            pe.matmul(B[:, 7, KEYS:KEYS + 4], L["centre64"][:, :], cols[:, COLS["bq"][0]:COLS["bq"][0] + 4],
                      start=True, stop=True)
            pe.wait_ge(sem("key_unit"), 2)
            pe.transpose(B[:, 7, 0:KEYS], kk[:, :, :, :].rearrange("p a b c -> p (a b c)"), L["ident"][0:KEYS, 0:KEYS]) \
              .then_inc(sem("key_turned"), 1)

            for c in range(4):
                pe.wait_ge(sem("tok_prod"), c + 1)
                if c >= 2:
                    pe.wait_ge(sem("tok_h"), c)
                pe.matmul(B[:, 4 + c % 2, 0:CHUNK], L["w3"][:, :], prod[:, c, :], start=True, stop=True) \
                  .then_inc(sem("tok_third"), 1)

            loaded(pe, "centre")
            ln_tensor(pe, LN_GAU, h, "tok_h", lambda c: c + 2)
            for c in range(4):
                pe.wait_ge(sem("l2_squared"), c + 1)
                spread(pe, "ones", sq, c * Q, SEQ, 2 * c + 1).then_inc(sem("l2_sum"), 1)
            for c in range(4):
                pe.wait_ge(sem("l2_steps"), 2 * c + 2)
                gathered(pe, inv[:, c * SEQ:(c + 1) * SEQ], SEQ, 2 * c + 1).then_inc(sem("l2_inverse"), 1)

            def gau_in(c):
                k = 4 * (c % 2)
                pe.wait_ge(sem("l2_done"), min(2 * c + 2, 4))
                if c >= 2:
                    pe.wait_ge(sem("gau_h"), 2 * c - 2)
                x = x2[:, c * Q:(c + 1) * Q]
                for n, at in ((0, 0), (1, P), (2, 4 * P)):
                    pe.matmul(B[:, k + n, 0:Q], L["uvw"][:, at:at + P], x, start=True, stop=True) \
                      .then_inc(sem("gau_uv"), 1)
                for pr in range(2):
                    if pr:
                        pe.wait_ge(sem("gau_u"), 2 * c + 1)
                    for m in range(2):
                        at = c * Q + (2 * pr + m) * SEQ
                        last = pe.matmul(B[0:SEQ, k + (3 if pr == 0 else 0), m * 256:(m + 1) * 256],
                                         x2[:, at:at + SEQ], L["uvw"][:, 2 * P:4 * P], start=True, stop=True)
                    last.then_inc(sem("gau_v"), 1)

            def gau_scores(c):
                k = 4 * (c % 2)
                pe.wait_ge(sem("gau_qk"), 2 * c + 2)
                for m in range(4):
                    last = pe.matmul(B[0:SEQ, k + 2, m * SEQ:(m + 1) * SEQ], kg[:, c % 2, m * SEQ:(m + 1) * SEQ],
                                     qg[:, c % 2, m * SEQ:(m + 1) * SEQ], start=True, stop=True)
                last.then_inc(sem("gau_scores"), 1)

            def gau_mix(c):
                u, k = c % 2, 4 * (c % 2)
                pe.wait_ge(sem("gau_kernel"), c + 1)
                pe.wait_ge(sem("gau_vtok"), 2 * c + 2)
                for blk in range(2):
                    for m in range(4):
                        last = pe.matmul(B[:, k + (1, 3)[blk], m * SEQ:(m + 1) * SEQ],
                                         vtok[:, u, m, blk * P:(blk + 1) * P], kern[:, u, m, :], start=True, stop=True)
                    last.then_inc(sem("gau_mixed"), 1)

            def gau_project(c):
                u, k = c % 2, 4 * (c % 2)
                pe.wait_ge(sem("gau_uo"), 2 * c + 2)
                for blk in range(2):
                    last = pe.matmul(B[:, k + 2, 0:Q], L["ow"][:, blk, :], uo[:, u, blk, :],
                                     start=(blk == 0), stop=(blk == 1))
                last.then_inc(sem("gau_out"), 1)

            loaded(pe, "uvw")
            loaded(pe, "ow")
            for c in range(0, 4, 2):
                gau_in(c)
                gau_in(c + 1)
                gau_scores(c)
                gau_scores(c + 1)
                gau_mix(c)
                gau_mix(c + 1)
                gau_project(c)
                gau_project(c + 1)

            ln_tensor(pe, LN_KEYS, h, "gau_h", lambda c: (2, 6, 6, 8)[c])
            pe.wait_ge(sem("wqc_ready"), 2)
            loaded(pe, "mean64")

            def q_centre(m):
                if m >= 2:
                    pe.wait_ge(sem("q_shifted"), m - 1)
                for q in range(2):
                    at = (2 * (m % 2) + q) * Q
                    last = pe.matmul(B[:, 2 * (m % 2) + q, 0:Q], wqc[:, m // 2, :], x2[:, at:at + Q],
                                     start=True, stop=True)
                last.then_inc(sem("q_centred"), 1)

            def q_variance(m):
                pe.wait_ge(sem("q_squared"), m + 1)
                if m >= 2:
                    pe.wait_ge(sem("q_z"), m - 1)
                spread(pe, "mean64", sq, m % 2 * HALF, EIGHTH, 4 + 2 * (m % 2)).then_inc(sem("q_variance"), 1)

            loaded(pe, "blk32")

            def q_norms(m):
                pe.wait_ge(sem("q_ln"), 2 * m + 2)
                k, hf = m // 2, m % 2
                for t in range(NT // 2):
                    at = NORMS + t * LISTS + 4 * k
                    token = hf * HALF + t * TILE
                    last = pe.matmul(B[0:TILE, 7 - 2 * hf, at:at + 4], sq2[:, k, token:token + TILE],
                                     L["blk32"][:, :], start=True, stop=True)
                last.then_inc(sem("q_norm2"), 1)

            pe.wait_ge(sem("ln_done"), 4 * LN_KEYS + 2)
            q_centre(0)
            pe.wait_ge(sem("ln_done"), 4 * LN_KEYS + 4)
            q_centre(1)
            q_variance(0)
            for m in range(8):
                pe.wait_ge(sem("q_inverse"), m + 1)
                gathered(pe, inv[:, m % 2 * EIGHTH:(m % 2 + 1) * EIGHTH], EIGHTH, 4 + 2 * (m % 2)).then_inc(sem("q_rstd"), 1)
                if m + 1 < 8:
                    q_variance(m + 1)
                if m + 2 < 8:
                    q_centre(m + 2)
                if 2 <= m < 7:
                    q_norms(m - 2)
            def pk_scores(i):
                pe.wait_ge(sem("pk_qt"), i + 1)
                for k in range(PAIRS):
                    last = pe.matmul(PS[0:TILE, k * 256:(k + 1) * 256], qt[:, k, :], kbd[:, :], start=True, stop=True)
                last.then_inc(sem("pk_scores"), 1)

            def pk_turn(i):
                pe.wait_ge(sem("pk_part2"), i + 1)
                pe.wait_ge(sem("pk_expert"), i + 1)
                for k in range((PARTS + 1) * PAIRS):
                    bank = PS[0:PAIR, (2 + k // 8) * 512:(3 + k // 8) * 512].bitcast(BF16)
                    arr, pr = k // PAIRS, k % PAIRS
                    last = pe.transpose(bank[:, (k % 8) * TILE:(k % 8 + 1) * TILE],
                                        x4b[:, arr, pr * PAIR:(pr + 1) * PAIR], L["identb"][0:TILE, 0:TILE])
                    if k % 8 == 7:
                        last.then_inc(sem("pk_turned"), 1)

            def pk_scatter(i, last_tile=False):
                pe.wait_ge(sem("pk_bt"), i + 1)
                pe.wait_ge(sem("pk_bt_pool"), i + 1)
                pe.wait_ge(sem("pk_bt_act"), i * 2 + (1 if last_tile else 2))
                pe.wait_ge(sem("pk_aw"), i + 1)
                for g in range(GROUPS):
                    for k in range(PAIRS):
                        last = pe.matmul(
                            B[:, 5 + g // PER_BANK, (g % PER_BANK) * 48:(g % PER_BANK + 1) * 48],
                            bt[:, k, :, :, g].rearrange("p j b -> p (j b)"),
                            aw[:, :, :, k, :].rearrange("p a q (j g) -> p j a q g", j=QUAD)[:, :, :, :, g],
                            start=(k == 0), stop=(k == PAIRS - 1))
                last.then_inc(sem("pk_scattered"), 1)

            def pk_up(i):
                pe.wait_ge(sem("pk_wg"), i * 4 + 4)
                pe.wait_ge(sem("pk_h"), i + 1)
                for a in range(EA):
                    for q in range(PARTS):
                        last = pe.matmul(B[:, 4, 0:TILE], L["up"][:, a, :], wg[:, :, 0:GROUPS, a, q],
                                         start=(a == 0 and q == 0), stop=(a == EA - 1 and q == PARTS - 1))
                last.then_inc(sem("pk_out"), 1)

            def pe_tile(i, prev, more):
                if prev:
                    pk_turn(i - 1)
                if more:
                    pe.wait_ge(sem("pk_s1"), i + 1)
                    pk_scores(i + 1)
                if prev == 2:
                    pk_up(i - 2)
                if prev:
                    pk_scatter(i - 1)

            pe.wait_ge(sem("kbd_ready"), 5)
            loaded(pe, "identb")
            loaded(pe, "up")
            for m in (5, 6, 7):
                pe.wait_ge(sem("q_z"), min(m + 2, 8))
                if m == 7:
                    pk_scores(0)
                q_norms(m)

            loaded(pe, "down")
            pe.wait_ge(sem("q_norm"), 2)
            for t in range(NT):
                if t >= 4:
                    pe.wait_ge(sem("pk_gelu"), t - 3)
                for a in range(EA):
                    last = pe.matmul(B[:, 4 + t % 4, a * TILE:(a + 1) * TILE], L["down"][:, a, :],
                                     x2[:, t * TILE:(t + 1) * TILE], start=True, stop=True)
                last.then_inc(sem("pk_inner"), 1)
            pe_tile(0, 0, True)
            pe.wait_ge(sem("pk_gelu"), NT)
            pe_tile(1, 1, True)
            with pe.Fori(2, NT - 1) as i:
                pe_tile(i, 2, True)
            pe_tile(NT - 1, 2, False)
            pk_turn(NT - 1)
            pe.wait_ge(sem("pk_h"), NT // 2 + 1)
            ln_centre(pe, 0, h)
            pk_up(NT - 2)
            pe.wait_ge(sem("pk_xt"), 2 * NT)
            ln_centre(pe, 1, h)
            for c in range(2):
                ln_variance(pe, LN_BLOCK, c)
            pk_scatter(NT - 1, True)
            for c in range(2):
                ln_back(pe, LN_BLOCK, c)
            pk_up(NT - 1)

            pe.wait_ge(sem("pk_h"), NT + 1)
            for c in range(2, 4):
                ln_centre(pe, c, h)
            for c in range(2, 4):
                ln_variance(pe, LN_BLOCK, c)
            for c in range(2, 4):
                ln_back(pe, LN_BLOCK, c)
            loaded(pe, "qkv")
            pe.wait_ge(sem("ln_done"), 4 * LN_BLOCK + 2)
            for hf in range(2):
                for k in range(4):
                    if hf:
                        pe.wait_ge(sem("rot_parts"), k + 1)
                    elif k == 2:
                        pe.wait_ge(sem("ln_done"), 4 * LN_BLOCK + 4)
                    for q in range(2):
                        at = (2 * hf + q) * Q
                        last = pe.matmul(B[:, 2 * k + q, 0:Q], L["qkv"][:, k, :], x2[:, at:at + Q],
                                         start=True, stop=True)
                    last.then_inc(sem("rot_linear"), 1)
            for g in range(4):
                pe.wait_ge(sem("rot_parts"), 4 + 2 + g // 2 + 1)
                for m in range(4):
                    at = (4 * g + m) * SEQ
                    last = pe.matmul(B[0:SEQ, 4 + g, m * P:(m + 1) * P], x2[:, at:at + SEQ], L["qkv"][:, 4, :],
                                     start=True, stop=True)
                last.then_inc(sem("at_v"), 1)

            def at_scores(i, u):
                pe.wait_ge(sem("at_operands"), i * 2 + 2)
                for b in range(2):
                    last = pe.matmul(B[0:SEQ, 2 * u + b, 0:4 * SEQ], qb[:, u, :],
                                     km[:, u, 4 * b:4 * b + 4, :].rearrange("p h n -> p (h n)"), start=True, stop=True)
                last.then_inc(sem("at_scores"), 1)

            def at_turn(i, u):
                pe.wait_ge(sem("at_exp"), i + 1)
                for hh in range(HEADS):
                    last = pe.transpose(B[0:SEQ, 4 + hh // 4, (hh % 4) * SEQ:(hh % 4 + 1) * SEQ], pe_[:, u, hh, :],
                                        L["ident"][0:SEQ, 0:SEQ])
                last.then_inc(sem("at_turned"), 1)

            def at_context(i, u):
                pe.wait_ge(sem("at_pt"), i + 1)
                for hh in range(HEADS):
                    last = pe.matmul(B[0:SEQ, 6, hh * (HD + 1):(hh + 1) * (HD + 1)], pt[:, u, hh, :],
                                     vaug[:, bass.ds(i, 1), hh, :].rearrange("p i d -> p (i d)"),
                                     start=True, stop=True)
                last.then_inc(sem("at_context"), 1)

            def at_cturn(i, u):
                pe.wait_ge(sem("at_cn"), i + 1)
                pe.wait_ge(sem("at_ct"), i + 1)
                pe.transpose(B[:, 7, 0:SEQ], cn[:, u, :, :].rearrange("p h d -> p (h d)"), L["ident"][0:SEQ, 0:SEQ]) \
                  .then_inc(sem("at_cturned"), 1)

            def at_step(i, u):
                pe.wait_ge(sem("at_dif"), i)
                at_scores(i + 1, 1 - u)
                at_cturn(i - 2, u)
                at_context(i - 1, 1 - u)
                at_turn(i, u)

            at_scores(0, 0)
            at_scores(1, 1)
            pe.wait_ge(sem("at_vaug"), 4)
            pe.wait_ge(sem("vaug_ones"), 1)
            at_turn(0, 0)
            pe.wait_ge(sem("at_dif"), 1)
            at_scores(2, 0)
            at_context(0, 0)
            at_turn(1, 1)
            with pe.Fori(1, IMAGES // 2 - 1) as p:
                for u in range(2):
                    at_step(p * 2 + u, u)
            at_step(IMAGES - 2, 0)
            at_cturn(IMAGES - 3, 1)
            at_context(IMAGES - 2, 0)
            at_turn(IMAGES - 1, 1)
            at_cturn(IMAGES - 2, 0)
            at_context(IMAGES - 1, 1)
            at_cturn(IMAGES - 1, 1)

            loaded(pe, "wo")
            pe.wait_ge(sem("at_ct"), IMAGES + 1)
            for c in range(4):
                pe.matmul(B[:, 2 * c, 0:Q], L["wo"][:, :], quarter(ct, c), start=True, stop=True) \
                  .then_inc(sem("wo_out"), 1)
            ln_tensor(pe, LN_POST1, xn, "wo_res", lambda c: c + 1)
            loaded(pe, "w1")
            loaded(pe, "w2")
            for hf in range(2):
                pe.wait_ge(sem("post1"), 2 * hf + 2)
                for k in range(4):
                    if 4 * hf + k >= 2:
                        pe.wait_ge(sem("ff_hid"), 4 * hf + k - 1)
                    for q in range(2):
                        at = (2 * hf + q) * Q
                        last = pe.matmul(B[:, 2 * (k % 2) + q, 0:Q], L["w1"][:, k, :], x4[:, at:at + Q],
                                         start=True, stop=True)
                    last.then_inc(sem("ff_up"), 1)
                pe.wait_ge(sem("ff_hid"), 4 * hf + 4)
                pe.wait_ge(sem("ln_done"), 4 * LN_POST1 + 4)
                for q in range(2):
                    for k in range(4):
                        last = pe.matmul(B[:, 4 + 2 * hf + q, 0:Q], L["w2"][:, k, :], hid[:, k, q * Q:(q + 1) * Q],
                                         start=(k == 0), stop=(k == 3))
                last.then_inc(sem("ff_down"), 1)
            ln_tensor(pe, LN_POST2, xn, "ff_res", lambda c: c // 2 + 1)

            ln_tensor(pe, LN_MOE, h, "post_h", lambda c: c + 1)
            loaded(pe, "wr")
            pe.wait_ge(sem("ln_done"), 4 * LN_MOE + 4)
            for t in range(NT):
                last = pe.matmul(B[0:TILE, 4, t * EXPERTS:(t + 1) * EXPERTS], x2[:, t * TILE:(t + 1) * TILE],
                                 L["wr"][:, :], start=True, stop=True)
            last.then_inc(sem("moe_logits"), 1)
            def split_products(out, pairs, first=True, last=True):
                for n, (w, x) in enumerate(pairs):
                    made = pe.matmul(out, w, x, start=first and n == 0,
                                     stop=last and n == len(pairs) - 1)
                return made

            def moe_up(c, e, at):
                for k in range(4):
                    pe.wait_ge(sem("moe_hid"), c * 32 + 4 * e + k + 1)
                    wh, wl = w1h[:, e, k * P:(k + 1) * P], w1l[:, e, k * P:(k + 1) * P]
                    split_products(B[:, k, 0:Q], ((wh, xh[:, at]), (wl, xh[:, at]), (wh, xl[:, at]))) \
                        .then_inc(sem("moe_up"), 1)

            pe.wait_ge(sem("moe_low"), 9)
            for name in ("mw1", "mw2"):
                loaded(pe, name)
            moe_up(0, 0, slice(0, Q))
            pe.wait_ge(sem("moe_parts"), 6)
            for t in range(NT):
                k, at = t // (NT // 2), t % (NT // 2) * TILE
                last = pe.transpose(B[0:PARTS * EXPERTS, 6 + k, 0:Q].bitcast(BF16)[:, at:at + TILE],
                                    mparts[:, t, :, :].rearrange("p q e -> p (q e)"), L["identb"][0:TILE, 0:TILE])
                if t % (NT // 2) == NT // 2 - 1:
                    last.then_inc(sem("moe_turned"), 1)
            pe.wait_ge(sem("moe_mt"), 2)
            pe.wait_ge(sem("moe_low"), 12)
            pe.sem_inc(sem("moe_down"), 2)

            def moe_down(c, e):
                n, u, out = c * 8 + e, e % 2, B[:, 4 + e % 2, 0:Q]
                pe.wait_ge(sem("moe_split"), n * 3 + 2)
                pe.wait_ge(sem("moe_tmp"), n + 1)
                split_products(out, [(w[:, e, k, :], mhh[:, u, k, :]) for k in range(4) for w in (w2h, w2l)],
                               last=False)
                pe.wait_ge(sem("moe_split"), n * 3 + 3)
                split_products(out, [(w2h[:, e, k, :], mhl[:, u, k, :]) for k in range(2)], first=False, last=False)
                pe.wait_ge(sem("moe_hl_pool"), n + 1)
                split_products(out, [(w2h[:, e, k, :], mhl[:, u, k, :]) for k in range(2, 4)], first=False) \
                    .then_inc(sem("moe_down"), 1)

            def moe_quarter(c, last_quarter):
                for e in range(EXPERTS):
                    hold(pe, sem("moe_mb"), c * 8 + e + 1)
                    pe.matmul(B[:, 6 + e % 2, 0:Q], L["selm"][:, e, :], mt[:, bass.ds(c * Q, Q)],
                              start=True, stop=True).then_inc(sem("moe_mask"), 1)
                    if e + 1 < EXPERTS:
                        moe_up(c, e + 1, bass.ds(c * Q, Q))
                    elif not last_quarter:
                        moe_up(c + 1, 0, bass.ds(c * Q + Q, Q))
                    moe_down(c, e)

            with pe.Fori(0, 3) as c:
                moe_quarter(c, False)
            moe_quarter(3, True)

        @block.vector
        def _(dve):
            dve.wait_ge(sem("noise_root"), 3)
            dve.tensor_tensor(noise[:, :], noise[:, :], nsign[:, :], ALU.mult).then_inc(sem("noise_root"), 1)
            dve.wait_ge(sem("noise_root"), 4)
            loaded(dve, "cols")
            for br in range(2):
                dve.scalar_tensor_tensor(bn[:, br:br + 1], col(("w1sb", "w2sb")[br]), noise[:, 4 + br:5 + br],
                                         col(("w1b", "w2b")[br]), ALU.mult, ALU.add).then_inc(sem("tok_weight_steps"), 1)
            loaded(dve, "tokw")
            for br in range(2):
                for k in range(2):
                    dve.scalar_tensor_tensor(wnt[:, br, k, :], noise[:, 6 + br * P:6 + (br + 1) * P],
                                             noise[:, 2 * br + k:2 * br + k + 1], L["tokw"][:, br, 1, k, :],
                                             ALU.mult, ALU.mult).then_inc(sem("tok_weight_steps"), 1)
            for br in range(2):
                for k in range(2):
                    dve.wait_ge(sem("tok_weight_steps"), 2 * br + k + 3)
                    dve.tensor_tensor(wnt[:, br, k, :], wnt[:, br, k, :], L["tokw"][:, br, 0, k, :], ALU.add) \
                       .then_inc(sem("tok_weight_steps"), 1)
            loaded(dve, "keys")
            dve.tensor_tensor(ksq[:, :, :], L["keys"][:, :, :], L["keys"][:, :, :], ALU.mult).then_inc(sem("key_steps"), 1)
            dve.wait_ge(sem("key_steps"), 1)
            dve.tensor_reduce(kn[:, :], ksq[:, :, :], AX.X, ALU.add).then_inc(sem("key_steps"), 1)
            dve.memset(kbd[:, :], 0.0).then_inc(sem("kbd_ready"), 1)
            dve.memset(gelu[:, :, T // QUAD:], 0.0).then_inc(sem("pk_zeroed"), 1)
            dve.memset(wg[:, :, :, :, :], 0.0).then_inc(sem("pk_zeroed"), 1)
            hv = h[:, :].rearrange("p (i s) -> p i s", i=IMAGES)
            dve.tensor_copy(hv[:, :, 0:1], col("cls").unsqueeze(1).to_broadcast([P, IMAGES, 1])) \
               .then_inc(sem("tok_h"), 1)
            dve.wait_ge(sem("key_norm"), 1)
            dve.tensor_scalar(knc[:, :], kn[:, :], 1e-12, None, ALU.max).then_inc(sem("key_steps"), 1)
            dve.wait_ge(sem("key_steps"), 3)
            dve.reciprocal(kr[:, :], knc[:, :]).then_inc(sem("key_steps"), 1)
            dve.wait_ge(sem("key_steps"), 4)
            for d in range(2):
                dve.tensor_tensor(kk[:, d], L["keys"][:, :, :], kr[:, :].unsqueeze(2).to_broadcast([KEYS, 2, 32]),
                                  ALU.mult).then_inc(sem("key_unit"), 1)

            dve.wait_ge(sem("tok_weight_steps"), 2)

            def tok_ratio(c):
                dve.wait_ge(sem("tok_exp"), c + 1)
                dve.tensor_scalar(gcap[:, c, :], gexp[:, c, :], float(np.exp(20.0)), None, ALU.min) \
                   .then_inc(sem("tok_num"), 1)
                dve.wait_ge(sem("tok_num"), 3 * c + 1)
                dve.scalar_tensor_tensor(gnum[:, c, :], gcap[:, c, :], 2.0, gcap[:, c, :], ALU.add, ALU.mult) \
                   .then_inc(sem("tok_num"), 1)
                dve.wait_ge(sem("tok_num"), 3 * c + 2)
                dve.tensor_scalar(gden[:, c, :], gnum[:, c, :], 2.0, None, ALU.add).then_inc(sem("tok_num"), 1)
                dve.wait_ge(sem("tok_num"), 3 * c + 3)
                dve.reciprocal(grec[:, c, :], gden[:, c, :]).then_inc(sem("tok_rec"), 1)

            def tok_product(c):
                dve.wait_ge(sem("tok_tanh"), c + 1)
                dve.scalar_tensor_tensor(gmul[:, c, :], B[:, c, 0:CHUNK], bn[:, 0:1], gact[:, c, :],
                                         ALU.add, ALU.mult).then_inc(sem("tok_mish"), 1)
                dve.wait_ge(sem("tok_mish"), c + 1)
                dve.scalar_tensor_tensor(prod[:, c, :], B[:, c, CHUNK:2 * CHUNK], bn[:, 1:2], gmul[:, c, :],
                                         ALU.add, ALU.mult).then_inc(sem("tok_prod"), 1)

            def tok_tokens(c):
                dve.wait_ge(sem("tok_third"), c + 1)
                dve.scalar_tensor_tensor(
                    hv[:, 4 * c:4 * c + 4, 1:SEQ], B[:, 4 + c % 2, 0:CHUNK].rearrange("p (i s) -> p i s", i=4),
                    col("w3b"), L["pos"][:, :].unsqueeze(1).to_broadcast([P, 4, PATCHES]), ALU.add, ALU.add) \
                    .then_inc(sem("tok_h"), 1)

            tok_ratio(0)
            tok_ratio(1)
            tok_product(0)
            loaded(dve, "pos")
            for c in range(2, 4):
                tok_ratio(c)
                tok_tokens(c - 2)
                tok_product(c - 1)
            dve.wait_ge(sem("kbd_ready"), 1)
            dve.wait_ge(sem("key_turned"), 1)
            for j in range(4):
                dve.tensor_copy(kbd[32 * j:32 * j + 32, j * KEYS:(j + 1) * KEYS], B[32 * j:32 * j + 32, 7, 0:KEYS]) \
                   .then_inc(sem("kbd_ready"), 1)
            dve.tensor_copy(wqc[:, :, :].rearrange("p k n -> p (k n)"), B[:, 6, :]).then_inc(sem("wqc_ready"), 1)
            dve.tensor_copy(bqc[:, :], B[:, 7, KEYS:KEYS + 4]).then_inc(sem("wqc_ready"), 1)
            tok_product(3)
            tok_tokens(2)
            tok_tokens(3)

            ln_vector(dve, LN_GAU, xn)
            for c in range(4):
                at = slice(c * SEQ, (c + 1) * SEQ)
                dve.wait_ge(sem("l2_norm"), c + 1)
                dve.tensor_scalar(dev[:, at], dev[:, at], 1e-5, None, ALU.max).then_inc(sem("l2_steps"), 1)
                dve.wait_ge(sem("l2_steps"), 2 * c + 1)
                dve.reciprocal(inv[:, at], dev[:, at]).then_inc(sem("l2_steps"), 1)
            for c in range(4):
                dve.wait_ge(sem("l2_inverse"), c + 1)
                dve.scalar_tensor_tensor(quarter(x2, c), quarter(xn, c), col("g"), B[:, 2 * c + 1, 0:Q],
                                         ALU.mult, ALU.mult).then_inc(sem("l2_done"), 1)
            loaded(dve, "relpos")

            def gau_qk(c):
                u = c % 2
                dve.wait_ge(sem("gau_base"), c + 1)
                for k, out in enumerate((qg, kg)):
                    dve.tensor_scalar(out[:, u, :], base[:, u, :], col("gamma", k), col("beta", k), ALU.mult, ALU.add) \
                       .then_inc(sem("gau_qk"), 1)

            def gau_bias(c):
                dve.wait_ge(sem("gau_scores"), c + 1)
                dve.tensor_tensor(biased[:, c % 2], B[0:SEQ, 4 * (c % 2) + 2, 0:Q].rearrange("p (i s) -> p i s", i=4),
                                  L["relpos"][:, :].unsqueeze(1).to_broadcast([SEQ, 4, SEQ]), ALU.add) \
                   .then_inc(sem("gau_biased"), 1)

            def gau_gate(c):
                u, k = c % 2, 4 * (c % 2)
                for blk in range(2):
                    dve.wait_ge(sem("gau_mixed"), 2 * c + blk + 1)
                    dve.tensor_tensor(uo[:, u, blk, :], B[:, k + (1, 3)[blk], 0:Q], ug[:, u, blk, :], ALU.mult) \
                       .then_inc(sem("gau_uo"), 1)

            def gau_add(c):
                u, at = c % 2, c * Q
                dve.wait_ge(sem("gau_out"), c + 1)
                dve.scalar_tensor_tensor(gres[:, u, :], xn[:, at:at + Q], col("res"), B[:, 4 * u + 2, 0:Q],
                                         ALU.mult, ALU.add).then_inc(sem("gau_h"), 1)
                dve.wait_ge(sem("gau_h"), 2 * c + 1)
                dve.tensor_tensor(h[:, at:at + Q], h[:, at:at + Q], gres[:, u, :], ALU.add).then_inc(sem("gau_h"), 1)

            for c in range(0, 4, 2):
                gau_qk(c)
                gau_qk(c + 1)
                gau_bias(c)
                gau_bias(c + 1)
                gau_gate(c)
                gau_gate(c + 1)
                gau_add(c)
                gau_add(c + 1)

            ln_vector(dve, LN_KEYS, x2)
            def q_shift(m):
                dve.wait_ge(sem("q_squared"), m + 1)
                if m >= 2:
                    dve.wait_ge(sem("q_ln"), 2 * (m - 2) + 2)
                dve.tensor_scalar(halves(z.rearrange("p f n -> p (f n)"), m % 2), banks(2 * (m % 2)),
                                  bqc[:, m // 2:m // 2 + 1], None, ALU.add).then_inc(sem("q_shifted"), 1)

            def q_invert(m):
                dve.wait_ge(sem("q_std"), m + 1)
                at = slice(m % 2 * EIGHTH, (m % 2 + 1) * EIGHTH)
                dve.reciprocal(inv[:, at], dev[:, at]).then_inc(sem("q_inverse"), 1)

            q_shift(0)
            q_invert(0)
            for m in range(8):
                if m + 1 < 8:
                    q_invert(m + 1)
                dve.wait_ge(sem("q_shifted"), m + 1)
                dve.wait_ge(sem("q_rstd"), m + 1)
                zz = halves(z.rearrange("p f n -> p (f n)"), m % 2)
                dve.tensor_tensor(zz, zz, banks(4 + 2 * (m % 2)), ALU.mult).then_inc(sem("q_z"), 1)
                if m + 1 < 8:
                    q_shift(m + 1)

            vals = vi[:, 0]

            def top8(i):
                hold(dve, sem("pk_s1"), i + 1)
                for l in range(LISTS):
                    last = dve.max(vals[:, l, 0:8], s1[:, l, :])
                last.then_inc(sem("pk_top8"), 1)

            def top8_index(i):
                hold(dve, sem("pk_top8"), i * 2 + 1)
                for l in range(LISTS):
                    dve.max_index(iu[:, l, 0:8], vals[:, l, 0:8], s1[:, l, :])
                    last = dve.match_replace(s2[:, l, :], vals[:, l, 0:8], s1[:, l, :], BIG)
                last.then_inc(sem("pk_lists"), 1)

            def next8(i):
                hold(dve, sem("pk_lists"), i + 1)
                for l in range(LISTS):
                    last = dve.max(vals[:, l, 8:16], s2[:, l, :])
                last.then_inc(sem("pk_top8"), 1)

            def next8_index(i):
                hold(dve, sem("pk_top8"), i * 2 + 2)
                for l in range(LISTS):
                    last = dve.max_index(iu[:, l, 8:16], vals[:, l, 8:16], s2[:, l, :])
                last.then_inc(sem("pk_index"), 1)

            def expert_digits(i, prev2):
                dve.wait_ge(sem("pk_xt"), i * 2 + 2)
                expert = xt[:, PARTS * PAIRS:, :].rearrange("p c t -> p (c t)")
                dve.tensor_scalar(ebf[:, :], expert, -15.5, 1.0 / EB, ALU.add, ALU.mult).then_inc(sem("pk_ab"), 1)
                if prev2:
                    activate_weights(i - 1, 2)
                dve.wait_ge(sem("pk_ab"), i * 3 + 1)
                dve.tensor_scalar(ea[:, :], ebf[:, :], ROUND, ROUND, ALU.add, ALU.subtract).then_inc(sem("pk_ab"), 1)
                if prev2:
                    activate_weights(i - 1, 3)
                dve.wait_ge(sem("pk_ab"), i * 3 + 2)
                dve.scalar_tensor_tensor(eb[:, :], ea[:, :], -float(EB), expert, ALU.mult, ALU.add) \
                   .then_inc(sem("pk_ab"), 1)
                for a in range(EA):
                    last = dve.tensor_scalar(ah[:, a].rearrange("p c t -> p (c t)"), ea[:, :], float(a), None,
                                             ALU.is_equal)
                last.then_inc(sem("pk_ah"), 1)
                dve.wait_ge(sem("pk_ab"), i * 3 + 3)

            def b_onehots(first, end):
                for b in range(first, end):
                    last = dve.tensor_scalar(bt[:, :, :, b, :], eb.rearrange("p (c j g) -> p c j g", c=PAIRS, j=QUAD),
                                             float(b), None, ALU.is_equal)
                return last

            def candidates(i, prev):
                v = vi[:, :, :, :].rearrange("p k (h l) r -> p (k h) l r", l=2)
                first, second = v[:, :, 0, :], v[:, :, 1, :]
                dve.wait_ge(sem("pk_values"), i + 1)
                dve.wait_ge(sem("pk_indices"), i + 1)
                for r in range(5):
                    n = ROW_LEN[r]
                    dve.tensor_tensor(cc[:, :, ROW_AT[r]:ROW_AT[r] + n],
                                      first[:, :, r:r + 1].to_broadcast([TILE, LISTS, n]), second[:, :, 0:n],
                                      ALU.add).then_inc(sem("pk_cand"), 1)
                dve.tensor_tensor(cc[:, :, ROW_AT[5]:ROW_AT[8]].rearrange("p k (r c) -> p k r c", c=2),
                                  first[:, :, 5:8].unsqueeze(3).to_broadcast([TILE, LISTS, 3, 2]),
                                  second[:, :, 0:2].unsqueeze(2).to_broadcast([TILE, LISTS, 3, 2]),
                                  ALU.add).then_inc(sem("pk_cand"), 1)
                dve.tensor_tensor(cc[:, :, ROW_AT[8]:CAND], first[:, :, 8:16],
                                  second[:, :, 0:1].to_broadcast([TILE, LISTS, 8]), ALU.add) \
                   .then_inc(sem("pk_cand"), 1)
                if prev:
                    b_onehots(DVE_B - 9, DVE_B - 8)
                hold(dve, sem("pk_cand"), i * 7 + 7)
                for k in range(HEADS):
                    last = dve.max(mm[:, k, 0:8], cc[:, k, :])
                last.then_inc(sem("pk_m"), 1)
                if prev:
                    b_onehots(DVE_B - 8, DVE_B - 7)
                hold(dve, sem("pk_m"), i * 3 + 1)
                dve.tensor_scalar(mneg[:, :], mm[:, :, 0], -1.0, None, ALU.mult).then_inc(sem("pk_mneg"), 1)
                for k in range(HEADS):
                    last = dve.match_replace(c2[:, k, :], mm[:, k, 0:8], cc[:, k, :], BIG)
                last.then_inc(sem("pk_m"), 1)
                if prev:
                    b_onehots(DVE_B - 7, DVE_B - 6)
                hold(dve, sem("pk_m"), i * 3 + 2)
                for k in range(HEADS):
                    last = dve.max(mm[:, k, 8:16], c2[:, k, :])
                last.then_inc(sem("pk_m"), 1)
                if prev:
                    b_onehots(DVE_B - 6, DVE_B - 5)
                hold(dve, sem("pk_m"), i * 3 + 3)
                for k in range(HEADS):
                    last = dve.match_replace(c2[:, k, :], mm[:, k, 8:16], c2[:, k, :], BIG)
                last.then_inc(sem("pk_taken"), 1)
                if prev:
                    b_onehots(DVE_B - 5, DVE_B).then_inc(sem("pk_bt"), 1)

            def weights(i):
                dve.wait_ge(sem("pk_exp"), i + 1)
                dve.wait_ge(sem("pk_taken"), i + 1)
                dve.scalar_tensor_tensor(wu[:, :, :], c2[:, :, :], 0.1 * BIG, ex[:, :, :], ALU.is_lt, ALU.mult) \
                   .then_inc(sem("pk_sum"), 1)
                dve.wait_ge(sem("pk_total"), i + 1)
                dve.reciprocal(wr[:, :], wz[:, :]).then_inc(sem("pk_sum"), 1)

            def activate_weights(i, j):
                dve.wait_ge(sem("pk_scattered"), i + 1)
                r = slice(EB * j, EB * (j + 1))
                own = B[r, 5:8, 0:PER_BANK * 48].rearrange("p k (g t n) -> p k g t n", g=PER_BANK, t=QUAD)[:, :, :, j, :]
                dve.tensor_tensor(
                    wg[r, j, :, :, :].rearrange("p (k g) a q -> p k g a q", k=3),
                    own.rearrange("p k g (a q) -> p k g a q", a=EA),
                    gelu[r, :, bass.ds(i * GROUPS, 3 * PER_BANK)].rearrange("p a (k g) -> p k g a", k=3).unsqueeze(4)
                    .to_broadcast([EB, 3, PER_BANK, EA, PARTS]), ALU.mult).then_inc(sem("pk_wg"), 1)

            def add_experts(i):
                dve.wait_ge(sem("pk_out"), i + 1)
                at = bass.ds(i * TILE, TILE)
                dve.tensor_tensor(h[:, at], h[:, at], B[:, 4, 0:TILE], ALU.add).then_inc(sem("pk_h"), 1)

            def dve_tile(i, prev):
                top8(i)
                if prev == 0:
                    dve.wait_ge(sem("q_norm"), 2)
                    dve.tensor_scalar(qnc[:, :], qn[:, :], 1e-12, None, ALU.max).then_inc(sem("q_inorm"), 1)
                    dve.wait_ge(sem("q_inorm"), 1)
                    dve.reciprocal(rn[:, :], qnc[:, :]).then_inc(sem("q_inorm"), 1)
                top8_index(i)
                if prev == 2:
                    activate_weights(i - 2, 0)
                next8(i)
                if prev == 2:
                    activate_weights(i - 2, 1)
                next8_index(i)
                if prev:
                    expert_digits(i - 1, prev == 2)
                    b_onehots(ACT_B, DVE_B - 9)
                candidates(i, prev)
                weights(i)
                if prev == 2:
                    add_experts(i - 2)

            dve.sem_inc(sem("pk_h"), 1)
            dve_tile(0, 0)
            dve.wait_ge(sem("pk_gelu"), NT)
            dve.memset(B[:, 7, (GROUPS - 2 * PER_BANK) * 48:PER_BANK * 48], 0.0).then_inc(sem("pk_zeroed"), 1)
            dve_tile(1, 1)
            dve.wait_ge(sem("pk_zeroed"), 3)
            with dve.Fori(2, NT) as i:
                dve_tile(i, 2)
            activate_weights(NT - 2, 0)
            activate_weights(NT - 2, 1)
            expert_digits(NT - 1, True)
            b_onehots(ACT_EARLY, EB).then_inc(sem("pk_bt"), 1)
            dve.wait_ge(sem("pk_ah"), NT)
            for a in range(DVE_A):
                last = dve.tensor_tensor(
                    aw[:, a].rearrange("p q c t -> p q (c t)"),
                    ah[:, a].rearrange("p c t -> p (c t)").unsqueeze(1).to_broadcast([PAIR, PARTS, PAIRS * TILE]),
                    xt[:, 0:PARTS * PAIRS, :].rearrange("p (q c) t -> p q (c t)", q=PARTS), ALU.mult)
            last.then_inc(sem("pk_bt_pool"), 1)
            add_experts(NT - 2)
            for c in range(2):
                ln_copy(dve, LN_BLOCK, c, x2)
            for c in range(2):
                ln_invert(dve, LN_BLOCK, c)
            for j in range(QUAD):
                activate_weights(NT - 1, j)
            add_experts(NT - 1)

            dve.memset(vaug[:, :, :, HD:HD + 1], 1.0).then_inc(sem("vaug_ones"), 1)
            for c in range(2):
                ln_scale(dve, LN_BLOCK, c, x2)
            for c in range(2, 4):
                ln_copy(dve, LN_BLOCK, c, x2)
            for c in range(2, 4):
                ln_invert(dve, LN_BLOCK, c)
            for c in range(2, 4):
                ln_scale(dve, LN_BLOCK, c, x2)
            loaded(dve, "rope")
            for hf in range(2):
                for k in range(4):
                    dve.wait_ge(sem("rot_linear"), 4 * hf + k + 1)
                    if hf and k % 2 == 0:
                        dve.wait_ge(sem("rot_done"), k // 2 + 1)
                    dve.tensor_tensor(rot[:, k // 2, k % 2, :].rearrange("p (q i s) -> p q i s", q=2, i=4),
                                      B[:, 2 * k:2 * k + 2, 0:Q].rearrange("p q (i s) -> p q i s", i=4),
                                      L["rope"][:, k % 2, :].unsqueeze(1).unsqueeze(1).to_broadcast([P, 2, 4, SEQ]),
                                      ALU.mult).then_inc(sem("rot_parts"), 1)

            def at_shift(i, u):
                dve.wait_ge(sem("at_scores"), i + 1)
                sc = B[0:SEQ, 2 * u:2 * u + 2, 0:4 * SEQ].rearrange("p b (h n) -> p b h n", h=4)
                dve.tensor_reduce(mx[:, u, :].rearrange("p (b h) -> p b h", b=2), sc, AX.X, ALU.max) \
                   .then_inc(sem("at_max"), 1)
                dve.wait_ge(sem("at_max"), i + 1)
                dve.tensor_tensor(sd[:, u, :, :].rearrange("p (b h) n -> p b h n", b=2), sc,
                                  mx[:, u, :].rearrange("p (b h) -> p b h", b=2).unsqueeze(3)
                                  .to_broadcast([SEQ, 2, 4, SEQ]), ALU.subtract).then_inc(sem("at_dif"), 1)

            def at_normalise(i, u):
                cx = B[0:SEQ, 6, 0:HEADS * (HD + 1)].rearrange("p (h d) -> p h d", h=HEADS)
                dve.wait_ge(sem("at_context"), i + 1)
                dve.reciprocal(rs[:, u, :], cx[:, :, HD]).then_inc(sem("at_rs"), 1)
                dve.wait_ge(sem("at_rs"), i + 1)
                dve.tensor_tensor(cn[:, u, :, :], cx[:, :, 0:HD],
                                  rs[:, u, :].unsqueeze(2).to_broadcast([SEQ, HEADS, HD]),
                                  ALU.mult).then_inc(sem("at_cn"), 1)

            at_shift(0, 0)
            at_shift(1, 1)
            with dve.Fori(1, IMAGES // 2) as p:
                for u in range(2):
                    dve.wait_ge(sem("at_exp"), p * 2 + u - 1)
                    at_shift(p * 2 + u, u)
                    at_normalise(p * 2 + u - 2, u)
            at_normalise(IMAGES - 2, 0)
            at_normalise(IMAGES - 1, 1)

            for c in range(4):
                dve.wait_ge(sem("wo_out"), c + 1)
                dve.tensor_tensor(quarter(xn, c), B[:, 2 * c, 0:Q], quarter(x2, c), ALU.add) \
                   .then_inc(sem("wo_res"), 1)
            ln_vector(dve, LN_POST1, x2)
            loaded(dve, "mw1")
            loaded(dve, "mw2")
            for k in range(4):
                at = slice(2 * k, 2 * k + 2)
                high_part(dve, w1h[:, at], L["mw1"][:, at]).then_inc(sem("moe_high"), 1)
                high_part(dve, w2h[:, at], L["mw2"][:, at]).then_inc(sem("moe_high"), 1)
            for hf in range(2):
                dve.wait_ge(sem("ff_down"), hf + 1)
                dve.scalar_tensor_tensor(halves(xn, hf), banks(4 + 2 * hf), col("b2"), halves(x4, hf),
                                         ALU.add, ALU.add).then_inc(sem("ff_res"), 1)
            ln_vector(dve, LN_POST2, x2)
            for c in range(4):
                dve.wait_ge(sem("post2"), c + 1)
                dve.tensor_tensor(quarter(h, c), quarter(h, c), quarter(x4, c), ALU.add).then_inc(sem("post_h"), 1)

            ln_vector(dve, LN_MOE, x2)
            for c in range(4):
                dve.wait_ge(sem("ln_done"), 4 * LN_MOE + c + 1)
                high_part(dve, quarter(xh, c), quarter(x2, c)).then_inc(sem("moe_high"), 1)
            loaded(dve, "br")
            loaded(dve, "order")
            dve.wait_ge(sem("moe_logits"), 1)
            wide = [TILE, NT, EXPERTS]
            dve.tensor_tensor(lg[:, :, :], B[0:TILE, 4, 0:NT * EXPERTS].rearrange("p (t e) -> p t e", t=NT),
                              L["br"][:, :].unsqueeze(1).to_broadcast(wide), ALU.add).then_inc(sem("moe_route"), 1)
            dve.wait_ge(sem("moe_route"), 1)
            dve.tensor_reduce(lm[:, :], lg[:, :, :], AX.X, ALU.max).then_inc(sem("moe_route"), 1)
            dve.wait_ge(sem("moe_route"), 2)
            dve.tensor_tensor(gd[:, :], lm[:, :], lm[:, :], ALU.subtract).then_inc(sem("moe_route"), 1)
            dve.tensor_tensor(leq[:, :, :], lg[:, :, :], lm[:, :].unsqueeze(2).to_broadcast(wide), ALU.is_equal) \
               .then_inc(sem("moe_route"), 1)
            dve.wait_ge(sem("moe_route"), 4)
            dve.tensor_tensor(lord[:, :, :], leq[:, :, :], L["order"][:, :].unsqueeze(1).to_broadcast(wide),
                              ALU.mult).then_inc(sem("moe_route"), 1)
            dve.wait_ge(sem("moe_route"), 5)
            dve.tensor_reduce(lfirst[:, :], lord[:, :, :], AX.X, ALU.max).then_inc(sem("moe_route"), 1)
            dve.wait_ge(sem("moe_route"), 6)
            dve.tensor_tensor(lmask[:, :, :], L["order"][:, :].unsqueeze(1).to_broadcast(wide),
                              lfirst[:, :].unsqueeze(2).to_broadcast(wide), ALU.is_equal).then_inc(sem("moe_route"), 1)
            dve.wait_ge(sem("moe_gexp"), 1)
            dve.reciprocal(gr[:, :], ge[:, :]).then_inc(sem("moe_route"), 1)
            dve.wait_ge(sem("moe_route"), 8)
            dve.tensor_tensor(gg[:, :], ge[:, :], gr[:, :], ALU.mult).then_inc(sem("moe_route"), 1)
            dve.wait_ge(sem("moe_route"), 9)
            dve.tensor_tensor(mgate[:, :, :], lmask[:, :, :], gg[:, :].unsqueeze(2).to_broadcast(wide), ALU.mult) \
               .then_inc(sem("moe_parts"), 1)
            dve.wait_ge(sem("moe_parts"), 1)
            dve.tensor_copy(mparts[:, :, 0], mgate[:, :, :]).then_inc(sem("moe_parts"), 1)
            dve.wait_ge(sem("moe_parts"), 2)
            dve.tensor_tensor(mrest[:, :, :], mgate[:, :, :], mparts[:, :, 0], ALU.subtract) \
               .then_inc(sem("moe_parts"), 1)
            dve.wait_ge(sem("moe_parts"), 3)
            dve.tensor_copy(mparts[:, :, 1], mrest[:, :, :]).then_inc(sem("moe_parts"), 1)
            dve.wait_ge(sem("moe_parts"), 4)
            dve.tensor_tensor(mrest[:, :, :], mrest[:, :, :], mparts[:, :, 1], ALU.subtract) \
               .then_inc(sem("moe_parts"), 1)
            dve.wait_ge(sem("moe_parts"), 5)
            dve.tensor_copy(mparts[:, :, 2], mrest[:, :, :]).then_inc(sem("moe_parts"), 1)

            def split_hidden(c, e):
                n, u = c * 8 + e, e % 2
                for k in range(2):
                    dve.wait_ge(sem("moe_hid"), n * 4 + 2 * k + 6)
                    high_part(dve, mhh[:, u, 2 * k:2 * k + 2, :], mhid[:, u, 2 * k:2 * k + 2, :]) \
                        .then_inc(sem("moe_split"), 1)
                dve.wait_ge(sem("moe_split"), n * 3 + 1)
                dve.tensor_tensor(mhl[:, u, 0:2, :], mhid[:, u, 0:2, :], mhh[:, u, 0:2, :], ALU.subtract).then_inc(sem("moe_split"), 1)

            def accumulate(c, e):
                dve.wait_ge(sem("moe_down"), c * 8 + e + 3)
                dve.wait_ge(sem("moe_mb"), c * 8 + e + 3)
                if e:
                    dve.wait_ge(sem("moe_acc"), c * 8 + e)
                dve.scalar_tensor_tensor((mtmp if e else macc)[:, :], B[:, 4 + e % 2, 0:Q], col("mb2", e),
                                         mb[:, e % 2, :], ALU.add, ALU.mult).then_inc(sem("moe_tmp"), 1)
                if e:
                    dve.wait_ge(sem("moe_tmp"), c * 8 + e + 3)
                    dve.tensor_tensor(macc[:, :], macc[:, :], mtmp[:, :], ALU.add).then_inc(sem("moe_acc"), 1)
                else:
                    dve.wait_ge(sem("moe_tmp"), c * 8 + 3)
                    dve.sem_inc(sem("moe_acc"), 1)

            dve.sem_inc(sem("moe_tmp"), 2)
            split_hidden(0, 0)

            def experts_of_quarter(c, last_quarter):
                for e in range(EXPERTS):
                    if e + 1 < EXPERTS:
                        split_hidden(c, e + 1)
                    elif not last_quarter:
                        split_hidden(c + 1, 0)
                    accumulate(c, e)
                dve.wait_ge(sem("moe_acc"), c * 8 + 8)
                at = bass.ds(c * Q, Q)
                dve.tensor_tensor(h[:, at], h[:, at], macc[:, :], ALU.add).then_inc(sem("out_ready"), 1)
                dve.wait_ge(sem("out_ready"), c + 1)

            with dve.Fori(0, 3) as c:
                experts_of_quarter(c, False)
            experts_of_quarter(3, True)


def layouts(x, cls_tok, **w):
    f = np.float32
    a = {k: np.asarray(v) for k, v in w.items()}
    x = np.asarray(x)
    out = {}
    out["eps"] = np.concatenate(
        [a["L0_tok_eps_in1"].reshape(2, P).T, a["L0_tok_eps_in2"].reshape(2, P).T,
         a["L0_tok_eps_out1"][:, None], a["L0_tok_eps_out2"][:, None],
         np.broadcast_to(a["L0_tok_eps_out1"], (P, P)), np.broadcast_to(a["L0_tok_eps_out2"], (P, P))], axis=1)
    out["keys"] = np.stack([a["L0_ffn_keys0"], a["L0_ffn_keys1"]], axis=1)
    cols = {
        "w1b": a["L0_tok_W1_b"], "w1sb": a["L0_tok_W1_sb"], "w2b": a["L0_tok_W2_b"], "w2sb": a["L0_tok_W2_sb"],
        "w3b": a["L0_tok_W3_b"], "gamma": a["L0_attn_gamma"].T, "beta": a["L0_attn_beta"].T,
        "res": a["L0_attn_res_scale"], "g": np.broadcast_to(a["L0_attn_g"].reshape(1), (P,)),
        "bq": a["L0_ffn_bq"].reshape(4, P).T,
        "lng": np.concatenate([a["L0_ffn_ln_g"]] * 2), "lnb": np.concatenate([a["L0_ffn_ln_b"]] * 2),
        "b1": a["L1_attn_b1"].reshape(4, P).T, "b2": a["L1_attn_b2"], "g1": a["L1_attn_g1"], "be1": a["L1_attn_be1"],
        "g2": a["L1_attn_g2"], "be2": a["L1_attn_be2"], "mb1": a["L1_ffn_b1"].reshape(32, P).T,
        "mb2": a["L1_ffn_b2"].T, "cls": np.asarray(cls_tok).reshape(P), "eps": np.full((P,), 1e-5, f),
        "minus": np.broadcast_to(-np.arange(ACT_B).astype(f), (P, ACT_B)),
    }
    out["cols"] = np.concatenate([cols[k].reshape(P, n) for k, (_, n) in COLS.items()], axis=1)
    out["tokw"] = np.stack([np.stack([a[f"L0_tok_W{br}_{k}"].T.reshape(2, P, P).transpose(1, 0, 2)
                                      for k in ("w", "sw")], axis=1) for br in (1, 2)], axis=1)
    out["pat"] = x.reshape(IMAGES, 8, 16, 8, 16).transpose(2, 4, 0, 1, 3).reshape(2, P, IMAGES * PATCHES) \
        .transpose(1, 0, 2)
    out["ident"] = np.eye(P, dtype=f)
    head = np.arange(P) // 64
    out["centre64"] = (np.eye(P) - (head[:, None] == head) / 64).astype(f)
    out["wq"] = a["L0_ffn_Wq"].reshape(4, P, P).transpose(1, 0, 2)
    out["w3"] = a["L0_tok_W3_w"].T
    div = np.exp(np.arange(0, P, 2, dtype=f) * f(-np.log(10000.0) / P)).astype(f)
    ang = (np.arange(PATCHES, dtype=f)[:, None] * div).astype(f)
    out["pos"] = np.stack([np.sin(ang), np.cos(ang)], axis=-1).reshape(PATCHES, P).T.astype(f)
    out["centre"] = (np.eye(P) - 1.0 / P).astype(f)
    out["mean"] = np.full((P, 32), 1.0 / P, f)
    out["ones"] = np.ones((P, 32), f)
    row, feat = np.arange(P)[:, None, None], np.arange(P)[None, None, :]
    out["back"] = (row == 32 * np.arange(4)[None, :, None] + 8 * (feat // 32)).astype(f)
    out["uvw"] = a["L0_attn_uv_w"]
    out["relpos"] = a["L0_attn_w"][SEQ - 1 + np.arange(SEQ)[:, None] - np.arange(SEQ)[None, :]]
    out["ow"] = a["L0_attn_o_w"].reshape(2, P, P).transpose(1, 0, 2)
    out["mean64"] = ((head[:, None] == np.arange(32) // 16) / 64).astype(f)
    out["blk32"] = (np.arange(P)[:, None] // 32 == np.arange(4)).astype(f)
    out["down"] = np.tile(a["L0_ffn_expert_down"][:P].T.reshape(P, EA, 1, EB), (1, 1, QUAD, 1)).reshape(P, EA, P)
    out["identb"] = np.eye(P, dtype=mybir.dt.np(BF16))
    out["up"] = np.tile(a["L0_ffn_expert_up"][:P].reshape(EA, EB, P).transpose(1, 0, 2), (QUAD, 1, 1))
    swap = np.arange(P) ^ 8
    wq, wk = a["L1_attn_Wq"], a["L1_attn_Wk"]
    out["qkv"] = np.stack([wq.T, wq[swap].T, wk.T, wk[swap].T, a["L1_attn_Wv"].T], axis=1)
    inv = (1.0 / (f(10000.0) ** (np.arange(0, HD, 2, dtype=f) / f(HD)))).astype(f)
    fr = (np.arange(SEQ, dtype=f)[:, None] * inv).astype(f)
    d = np.arange(P) % HD
    out["rope"] = np.stack([np.cos(fr)[:, d % 8].T, np.where(d < 8, -1.0, 1.0)[:, None] * np.sin(fr)[:, d % 8].T],
                           axis=1).astype(f)
    out["headmask"] = (np.arange(P)[:, None] // HD == np.arange(HEADS)).astype(f)
    out["wo"] = a["L1_attn_Wo"].T
    out["w1"] = a["L1_attn_W1"].T.reshape(P, 4, P)
    out["w2"] = a["L1_attn_W2"].T.reshape(4, P, P).transpose(1, 0, 2)
    out["wr"] = a["L1_ffn_Wr"]
    out["br"] = np.broadcast_to(a["L1_ffn_br"], (TILE, EXPERTS))
    out["order"] = np.broadcast_to(np.arange(EXPERTS, 0, -1).astype(f), (TILE, EXPERTS))
    part = np.tile(np.eye(EXPERTS, dtype=mybir.dt.np(BF16)), (PARTS, 1))
    out["selm"] = np.broadcast_to(part[:, :, None], (PARTS * EXPERTS, EXPERTS, P))
    out["mw2"] = a["L1_ffn_W2"].reshape(EXPERTS, 4, P, P).transpose(2, 0, 1, 3)
    out["mw1"] = a["L1_ffn_W1"].transpose(1, 0, 2)
    return out


def kernel(**inputs):
    import concourse.bacc as _bacc
    from concourse.bass_utils import run_bass_kernel_spmd as _run

    nc = _bacc.Bacc("TRN2", target_bir_lowering=False, num_devices=1)
    arrays, aps = {}, {}
    for name, v in layouts(**inputs).items():
        v = np.ascontiguousarray(v)
        arrays["in_" + name + "_dram"] = v
        aps[name] = nc.dram_tensor("in_" + name + "_dram", v.shape, mybir.dt.from_np(v.dtype), kind="ExternalInput").ap()
    y = nc.dram_tensor("out_dram", (P, T), F32, kind="ExternalOutput").ap()
    build(nc, aps, y)
    r = _run(nc, [arrays], core_ids=[0])
    return np.ascontiguousarray(r.results[0]["out_dram"].T.reshape(IMAGES, SEQ, P))
```
